# Optimizing a Trainium2 kernel written in Bass

```python
import numpy as np
import jax
import jax.numpy as jnp

def _softmax(x, axis=-1):
    return jax.nn.softmax(x, axis=axis)

def _gelu(x):
    return jax.nn.gelu(x, approximate=True)

def _silu(x):
    return jax.nn.silu(x)

def _sigmoid(x):
    return jax.nn.sigmoid(x)

def _layernorm(x, axis=-1, eps=1e-05):
    m = jnp.mean(x, axis=axis, keepdims=True)
    v = jnp.var(x, axis=axis, keepdims=True)
    return (x - m) / jnp.sqrt(v + eps)

def _scatter_add(tgt, idx, src, axis=0):
    return tgt.at[idx].add(src)

def _segment_sum(src, seg, n):
    return jax.ops.segment_sum(src, seg, n)
kernel_name = 'mk_adj_preln_d4_adj_r2_b35f99'

def setup_inputs(seed: int=0):
    np.random.seed(seed)
    _w = jnp.asarray

    def _rec_inputs():
        import jax
        import jax.numpy as jnp
        _gk = jax.random.key(seed)
        x = -0.000929 + 1 * jax.random.normal(jax.random.fold_in(_gk, 1), (4096, 128), jnp.float32)
        _a = jax.random.bernoulli(jax.random.fold_in(_gk, 2), 0.000976562, (4096, 4096))
        _af = _a.astype(jnp.float32)
        adj = _af
        return (x, adj)
    x, adj = _rec_inputs()

    def _L0_gnn_setup():
        import jax, jax.numpy as jnp
        import numpy as np
        NEG = -9000000000000000.0
        ALPHA = 0.2
        key = jax.random.key(seed)
        k1, k2, k3, k4, k5 = jax.random.split(key, 5)
        N, F_in, F_out = (4096, 128, 128)
        x = jax.random.normal(k1, (N, F_in), dtype=jnp.float32)
        adj = jax.random.randint(k2, (N, N), 0, 2).astype(jnp.float32)
        W = jax.random.normal(k3, (F_in, F_out), dtype=jnp.float32) * (1.0 / np.sqrt(F_in))
        a1 = jax.random.normal(k4, (F_out,), dtype=jnp.float32) * (1.0 / np.sqrt(2 * F_out))
        a2 = jax.random.normal(k5, (F_out,), dtype=jnp.float32) * (1.0 / np.sqrt(2 * F_out))
        a_bias = jnp.zeros((1,), dtype=jnp.float32)
        return {'x': x, 'adj': adj, 'W': W, 'a1': a1, 'a2': a2, 'a_bias': a_bias}
    _L0_gnn_all = _L0_gnn_setup()
    _L0_gnn_in = {k: v for k, v in _L0_gnn_all.items() if k in ('W', 'a1', 'a2', 'a_bias')}
    del _L0_gnn_all

    def _L1_gnn_setup():
        import jax, jax.numpy as jnp
        import numpy as np
        N, D = (4096, 128)
        EDGE_PROB = 0.005
        COS_EPS = 1e-08
        key = jax.random.key(seed)
        kx, ka = jax.random.split(key)
        x = jax.random.normal(kx, (N, D), dtype=jnp.float32)
        adj = (jax.random.uniform(ka, (N, N)) < EDGE_PROB).astype(jnp.float32)
        return {'t': jnp.float32(0.0), 'x': x, 'adj': adj, 'alpha': jnp.float32(0.5), 'beta': jnp.float32(1.0)}
    _L1_gnn_all = _L1_gnn_setup()
    _L1_gnn_in = {k: v for k, v in _L1_gnn_all.items() if k in ('t', 'alpha', 'beta')}
    del _L1_gnn_all

    def _L2_gnn_setup():
        import jax, jax.numpy as jnp
        import numpy as np
        N, EMB, HID = (4096, 128, 128)
        key = jax.random.key(seed)
        k1, k2, k3, k4, k5, k6, k7, k8 = jax.random.split(key, 8)
        inlayer = jax.random.normal(k1, (N, EMB), dtype=jnp.float32)
        inlayer2 = jax.random.normal(k2, (N, 2 * EMB), dtype=jnp.float32)
        adj_mat = jax.random.randint(k3, (N, N), 0, 2).astype(jnp.float32)
        W1 = jax.random.normal(k4, (HID, 2 * EMB), dtype=jnp.float32) / np.sqrt(2 * EMB)
        w2 = jax.random.normal(k5, (HID,), dtype=jnp.float32) / np.sqrt(HID)
        b2 = jax.random.normal(k6, (), dtype=jnp.float32) * 0.01
        w3 = jax.random.normal(k7, (HID,), dtype=jnp.float32) / np.sqrt(HID)
        b3 = jax.random.normal(k8, (), dtype=jnp.float32) * 0.01
        return {'inlayer': inlayer, 'inlayer2': inlayer2, 'adj_mat': adj_mat, 'W1': W1, 'w2': w2, 'b2': b2, 'w3': w3, 'b3': b3}
    _L2_gnn_all = _L2_gnn_setup()
    _L2_gnn_in = {k: v for k, v in _L2_gnn_all.items() if k in ('inlayer2', 'W1', 'w2', 'b2', 'w3', 'b3')}
    del _L2_gnn_all

    def _L3_gnn_setup():
        import jax, jax.numpy as jnp
        import numpy as np
        N, D_IN, D_HID, D_OUT, K = (5000, 128, 128, 128, 3)

        def cheb_conv(x, L, W, b):
            Tx0 = x
            out = Tx0 @ W[0]
            Tx1 = L @ x
            out = out + Tx1 @ W[1]
            for k in range(2, W.shape[0]):
                Tx2 = 2.0 * (L @ Tx1) - Tx0
                out = out + Tx2 @ W[k]
                Tx0, Tx1 = (Tx1, Tx2)
            return out + b
        key = jax.random.key(seed)
        ks = jax.random.split(key, 4)
        x = jax.random.normal(ks[0], (N, D_IN), dtype=jnp.float32)
        L = jax.random.normal(ks[1], (N, N), dtype=jnp.float32) / jnp.sqrt(jnp.float32(N))
        W0 = jax.random.normal(ks[2], (K, D_IN, D_HID), dtype=jnp.float32) / jnp.sqrt(jnp.float32(D_IN))
        b0 = jnp.zeros((D_HID,), dtype=jnp.float32)
        W1 = jax.random.normal(ks[3], (K, D_HID, D_OUT), dtype=jnp.float32) / jnp.sqrt(jnp.float32(D_HID))
        b1 = jnp.zeros((D_OUT,), dtype=jnp.float32)
        return {'x': x, 'L': L, 'W0': W0, 'b0': b0, 'W1': W1, 'b1': b1}
    _L3_gnn_all = _L3_gnn_setup()
    _L3_gnn_in = {k: v for k, v in _L3_gnn_all.items() if k in ('W0', 'b0', 'W1', 'b1')}
    del _L3_gnn_all
    return {'x': x, 'adj': adj, 'L0_gnn_W': _L0_gnn_in['W'], 'L0_gnn_a1': _L0_gnn_in['a1'], 'L0_gnn_a2': _L0_gnn_in['a2'], 'L0_gnn_a_bias': _L0_gnn_in['a_bias'], 'L1_gnn_t': _L1_gnn_in['t'], 'L1_gnn_alpha': _L1_gnn_in['alpha'], 'L1_gnn_beta': _L1_gnn_in['beta'], 'L2_gnn_inlayer2': _L2_gnn_in['inlayer2'], 'L2_gnn_W1': _L2_gnn_in['W1'], 'L2_gnn_w2': _L2_gnn_in['w2'], 'L2_gnn_b2': _L2_gnn_in['b2'], 'L2_gnn_w3': _L2_gnn_in['w3'], 'L2_gnn_b3': _L2_gnn_in['b3'], 'L3_gnn_W0': _L3_gnn_in['W0'], 'L3_gnn_b0': _L3_gnn_in['b0'], 'L3_gnn_W1': _L3_gnn_in['W1'], 'L3_gnn_b1': _L3_gnn_in['b1']}

def reference(x, adj, L0_gnn_W, L0_gnn_a1, L0_gnn_a2, L0_gnn_a_bias, L1_gnn_t, L1_gnn_alpha, L1_gnn_beta, L2_gnn_inlayer2, L2_gnn_W1, L2_gnn_w2, L2_gnn_b2, L2_gnn_w3, L2_gnn_b3, L3_gnn_W0, L3_gnn_b0, L3_gnn_W1, L3_gnn_b1):
    import jax
    import jax.numpy as jnp

    def _L0_gnn_ref(x, adj, W, a1, a2, a_bias):
        import jax, jax.numpy as jnp
        import numpy as np
        NEG = -9000000000000000.0
        ALPHA = 0.2
        h = x @ W
        s1 = h @ a1
        s2 = h @ a2
        e = jax.nn.leaky_relu(s1[:, None] + s2[None, :] + a_bias[0], negative_slope=ALPHA)
        e = jnp.where(adj > 0, e, NEG)
        attention = jax.nn.softmax(e, axis=1)
        return attention @ h

    def _L1_gnn_ref(t, x, adj, alpha, beta):
        import jax, jax.numpy as jnp
        import numpy as np
        N, D = (4096, 128)
        EDGE_PROB = 0.005
        COS_EPS = 1e-08
        deg = jnp.clip(adj.sum(axis=1), 1.0)
        dis = deg ** (-0.5)
        adj_norm = dis[:, None] * adj * dis[None, :]
        diffusion = adj_norm @ x - x
        norms = jnp.maximum(jnp.linalg.norm(x, axis=-1), COS_EPS)
        sim = x @ x.T / (norms[:, None] * norms[None, :])
        attn = jax.nn.softmax(beta * sim * adj, axis=1)
        attn = jax.lax.stop_gradient(attn)
        return diffusion + jax.nn.sigmoid(alpha) * (attn @ x - x)

    def _L2_gnn_ref(inlayer, inlayer2, adj_mat, W1, w2, b2, w3, b3):
        import jax, jax.numpy as jnp
        import numpy as np
        N, EMB, HID = (4096, 128, 128)
        in_fts = jnp.einsum('ne,he->nh', inlayer2, W1)
        f1 = in_fts @ w2 + b2
        f2 = in_fts @ w3 + b3
        logits = f1[:, None] + f2[None, :]
        logits = adj_mat * logits
        bias_mat = -1000000000.0 * (1.0 - (adj_mat > 0).astype(jnp.float32))
        coefs = jax.nn.softmax(jax.nn.leaky_relu(logits, 0.01) + bias_mat, axis=1)
        vals = coefs @ inlayer
        return vals

    def _L3_gnn_ref(x, L, W0, b0, W1, b1):
        import jax, jax.numpy as jnp
        import numpy as np
        N, D_IN, D_HID, D_OUT, K = (5000, 128, 128, 128, 3)

        def cheb_conv(x, L, W, b):
            Tx0 = x
            out = Tx0 @ W[0]
            Tx1 = L @ x
            out = out + Tx1 @ W[1]
            for k in range(2, W.shape[0]):
                Tx2 = 2.0 * (L @ Tx1) - Tx0
                out = out + Tx2 @ W[k]
                Tx0, Tx1 = (Tx1, Tx2)
            return out + b
        h = jax.nn.elu(cheb_conv(x, L, W0, b0))
        h = jax.nn.elu(cheb_conv(h, L, W1, b1))
        return h
    h = jnp.maximum(_layernorm(x, axis=-1), 0.0)
    x = x + _L0_gnn_ref(h, adj, L0_gnn_W, L0_gnn_a1, L0_gnn_a2, L0_gnn_a_bias)
    h = jnp.maximum(_layernorm(x, axis=-1), 0.0)
    x = x + _L1_gnn_ref(L1_gnn_t, h, adj, L1_gnn_alpha, L1_gnn_beta)
    h = jnp.maximum(_layernorm(x, axis=-1), 0.0)
    x = x + _L2_gnn_ref(h, L2_gnn_inlayer2, adj, L2_gnn_W1, L2_gnn_w2, L2_gnn_b2, L2_gnn_w3, L2_gnn_b3)
    h = jnp.maximum(_layernorm(x, axis=-1), 0.0)
    x = x + _L3_gnn_ref(h, adj, L3_gnn_W0, L3_gnn_b0, L3_gnn_W1, L3_gnn_b1)
    return x

_drawn_inputs = setup_inputs


def setup_inputs(seed=0):
    import zlib

    import numpy as np

    out = dict(_drawn_inputs(seed))
    spreads = {'L3_gnn_b0': (0.0, 0.8), 'L3_gnn_b1': (0.0, 0.8)}
    factors = {'L0_gnn_a1': 8.0,
     'L2_gnn_inlayer2': 4.126,
     'L2_gnn_W1': 4.346,
     'L2_gnn_w2': 8.0,
     'L2_gnn_w3': 4.453}
    for name, (base, spread) in spreads.items():
        noise = np.random.default_rng([zlib.crc32(name.encode()), seed]).standard_normal(out[name].shape)
        drawn = base * np.exp(spread * noise) if base else spread * noise
        out[name] = jnp.asarray(drawn.astype(out[name].dtype))
    for name, factor in factors.items():
        out[name] = (out[name] * factor).astype(out[name].dtype)
    return out
```

```python
from contextlib import ExitStack

import concourse.bass as bass
from concourse import mybir

ALU = mybir.AluOpType
ACT = mybir.ActivationFunctionType
AXX = mybir.AxisListType.X
F32 = mybir.dt.float32
F16 = mybir.dt.float16
FP8 = mybir.dt.float8e5
U8 = mybir.dt.uint8
U32 = mybir.dt.uint32
RMAX = bass.bass_isa.ReduceOp.max
ds = bass.ds

P = 128
CI = 512
IB = CI // P
SUBS = 4
ONE = 32768.0
ONE_BYTE = 120
EPS = 1e-5
COS_EPS = 1e-8


class Chain:

    def __init__(self, eng, sem):
        self.eng, self.sem, self.n = eng, sem, 0

    def done(self, ins):
        self.n += 1
        ins.then_inc(self.sem, 1)
        self.eng.wait_ge(self.sem, self.n)


class Net:

    def __init__(self, nc, ctx, dram):
        self.nc, self.ctx, self.dram = nc, ctx, dram
        self.phase_sems = []
        self.passed, self.phase = {}, 0
        self.N, self.D = dram["x"].shape
        self.NB = self.N // P
        self.NC = self.N // CI
        self.JS = self.NB // SUBS
        self.PW = self.JS * CI // 4
        assert self.D == P and self.JS * SUBS == self.NB

    def sb(self, ctx, name, shape, dt):
        return ctx.enter_context(self.nc.sbuf_tensor(name, shape, dt))

    def ps(self, ctx, name, shape, dt=F32):
        return ctx.enter_context(self.nc.psum_tensor(name, shape, dt))

    def sem(self, name):
        s = self.nc.alloc_semaphore(name=name)
        self.phase_sems.append(s)
        return s

    def met(self, eng):
        key = str(eng.engine)
        if key not in self.passed:
            self.passed[key] = self.sem(f"passed{self.phase}_{len(self.passed)}")
        eng.sem_inc(self.passed[key], 1)

    def phase_end(self):
        self.nc.clear_and_free_semaphores(self.phase_sems)
        self.phase_sems, self.passed, self.phase = [], {}, self.phase + 1
        self.nc.all_engine_barrier()


def rows_view(ap):
    return ap.rearrange("(b p) w -> p b w", p=P)


def newton_rsqrt(dve, ch, r, v, tmp):
    ch.done(dve.tensor_tensor(tmp, r, r, ALU.mult))
    ch.done(dve.tensor_tensor(tmp, tmp, v, ALU.mult))
    ch.done(dve.tensor_scalar(tmp, tmp, -0.5, 1.5, ALU.mult, ALU.add))
    ch.done(dve.tensor_tensor(r, r, tmp, ALU.mult))


def layernorm_relu(net, dve, ch, xt, xc, h, st, need_root, root_done):
    NB, D = net.NB, net.D
    full = [P, NB, D]
    mean, var, r, tmp = st[:, 0, :], st[:, 1, :], st[:, 2, :], st[:, 3, :]
    ch.done(dve.tensor_reduce(mean, xt, AXX, ALU.add))
    ch.done(dve.tensor_scalar(mean, mean, 1.0 / D, None, ALU.mult))
    dve.tensor_tensor(xc, xt, mean.unsqueeze(2).to_broadcast(full), ALU.subtract).then_inc(need_root, 1)
    dve.wait_ge(root_done, 1)
    ch.done(dve.tensor_reduce(var, h, AXX, ALU.add))
    ch.done(dve.tensor_scalar(var, var, 1.0 / D, EPS, ALU.mult, ALU.add))
    ch.done(dve.reciprocal(tmp, var))
    dve.nop().then_inc(need_root, 1)
    dve.wait_ge(root_done, 2)
    newton_rsqrt(dve, ch, r, var, tmp)
    ch.done(dve.scalar_tensor_tensor(h, xc, 0.0, r.unsqueeze(2).to_broadcast(full), ALU.max, ALU.mult))


def layernorm_scalar_part(act, nc, xc, h, st, need_root, root_done):
    act.wait_ge(need_root, 1)
    nc.scalar.activation(h, xc, ACT.Square).then_inc(root_done, 1)
    act.wait_ge(need_root, 2)
    nc.scalar.activation(st[:, 2, :], st[:, 3, :], ACT.Sqrt).then_inc(root_done, 1)


def setup(net, g):
    nc, dram, NB, D = net.nc, net.dram, net.NB, net.D
    E2 = dram["L2_gnn_inlayer2"].shape[1] // P
    with ExitStack() as c:
        X = net.sb(c, "x_in", [P, NB, D], F32)
        XC = net.sb(c, "x_centred", [P, NB, D], F32)
        IN2 = g["store"][:, 0:NB * E2 * D].bitcast(F32).rearrange("p (b e) -> p b e", b=NB)
        W = net.sb(c, "w_gat", [P, D], F32)
        W1 = net.sb(c, "w1_gat2", [P, E2 * D], F32)
        A12 = net.sb(c, "a12", [P, 2], F32)
        W23 = net.sb(c, "w23", [P, 2], F32)
        SC = net.sb(c, "scalars_in", [P, 5], F32)
        WT = net.sb(c, "w_gat_T", [P, D], F32)
        VC = net.sb(c, "score_vectors", [P, 1 + E2, 2], F32)
        TT = net.sb(c, "transposed", [P, 2, 4, P], F32)
        MX = net.sb(c, "absmax", [P, 2], F32)
        MR = net.sb(c, "absmax_all", [P, 2], F32)
        st, ident, H = g["ln_cols"], g["ident"], g["H"]
        pW = net.ps(c, "p_wt", [P, D])
        pV = net.ps(c, "p_vec", [P, 1 + E2, 2])
        pT = net.ps(c, "p_tr", [P, 2, 4, P])
        pS = net.ps(c, "p_scores", [P, 2, NB, 2])
        ld_x, ld_in2, ld_w = net.sem("a_ld_x"), net.sem("a_ld_in2"), net.sem("a_ld_w")
        id0, id1 = net.sem("a_id0"), net.sem("a_ident")
        ch_s, pc_s = net.sem("a_dve_steps"), net.sem("a_act_steps")
        need_root, root_done = net.sem("a_need_root"), net.sem("a_root_done")
        wt_ps, wt_sb, vec_ps, vec_sb = (net.sem(n) for n in ("a_wt_ps", "a_wt_sb", "a_vec_ps", "a_vec_sb"))
        h_rdy, tr_ps, tr_sb, tr_used, sc_ps = (net.sem(n) for n in ("a_h", "a_tr_ps", "a_tr_sb", "a_tr_used", "a_sc_ps"))
        mx_rdy, mx_all = net.sem("a_mx"), net.sem("a_mx_all")
        GROUPS = [(1 + e, b) for b in range(0, NB, 4) for e in range(E2)] + [(0, b) for b in range(0, NB, 4)]

        with nc.Block() as block:
            @block.sync
            def _(sp):
                sp.dma_start(X[:, :, :], rows_view(dram["x"])).then_inc(ld_x, 16)
                for dst, src in ((W[:, :], dram["L0_gnn_W"]), (W1[:, :], dram["L2_gnn_W1"]),
                                 (A12[:, 0:1], dram["L0_gnn_a1"].unsqueeze(1)), (A12[:, 1:2], dram["L0_gnn_a2"].unsqueeze(1)),
                                 (W23[:, 0:1], dram["L2_gnn_w2"].unsqueeze(1)), (W23[:, 1:2], dram["L2_gnn_w3"].unsqueeze(1))):
                    sp.dma_start(dst, src).then_inc(ld_w, 16)
                for k, n in enumerate(("L0_gnn_a_bias", "L2_gnn_b2", "L2_gnn_b3", "L1_gnn_alpha", "L1_gnn_beta")):
                    sp.dma_start(SC[:, k:k + 1], dram[n].partition_broadcast(P)).then_inc(ld_w, 16)
                sp.dma_start(IN2, rows_view(dram["L2_gnn_inlayer2"])).then_inc(ld_in2, 16)

            @block.gpsimd
            def _(pool):
                nc.gpsimd.memset(ident[:, :], 0.0).then_inc(id0, 1)
                pool.wait_ge(id0, 1)
                nc.gpsimd.affine_select(out=ident[:, :], in_=ident[:, :], compare_op=ALU.not_equal, fill=1.0,
                                        base=0, pattern=[[-1, P]], channel_multiplier=1).then_inc(id1, 1)
                pool.wait_ge(mx_rdy, 1)
                nc.gpsimd.partition_all_reduce(MR[:, :], MX[:, :], P, RMAX).then_inc(mx_all, 1)

            @block.tensor
            def _(pe):
                pe.wait_ge(id1, 1)
                pe.wait_ge(ld_w, 16 * 11)
                pe.transpose(pW[:, :], W[:, :], ident[:, :]).then_inc(wt_ps, 1)
                pe.wait_ge(wt_sb, 1)
                pe.matmul(pV[:, 0, :], WT[:, :], A12[:, :], start=True, stop=True)
                for e in range(E2):
                    last = pe.matmul(pV[:, 1 + e, :], W1[:, e * P:(e + 1) * P], W23[:, :], start=True, stop=True)
                last.then_inc(vec_ps, 1)

                def project(n):
                    kind, b0 = GROUPS[n]
                    pe.wait_ge(tr_sb, n + 1)
                    for k in range(4):
                        last = pe.matmul(pS[:, 0 if kind == 0 else 1, b0 + k, :], TT[:, n % 2, k, :], VC[:, kind, :],
                                         start=kind == 0 or (kind == 1 and k == 0), stop=kind in (0, E2), skip_group_check=True)
                    last.then_inc(tr_used, 1)

                pe.wait_ge(ld_in2, 16)
                for n, (kind, b0) in enumerate(GROUPS):
                    if kind == 0 and b0 == 0:
                        pe.wait_ge(h_rdy, 1)
                    if n >= 2:
                        pe.wait_ge(tr_sb, n - 1)
                    for k in range(4):
                        src = H[:, b0 + k, 0:D] if kind == 0 else IN2[:, b0 + k, (kind - 1) * P:kind * P]
                        last = pe.transpose(pT[:, n % 2, k, :], src, ident[:, :])
                    last.then_inc(tr_ps, 1)
                    if n == 0:
                        pe.wait_ge(vec_sb, 1)
                    else:
                        project(n - 1)
                project(len(GROUPS) - 1)
                pe.wait_ge(tr_used, len(GROUPS))
                pe.nop().then_inc(sc_ps, 1)

            @block.scalar
            def _(act):
                n_ln = 0
                pc = Chain(act, pc_s)
                act.wait_ge(wt_ps, 1)
                nc.scalar.copy(WT[:, :], pW[:, :]).then_inc(wt_sb, 1)
                act.wait_ge(vec_ps, 1)
                nc.scalar.copy(VC[:, :, :], pV[:, :, :]).then_inc(vec_sb, 1)
                for n, (kind, b0) in enumerate(GROUPS):
                    if kind == 0 and b0 == 0:
                        layernorm_scalar_part(act, nc, XC[:, :, :], H[:, :, 0:D], st, need_root, root_done)
                    act.wait_ge(tr_ps, n + 1)
                    if n >= 2:
                        act.wait_ge(tr_used, n - 1)
                    nc.scalar.copy(TT[:, n % 2, :, :], pT[:, n % 2, :, :]).then_inc(tr_sb, 1)
                act.wait_ge(h_rdy, 2)
                pc.done(nc.scalar.activation(g["sig"][:, :], SC[:, 3:4], ACT.Exp, scale=-1.0))
                pc.done(nc.scalar.activation(g["exp_shift"][:, :], g["zero"][:, :], ACT.Exp,
                                             bias=g["neg_shift"][:, 0:1], scale=g["beta"][:, 0:1]))

            @block.vector
            def _(dve):
                ch = Chain(dve, ch_s)
                ch.done(dve.memset(g["ones"][:, :], 1.0))
                dve.memset(g["ones16"][:, :], 1.0)
                dve.memset(g["zero"][:, :], 0.0)
                ch.done(dve.memset(H[:, :, D:D + 1], 1.0))
                dve.wait_ge(ld_x, 16)
                layernorm_relu(net, dve, ch, X[:, :, :], XC[:, :, :], H[:, :, 0:D], st, need_root, root_done)
                dve.nop().then_inc(h_rdy, 1)
                dve.wait_ge(ld_w, 16 * 11)
                ch.done(dve.tensor_scalar(g["neg_shift"][:, :], SC[:, 4:5], 0.0, -1.0, ALU.max, ALU.mult))
                ch.done(dve.tensor_scalar(g["beta"][:, :], SC[:, 4:5], 1.0, None, ALU.mult))
                dve.nop().then_inc(h_rdy, 1)
                dve.wait_ge(pc_s, 2)
                ch.done(dve.tensor_scalar(g["sig"][:, :], g["sig"][:, :], 1.0, None, ALU.add))
                ch.done(dve.reciprocal(g["sig"][:, :], g["sig"][:, :]))
                dve.wait_ge(sc_ps, 1)
                for k, (own, oth) in enumerate(((SC[:, 0:1], None), (SC[:, 1:2], SC[:, 2:3]))):
                    sc = g["score"][k]
                    ch.done(dve.tensor_scalar(sc[:, 0, :], pS[:, k, :, 0], own, None, ALU.add))
                    if oth is None:
                        ch.done(dve.tensor_scalar(sc[:, 1, :], pS[:, k, :, 1], 1.0, None, ALU.mult))
                    else:
                        ch.done(dve.tensor_scalar(sc[:, 1, :], pS[:, k, :, 1], oth, None, ALU.add))
                    ch.done(dve.tensor_scalar(sc[:, 2, :], sc[:, 1, :], g["slope"][k], None, ALU.mult))
                    ch.done(dve.tensor_reduce(MX[:, k:k + 1], sc[:, 1, :], AXX, ALU.max, apply_absolute_value=True))
                dve.nop().then_inc(mx_rdy, 1)
                dve.wait_ge(mx_all, 1)
                ch.done(dve.tensor_scalar(g["lift"][:, :], MR[:, :], 1.0, None, ALU.add))
                for k in range(2):
                    ch.done(dve.tensor_scalar(g["score"][k][:, 3, :], g["score"][k][:, 1, :], g["lift"][:, k:k + 1],
                                              None, ALU.add))


def transpose_adj(net, g):
    nc, NB, NC, JS, PW = net.nc, net.NB, net.NC, net.JS, net.PW
    RING, TILES = 8, SUBS * IB
    MOPS = 2 * NB
    TC = JS * P
    stage, store, ident = g["stage"], g["store"], g["ident"]
    with ExitStack() as c:
        A = net.sb(c, "adj_rows", [P, RING, TC], F32)
        MA = net.sb(c, "max_acc", [P, 2, CI], F32)
        pT = net.ps(c, "p_adjT", [P, 2, JS, P])
        pM = net.ps(c, "p_max", [P, 2, IB, P])
        pD = net.ps(c, "p_deg", [P, IB])
        ld = [net.sem(f"b_ld{k}") for k in range(RING)]
        transposed, staged = net.sem("b_transposed"), net.sem("b_staged")
        stored = [net.sem(f"b_stored{k}") for k in range(SUBS)]
        degs, deg_read = net.sem("b_degrees"), net.sem("b_degree_read")
        maxed, max_ps, max_read = net.sem("b_maxed"), net.sem("b_max_ps"), net.sem("b_max_read")
        rows = net.dram["adj"].rearrange("(c i p) j -> p c i j", p=P, i=IB)

        def degree(pe, cc, q):
            pe.wait_ge(staged, cc * TILES + (q + 1) * IB + 2)
            if q == 0:
                pe.wait_ge(deg_read, cc)
            net.met(pe)
            for k in range(JS):
                for i in range(IB):
                    last = pe.matmul(pD[:, i:i + 1], stage[:, q, k, i * P:(i + 1) * P], g["ones16"][:, 0:1],
                                     start=(q == 0 and k == 0 and i == 0), stop=(q == SUBS - 1 and k == JS - 1),
                                     skip_group_check=True)
            last.then_inc(degs, 1)

        with nc.Block() as block:
            @block.sync
            def _(sp):
                def load(cc, t):
                    sp.dma_start(A[:, t % RING, :], rows[:, cc, t % IB, (t // IB) * TC:(t // IB + 1) * TC]
                                 if isinstance(cc, int) else
                                 rows[:, ds(cc, 1), t % IB, (t // IB) * TC:(t // IB + 1) * TC].rearrange("p c j -> p (c j)")
                                 ).then_inc(ld[t % RING], 16)
                for t in range(RING):
                    load(0, t)
                with sp.Fori(0, NC - 1) as cc:
                    for t in range(RING, TILES + RING):
                        sp.wait_ge(transposed, cc * TILES + (t - RING + 1))
                        load(cc if t < TILES else cc + 1, t % TILES)
                for t in range(RING, TILES):
                    sp.wait_ge(transposed, (NC - 1) * TILES + t - RING + 1)
                    load(NC - 1, t)

            @block.tensor
            def _(pe):
                pe.sem_inc(degs, SUBS)
                with pe.Fori(0, NC) as cc:
                    for t in range(TILES):
                        q, i = t // IB, t % IB
                        pe.wait_ge(ld[t % RING], cc * (16 * TILES // RING) + 16 * (t // RING + 1))
                        pe.wait_ge(staged, cc * TILES + t + 1)
                        for k in range(JS):
                            last = pe.transpose(pT[:, t % 2, k, :], A[:, t % RING, k * P:(k + 1) * P], ident[:, :])
                        last.then_inc(transposed, 1)
                        if t % IB == 1 and t > IB:
                            degree(pe, cc, q - 1)
                    degree(pe, cc, SUBS - 1)
                    pe.wait_ge(maxed, cc * MOPS + 2 * MOPS)
                    pe.wait_ge(max_read, cc)
                    for k in range(2):
                        for i in range(IB):
                            last = pe.transpose(pM[:, k, i, :], MA[:, k, i * P:(i + 1) * P], ident[:, :])
                    last.then_inc(max_ps, 1)

            @block.scalar
            def _(act):
                act.sem_inc(staged, 2)
                with act.Fori(0, NC) as cc:
                    for t in range(TILES):
                        q, i = t // IB, t % IB
                        if i == 0:
                            act.wait_ge(stored[q], cc * 16)
                            act.wait_ge(degs, cc * SUBS + q + 1)
                            act.wait_ge(maxed, cc * MOPS + (q + 1) * MOPS // SUBS)
                        act.wait_ge(transposed, cc * TILES + t + 1)
                        net.met(act)
                        nc.scalar.activation(stage[:, q, :, i * P:(i + 1) * P], pT[:, t % 2, :, :], ACT.Copy,
                                             scale=ONE, saturate=False).then_inc(staged, 1)

            @block.gpsimd
            def _(pool):
                with pool.Fori(0, NC - 1) as cc:
                    for q in range(SUBS):
                        pool.wait_ge(staged, cc * TILES + (q + 1) * IB + 2)
                        pool.dma_start(store[:, ds(cc * (SUBS * PW) + q * PW, PW)],
                                       stage[:, q, :, :].rearrange("p k i -> p (k i)").bitcast(U32)).then_inc(stored[q], 16)
                for q in range(SUBS):
                    pool.wait_ge(staged, (NC - 1) * TILES + (q + 1) * IB + 2)
                    pool.dma_start(g["last_chunk"][:, q, :],
                                   stage[:, q, :, :].rearrange("p k i -> p (k i)").bitcast(U32)).then_inc(stored[q], 16)
                for q in range(SUBS):
                    pool.wait_ge(stored[q], NC * 16)

            @block.vector
            def _(dve):
                dve.sem_inc(maxed, MOPS)
                with dve.Fori(0, NC) as cc:
                    dve.wait_ge(max_ps, cc)
                    for q in range(SUBS):
                        dve.wait_ge(staged, cc * TILES + (q + 1) * IB + 2)
                        for k in range(JS):
                            jt = q * JS + k
                            for m in range(2):
                                s = g["score"][m][:, 3, jt:jt + 1]
                                if jt > 0:
                                    dve.wait_ge(maxed, cc * MOPS + MOPS + 2 * jt + m - 1)
                                net.met(dve)
                                if jt == 0:
                                    dve.tensor_scalar(MA[:, m, :], stage[:, q, k, :], s, None, ALU.mult).then_inc(maxed, 1)
                                else:
                                    dve.scalar_tensor_tensor(MA[:, m, :], stage[:, q, k, :], s, MA[:, m, :],
                                                             ALU.mult, ALU.max).then_inc(maxed, 1)
                    dve.wait_ge(max_ps, cc + 1)
                    for m in range(2):
                        last = dve.tensor_reduce(g["top"][m][:, ds(cc * IB, IB)], pM[:, m, :, :], AXX, ALU.max)
                    last.then_inc(max_read, 1)
                    dve.wait_ge(degs, cc * SUBS + 2 * SUBS)
                    dve.tensor_scalar(g["deg"][:, ds(cc * IB, IB)], pD[:, :], 1.0 / ONE, None, ALU.mult).then_inc(deg_read, 1)


def load_pieces(sp, g, net, arrived, used, per_piece):
    SUBS_W = SUBS * net.PW

    def load(src, q):
        sp.dma_start(g["stage"][:, q, :, :].rearrange("p k i -> p (k i)").bitcast(U32), src).then_inc(arrived[q], 16)

    for q in range(SUBS):
        load(g["store"][:, q * net.PW:(q + 1) * net.PW], q)
    with sp.Fori(0, net.NC - 2) as cc:
        for q in range(SUBS):
            sp.wait_ge(used, cc * (SUBS * per_piece) + (q + 1) * per_piece)
            load(g["store"][:, ds(cc * SUBS_W + (SUBS_W + q * net.PW), net.PW)], q)
    for q in range(SUBS):
        sp.wait_ge(used, (net.NC - 2) * (SUBS * per_piece) + (q + 1) * per_piece)
        load(g["last_chunk"][:, q, :], q)


def attend_masked(net, g, m, H, num):
    nc, NB, NC, JS, D = net.nc, net.NB, net.NC, net.JS, net.D
    stage, ident, ones = g["stage"], g["ident"], g["ones"]
    sc, slope = g["score"][m], g["slope"][m]
    PAIRS = NB // 2
    RT = 4
    with ExitStack() as c:
        R = net.sb(c, f"rows{m}", [P, 2, net.N], F32)
        T = net.sb(c, f"logits{m}", [P, RT, 2, CI], F32)
        PR = net.sb(c, f"probs{m}", [P, 2, 2, CI], F32)
        O = net.sb(c, f"num_out{m}", [P, IB, D + 1], F32)
        RC = net.sb(c, f"row_cols{m}", [P, 3, NB], F32)
        acc = net.ps(c, f"p_acc{m}", [P, 2, 512])
        pR = net.ps(c, f"p_rows{m}", [P, 2, CI])
        pH = net.ps(c, f"p_hsum{m}", [P, D + 1])
        names = ("steps", "diag", "rows_ps", "rows_sb", "hsum", "branch", "logit", "exped", "masked", "summed",
                 "acc_read", "out_dma")
        (steps, diag, rows_ps, rows_sb, hs, branch, logit, exped, masked, summed,
         acc_read, out_dma) = (net.sem(f"c{m}_{n}") for n in names)
        arrived = [net.sem(f"c{m}_piece{k}") for k in range(SUBS)]
        num_rows = num.rearrange("(c i p) w -> p c i w", p=P, i=IB)

        def block_of(i):
            return acc[:, i // 2, (i % 2) * (D + 1):(i % 2 + 1) * (D + 1)]

        with nc.Block() as block:
            @block.sync
            def _(sp):
                load_pieces(sp, g, net, arrived, masked, JS // 2)

            @block.gpsimd
            def _(pool):
                with pool.Fori(0, NC) as cc:
                    pool.wait_ge(acc_read, cc + 2)
                    pool.dma_start(num_rows[:, ds(cc, 1), :, :].rearrange("p c i w -> p (c i) w"),
                                   O[:, :, :]).then_inc(out_dma, 16)
                pool.wait_ge(out_dma, NC * 16)

            @block.tensor
            def _(pe):
                for b in range(NB):
                    last = pe.matmul(pH[:, :], ones[:, :], H[:, b, :], start=b == 0, stop=b == NB - 1)
                last.then_inc(hs, 1)
                with pe.Fori(0, NC) as cc:
                    pe.wait_ge(diag, cc + 1)
                    pe.wait_ge(rows_sb, cc)
                    for k in range(2):
                        last = pe.matmul(pR[:, k, :], ones[:, :], T[:, 0, k, :], start=True, stop=True)
                    last.then_inc(rows_ps, 1)
                with pe.Fori(0, NC) as cc:
                    pe.wait_ge(acc_read, cc + 1)
                    for u in range(PAIRS):
                        pe.wait_ge(exped, cc * PAIRS + u + 1)
                        for k in range(2):
                            jt = 2 * u + k
                            for i in range(IB):
                                last = pe.matmul(block_of(i), PR[:, u % 2, k, i * P:(i + 1) * P], H[:, jt, :],
                                                 start=(jt == 0 and i % 2 == 0), stop=(jt == NB - 1),
                                                 skip_group_check=True)
                        last.then_inc(summed, 1)

            @block.scalar
            def _(act):
                with act.Fori(0, NC) as cc:
                    act.wait_ge(rows_ps, cc + 1)
                    net.met(act)
                    nc.scalar.copy(R[:, :, ds(cc * CI, CI)], pR[:, :, :]).then_inc(rows_sb, 1)
                act.wait_ge(rows_sb, NC)
                act.sem_inc(acc_read, 1)

                def slope_branch(cc, u):
                    act.wait_ge(exped, cc * PAIRS + max(u - RT + 1, 0))
                    net.met(act)
                    for k in range(2):
                        last = nc.scalar.activation(T[:, u % RT, k, :], R[:, 1, ds(cc * CI, CI)], ACT.Identity,
                                                    bias=sc[:, 2, 2 * u + k:2 * u + k + 1])
                    last.then_inc(branch, 1)

                with act.Fori(0, NC) as cc:
                    slope_branch(cc, 0)
                    slope_branch(cc, 1)
                    for u in range(PAIRS):
                        if u + 2 < PAIRS:
                            slope_branch(cc, u + 2)
                        act.wait_ge(masked, cc * PAIRS + u + 1)
                        act.wait_ge(summed, cc * PAIRS + max(u - 1, 0))
                        nc.scalar.activation(PR[:, u % 2, :, :], T[:, u % RT, :, :], ACT.Exp).then_inc(exped, 1)
                    act.wait_ge(summed, cc * PAIRS + PAIRS)
                    act.wait_ge(out_dma, cc * 16)
                    nc.scalar.copy(O[:, :, :].rearrange("p (a b) w -> p a (b w)", a=2),
                                   acc[:, :, 0:2 * (D + 1)]).then_inc(acc_read, 1)

            @block.vector
            def _(dve):
                ch = Chain(dve, steps)
                top = RC[:, 2, :]
                ch.done(dve.tensor_scalar(top, g["top"][m][:, :], 1.0 / ONE, g["lift"][:, m:m + 1], ALU.mult, ALU.subtract))
                ch.done(dve.tensor_tensor(top, top, sc[:, 0, :], ALU.add))
                ch.done(dve.scalar_tensor_tensor(top, top, slope, top, ALU.mult, ALU.max))
                ch.done(dve.tensor_tensor(RC[:, 0, :], sc[:, 0, :], top, ALU.subtract))
                ch.done(dve.scalar_tensor_tensor(RC[:, 1, :], sc[:, 0, :], slope, top, ALU.mult, ALU.subtract))
                with dve.Fori(0, NC) as cc:
                    dve.wait_ge(rows_ps, cc)
                    for k in range(2):
                        last = dve.tensor_tensor(T[:, 0, k, :].rearrange("p (i f) -> p i f", i=IB),
                                                 ident[:, :].unsqueeze(1).to_broadcast([P, IB, P]),
                                                 RC[:, k, ds(cc * IB, IB)].unsqueeze(2).to_broadcast([P, IB, P]),
                                                 ALU.mult)
                    last.then_inc(diag, 1)
                dve.wait_ge(hs, 1)
                dve.tensor_copy(g["hsum"][:, 0:D + 1], pH[:, :])
                dve.wait_ge(rows_sb, NC)

                def logits(cc, u):
                    dve.wait_ge(branch, cc * PAIRS + u + 1)
                    for k in range(2):
                        last = dve.scalar_tensor_tensor(T[:, u % RT, k, :], R[:, 0, ds(cc * CI, CI)],
                                                        sc[:, 1, 2 * u + k:2 * u + k + 1], T[:, u % RT, k, :],
                                                        ALU.add, ALU.max)
                    last.then_inc(logit, 1)

                with dve.Fori(0, NC) as cc:
                    logits(cc, 0)
                    for u in range(PAIRS):
                        if u + 1 < PAIRS:
                            logits(cc, u + 1)
                        q, k0 = 2 * u // JS, 2 * u % JS
                        if k0 == 0:
                            dve.wait_ge(arrived[q], cc * 16 + 16)
                        dve.wait_ge(logit, cc * PAIRS + u + 1)
                        dve.scalar_tensor_tensor(T[:, u % RT, :, :], stage[:, q, k0:k0 + 2, :].bitcast(U8), float(ONE_BYTE),
                                                 T[:, u % RT, :, :], ALU.subtract, ALU.min).then_inc(masked, 1)


def attend_cosine(net, g, XT, HL, DH, num):
    nc, NB, NC, JS, D = net.nc, net.NB, net.NC, net.JS, net.D
    stage = g["stage"]
    PAIRS = NB // 2
    WH = 2 * D + 1
    WO = WH + D
    with ExitStack() as c:
        E = net.sb(c, "cos_exp", [P, 2, 2, CI], F32)
        PH = net.sb(c, "cos_hi", [P, 2, 2, CI], F16)
        PL = net.sb(c, "cos_lo", [P, 2, 2, CI], F16)
        O = net.sb(c, "cos_out", [P, IB, WO], F32)
        acc = net.ps(c, "p_cos_acc", [P, IB, 512])
        pS = net.ps(c, "p_cos", [P, 2, 2, CI])
        names = ("hsum", "hsum_read", "cos", "exped", "prob", "hi", "lo", "summed", "acc_read", "out_dma")
        (hs, hs_read, cos, exped, prob, hi, lo, summed, acc_read, out_dma) = (net.sem(f"d_{n}") for n in names)
        arrived = [net.sem(f"d_piece{k}") for k in range(SUBS)]
        num_rows = num.rearrange("(c i p) w -> p c i w", p=P, i=IB)

        with nc.Block() as block:
            @block.sync
            def _(sp):
                load_pieces(sp, g, net, arrived, summed, JS // 2)

            @block.gpsimd
            def _(pool):
                with pool.Fori(0, NC) as cc:
                    pool.wait_ge(acc_read, cc + 2)
                    pool.dma_start(num_rows[:, ds(cc, 1), :, :].rearrange("p c i w -> p (c i) w"),
                                   O[:, :, :]).then_inc(out_dma, 16)
                pool.wait_ge(out_dma, NC * 16)

            @block.tensor
            def _(pe):
                for b in range(NB):
                    last = pe.matmul(acc[:, 0, 0:WH], g["ones16"][:, :], HL[:, b, :], start=b == 0, stop=b == NB - 1)
                last.then_inc(hs, 1)
                pe.wait_ge(hs_read, 1)

                def cosines(cc, u):
                    pe.wait_ge(exped, cc * PAIRS + u + 1)
                    for k in range(2):
                        jt = 2 * u + k
                        for n, (a, b) in enumerate(((0, 0), (0, 1), (1, 0))):
                            last = pe.matmul(pS[:, u % 2, k, :], XT[:, a, jt * P:(jt + 1) * P],
                                             XT[:, b, ds(cc * CI, CI)], start=n == 0, stop=n == 2)
                    last.then_inc(cos, 1)

                with pe.Fori(0, NC) as cc:
                    cosines(cc, 0)
                    cosines(cc, 1)
                    pe.wait_ge(acc_read, cc + 1)
                    for u in range(PAIRS):
                        q, k0 = 2 * u // JS, 2 * u % JS
                        if k0 == 0:
                            pe.wait_ge(arrived[q], cc * 16 + 16)
                        pe.wait_ge(lo, cc * PAIRS + u + 1)
                        for k in range(2):
                            jt = 2 * u + k
                            for i in range(IB):
                                blk = slice(i * P, (i + 1) * P)
                                adj = stage[:, q, k0 + k, blk]
                                first, end = jt == 0, jt == NB - 1
                                pe.matmul(acc[:, i, 0:WH], PH[:, u % 2, k, blk], HL[:, jt, :],
                                          start=first, stop=end, skip_group_check=True)
                                pe.matmul(acc[:, i, D:WH], PL[:, u % 2, k, blk], HL[:, jt, D:WH],
                                          start=False, stop=end, skip_group_check=True)
                                for part in range(2):
                                    last = pe.matmul(acc[:, i, WH:WO], adj, DH[:, part, jt, :],
                                                     start=False, stop=end, skip_group_check=True)
                        last.then_inc(summed, 1)
                        if u + 2 < PAIRS:
                            cosines(cc, u + 2)

            @block.scalar
            def _(act):
                act.sem_inc(acc_read, 1)
                act.sem_inc(exped, 2)

                def exps(cc, u):
                    act.wait_ge(cos, cc * PAIRS + u + 1)
                    act.wait_ge(lo, cc * PAIRS + max(u - 1, 0))
                    nc.scalar.activation(E[:, u % 2, :, :], pS[:, u % 2, :, :], ACT.Exp, bias=g["neg_shift"][:, 0:1],
                                         scale=g["beta"][:, 0:1]).then_inc(exped, 1)

                with act.Fori(0, NC) as cc:
                    exps(cc, 0)
                    for u in range(PAIRS):
                        if u + 1 < PAIRS:
                            exps(cc, u + 1)
                        act.wait_ge(prob, cc * PAIRS + u + 1)
                        act.wait_ge(summed, cc * PAIRS + max(u - 1, 0))
                        nc.scalar.copy(PH[:, u % 2, :, :], E[:, u % 2, :, :]).then_inc(hi, 1)
                    act.wait_ge(summed, cc * PAIRS + PAIRS)
                    act.wait_ge(out_dma, cc * 16)
                    nc.scalar.mul(O[:, :, :], acc[:, :, 0:WO], 1.0 / ONE).then_inc(acc_read, 1)

            @block.vector
            def _(dve):
                dve.wait_ge(hs, 1)
                dve.tensor_copy(g["hsum"][:, 0:WH], acc[:, 0, 0:WH]).then_inc(hs_read, 1)

                def probs(cc, u):
                    q, k0 = 2 * u // JS, 2 * u % JS
                    if k0 == 0:
                        dve.wait_ge(arrived[q], cc * 16 + 16)
                    dve.wait_ge(exped, cc * PAIRS + u + 3)
                    net.met(dve)
                    dve.scalar_tensor_tensor(E[:, u % 2, :, :], E[:, u % 2, :, :], g["exp_shift"][:, 0:1],
                                             stage[:, q, k0:k0 + 2, :], ALU.subtract, ALU.mult).then_inc(prob, 1)

                with dve.Fori(0, NC) as cc:
                    probs(cc, 0)
                    for u in range(PAIRS):
                        if u + 1 < PAIRS:
                            probs(cc, u + 1)
                        dve.wait_ge(hi, cc * PAIRS + u + 1)
                        dve.tensor_tensor(PL[:, u % 2, :, :], E[:, u % 2, :, :], PH[:, u % 2, :, :],
                                          ALU.subtract).then_inc(lo, 1)


def update(net, g, kind, NUM, X, x_src, num, x_dst, XT=None, HL=None, DH=None, HT=None, NT=None):
    nc, NB, D = net.nc, net.NB, net.D
    full = [P, NB, D]
    XC = g["stage"].rearrange("p q k i -> p (q k i)").bitcast(F32).rearrange("p (b d) -> p b d", b=NB)
    h, ident, st = NUM[:, :, 0:D], g["ident"], g["ln_cols"]
    with ExitStack() as c:
        W = net.sb(c, f"w_up{kind}", [P, D], F32) if kind == 0 else None
        TT = net.sb(c, f"tt_up{kind}", [P, 2, 4, P], F32) if kind == 0 else None
        pT = net.ps(c, f"p_up_t{kind}", [P, 2, 4, P])
        pW = net.ps(c, f"p_up_w{kind}", [P, 2, 4, P])
        names = ("ld", "ld_x", "ld_lo", "steps", "act_steps", "att", "tr_ps", "tr_sb", "tr_sb2", "w_ps", "w_read", "need_root",
                 "root_done", "xdone", "xout", "ask", "told", "turned")
        (ld, ld_x, ld_lo, steps, act_steps, att, tr_ps, tr_sb, tr_sb2, w_ps, w_read, need_root, root_done, xdone, xout,
         ask, told, turned) = (net.sem(f"u{kind}_{n}") for n in names)
        G = NB // 4

        with nc.Block() as block:
            @block.sync
            def _(sp):
                rows = rows_view(num)
                if kind == 1:
                    sp.dma_start(NUM[:, :, :], rows[:, :, D:2 * D + 1]).then_inc(ld, 16)
                    sp.dma_start(XC, rows[:, :, 0:D]).then_inc(ld_lo, 16)
                    sp.dma_start(DH[:, :, :], rows[:, :, 2 * D + 1:3 * D + 1]).then_inc(ld_lo, 16)
                else:
                    sp.dma_start(NUM[:, :, :], rows).then_inc(ld, 16)
                sp.dma_start(X[:, :, :], rows_view(x_src)).then_inc(ld_x, 16)
                if kind == 0:
                    sp.dma_start(W[:, :], net.dram["L0_gnn_W"]).then_inc(ld_x, 16)
                sp.wait_ge(xdone, 1)
                sp.dma_start(rows_view(x_dst), X[:, :, :]).then_inc(xout, 16)
                sp.wait_ge(xout, 16)

            @block.vector
            def _(dve):
                ch = Chain(dve, steps)
                e, rz = st[:, 0, :], st[:, 1, :]
                dve.wait_ge(ld, 16)
                if kind == 1:
                    dve.wait_ge(ld_lo, 32)
                    hs = g["hsum"]
                    ch.done(dve.tensor_tensor(hs[:, D:2 * D], hs[:, D:2 * D], hs[:, 0:D], ALU.add))
                    ch.done(dve.tensor_scalar(hs[:, D:2 * D + 1], hs[:, D:2 * D + 1], g["exp_shift"][:, 0:1], None, ALU.mult))
                    ch.done(dve.tensor_tensor(h, h, XC, ALU.add))
                    ch.done(dve.tensor_tensor(NUM[:, :, :], NUM[:, :, :],
                                              hs[:, D:2 * D + 1].unsqueeze(1).to_broadcast([P, NB, D + 1]), ALU.add))
                else:
                    ch.done(dve.tensor_scalar(e, g["deg"][:, :], 0.5, None, ALU.is_lt))
                    for b in range(NB):
                        last = dve.scalar_tensor_tensor(NUM[:, b, :], g["hsum"][:, 0:D + 1], e[:, b:b + 1], NUM[:, b, :],
                                                        ALU.mult, ALU.add)
                    ch.done(last)
                ch.done(dve.reciprocal(rz, NUM[:, :, D]))
                wide = rz.unsqueeze(2).to_broadcast(full)
                dve.wait_ge(ld_x, 32 if kind == 0 else 16)
                if kind == 0:
                    ch.done(dve.tensor_tensor(XC, h, wide, ALU.mult))
                    dve.nop().then_inc(att, 1)
                    for n in range(G):
                        dve.wait_ge(w_ps, n + 1)
                        last = dve.tensor_tensor(X[:, 4 * n:4 * n + 4, :], X[:, 4 * n:4 * n + 4, :], pW[:, n % 2, :, :],
                                                 ALU.add)
                        last.then_inc(w_read, 1)
                    dve.wait_ge(w_read, G)
                elif kind == 1:
                    ch.done(dve.tensor_tensor(DH[:, :, :], DH[:, :, :], g["dis"][:, :].unsqueeze(2).to_broadcast(full), ALU.mult))
                    ch.done(dve.tensor_tensor(X[:, :, :], X[:, :, :], DH[:, :, :], ALU.add))
                    ch.done(dve.tensor_tensor(XC, h, wide, ALU.mult))
                    ch.done(dve.scalar_tensor_tensor(X[:, :, :], XC, g["sig"][:, 0:1], X[:, :, :], ALU.mult, ALU.add))
                else:
                    ch.done(dve.tensor_tensor(XC, h, wide, ALU.mult))
                    ch.done(dve.tensor_tensor(X[:, :, :], X[:, :, :], XC, ALU.add))
                if kind != 0:
                    dve.nop().then_inc(xdone, 1)
                layernorm_relu(net, dve, ch, X[:, :, :], XC, h, st, need_root, root_done)
                if kind == 0:
                    nsq, tmp, r = st[:, 0, :], st[:, 1, :], st[:, 2, :]
                    dve.nop().then_inc(ask, 1)
                    dve.wait_ge(told, 1)
                    ch.done(dve.tensor_reduce(nsq, XC, AXX, ALU.add))
                    ch.done(dve.tensor_scalar(nsq, nsq, COS_EPS * COS_EPS, None, ALU.max))
                    ch.done(dve.reciprocal(tmp, nsq))
                    ch.done(dve.tensor_scalar(st[:, 3, :], g["deg"][:, :], 1.0, None, ALU.max))
                    ch.done(dve.reciprocal(g["dis"][:, :], st[:, 3, :]))
                    dve.nop().then_inc(ask, 1)
                    dve.wait_ge(told, 3)
                    newton_rsqrt(dve, ch, r, nsq, tmp)
                    newton_rsqrt(dve, ch, g["dis"][:, :], st[:, 3, :], tmp)
                    ch.done(dve.tensor_tensor(XC, h, r.unsqueeze(2).to_broadcast(full), ALU.mult))
                    dve.nop().then_inc(att, 1)
                    ch.done(dve.tensor_scalar(tmp[:, 0:1], g["sig"][:, :], -1.0, -1.0, ALU.mult, ALU.add))
                    ch.done(dve.scalar_tensor_tensor(X[:, :, :], h, tmp[:, 0:1], X[:, :, :], ALU.mult, ALU.add))
                    dve.nop().then_inc(xdone, 1)
                    dve.wait_ge(told, 4)
                    dve.tensor_tensor(HL[:, :, 0:D], h, HL[:, :, D:2 * D], ALU.subtract)
                    dve.memset(HL[:, :, 2 * D:2 * D + 1], 1.0)
                    for n in range(G):
                        dve.wait_ge(tr_sb, G + n + 1)
                        dve.tensor_tensor(XT[:, 1, 4 * n * P:4 * (n + 1) * P], pT[:, n % 2, :, :].rearrange("p k i -> p (k i)"),
                                          XT[:, 0, 4 * n * P:4 * (n + 1) * P], ALU.subtract).then_inc(turned, 1)
                    dve.wait_ge(turned, G)
                    ch.done(dve.tensor_tensor(XC, h, g["dis"][:, :].unsqueeze(2).to_broadcast(full), ALU.mult))
                    dve.nop().then_inc(ask, 1)
                    dve.wait_ge(told, 5)
                    dve.tensor_tensor(DH[:, 1, :, :], XC, DH[:, 0, :, :], ALU.subtract)
                elif kind == 1:
                    dve.memset(NUM[:, :, D:D + 1], 1.0)
                else:
                    dve.nop().then_inc(att, 1)
                    dve.nop().then_inc(ask, 1)
                    dve.wait_ge(told, 1)
                    dve.tensor_tensor(NT[:, 1, :, :], h, NT[:, 0, :, :], ALU.subtract)

            @block.tensor
            def _(pe):
                def turn(n, first, src, freed, need):
                    if n >= 2:
                        pe.wait_ge(freed, need + n - 1)
                    for k in range(4):
                        last = pe.transpose(pT[:, n % 2, k, :], src(4 * n + k), ident[:, :])
                    last.then_inc(tr_ps, 1)
                if kind == 0:
                    pe.wait_ge(att, 1)
                    for n in range(G + 1):
                        if n < G:
                            turn(n, 0, lambda b: XC[:, b, :], tr_sb, 0)
                        if n >= 1:
                            pe.wait_ge(tr_sb, n)
                            if n >= 3:
                                pe.wait_ge(w_read, n - 2)
                            for k in range(4):
                                last = pe.matmul(pW[:, (n - 1) % 2, k, :], TT[:, (n - 1) % 2, k, :], W[:, :],
                                                 start=True, stop=True, skip_group_check=True)
                            last.then_inc(w_ps, 1)
                    pe.wait_ge(att, 2)
                    for n in range(G):
                        turn(n, 1, lambda b: XC[:, b, :], turned, 0)
                elif kind == 2:
                    pe.wait_ge(att, 1)
                    for n in range(G):
                        turn(n, 0, lambda b: h[:, b, :], tr_sb, 0)

            @block.scalar
            def _(act):
                if kind == 0:
                    for n in range(G):
                        act.wait_ge(tr_ps, n + 1)
                        if n >= 2:
                            act.wait_ge(w_ps, n - 1)
                        nc.scalar.copy(TT[:, n % 2, :, :], pT[:, n % 2, :, :]).then_inc(tr_sb, 1)
                layernorm_scalar_part(act, nc, XC, h, st, need_root, root_done)
                if kind == 0:
                    act.wait_ge(ask, 1)
                    nc.scalar.activation(XC, h, ACT.Square).then_inc(told, 1)
                    act.wait_ge(ask, 2)
                    nc.scalar.activation(st[:, 2, :], st[:, 1, :], ACT.Sqrt).then_inc(told, 1)
                    nc.scalar.activation(g["dis"][:, :], g["dis"][:, :], ACT.Sqrt).then_inc(told, 1)
                    nc.scalar.copy(HL[:, :, D:2 * D], h).then_inc(told, 1)
                    for n in range(G):
                        act.wait_ge(tr_ps, G + n + 1)
                        nc.scalar.copy(XT[:, 0, 4 * n * P:4 * (n + 1) * P],
                                       pT[:, n % 2, :, :].rearrange("p k i -> p (k i)")).then_inc(tr_sb, 1)
                    act.wait_ge(ask, 3)
                    act.wait_ge(xout, 16)
                    nc.scalar.copy(DH[:, 0, :, :], XC).then_inc(told, 1)
                elif kind == 2:
                    act.wait_ge(ask, 1)
                    nc.scalar.copy(NT[:, 0, :, :], h).then_inc(told, 1)
                    for n in range(G):
                        act.wait_ge(tr_ps, n + 1)
                        nc.scalar.copy(HT[:, 4 * n * P:4 * (n + 1) * P],
                                       pT[:, n % 2, :, :].rearrange("p k i -> p (k i)")).then_inc(tr_sb, 1)


def chebyshev(net, g, layer, W, B, HT, NT, N2, x_src, out):
    nc, NB, NC, JS, D = net.nc, net.NB, net.NC, net.JS, net.D
    stage, ident = g["stage"], g["ident"]
    with ExitStack() as c:
        T1 = net.sb(c, f"cheb_t{layer}", [P, 2, CI], F32)
        EX = net.sb(c, f"cheb_e{layer}", [P, 2, CI], F32)
        XR = net.sb(c, f"cheb_x{layer}", [P, IB, D], F32)
        pA = net.ps(c, f"p_prod{layer}", [P, 2, CI])
        pN = net.ps(c, f"p_nat{layer}", [P, IB, P])
        pO = net.ps(c, f"p_out{layer}", [P, CI])

        for product in range(2):
            names = ("used", "prod", "t1", "nat", "nat_hi", "nat_lo", "part", "part_read", "z", "ex", "xin", "y", "ynat", "xout", "steps")
            (used, prod, t1, nat, nat_hi, nat_lo, part, part_read, zs, ex, xin, ys, ynat, xout, steps) = (
                net.sem(f"e{layer}{product}_{n}") for n in names)
            arrived = [net.sem(f"e{layer}{product}_piece{k}") for k in range(SUBS)]
            SRC = NT if product == 0 else N2
            final = product == 1 and layer == 1
            xr_in = x_src.rearrange("(c i p) w -> p c i w", p=P, i=IB)
            xr_out = out.rearrange("(c i p) w -> p c i w", p=P, i=IB)

            with nc.Block() as block:
                @block.sync
                def _(sp):
                    load_pieces(sp, g, net, arrived, used, 1)

                @block.gpsimd
                def _(pool):
                    if final:
                        with pool.Fori(0, NC) as cc:
                            pool.wait_ge(xout, cc * 16)
                            pool.dma_start(XR[:, :, :], xr_in[:, ds(cc, 1), :, :].rearrange("p c i w -> p (c i) w")
                                           ).then_inc(xin, 16)
                            pool.wait_ge(ynat, cc + 1)
                            net.met(pool)
                            pool.dma_start(xr_out[:, ds(cc, 1), :, :].rearrange("p c i w -> p (c i) w"),
                                           XR[:, :, :]).then_inc(xout, 16)
                        pool.wait_ge(xout, NC * 16)

                @block.tensor
                def _(pe):
                    def product_rows(cc, half):
                        for jt in range(NB):
                            q, k = jt // JS, jt % JS
                            if k == 0:
                                pe.wait_ge(arrived[q], cc * 16 + 16)
                                net.met(pe)
                            for part_ in range(2):
                                last = pe.matmul(pA[:, half, :], SRC[:, part_, jt, :], stage[:, q, k, :],
                                                 start=jt == 0 and part_ == 0, stop=jt == NB - 1 and part_ == 1)
                            if k == JS - 1:
                                last.then_inc(used, 1)

                    def weights(cc, half):
                        pe.wait_ge(t1, cc + 1)
                        if product == 0:
                            pe.wait_ge(nat_lo, cc)
                            for i in range(IB):
                                last = pe.transpose(pN[:, i, :], T1[:, half, i * P:(i + 1) * P], ident[:, :])
                            last.then_inc(nat, 1)
                            pe.wait_ge(part_read, cc)
                            pe.matmul(pO[:, :], W[:, 0, :], HT[:, ds(cc * CI, CI)], start=True, stop=False)
                            pe.matmul(pO[:, :], W[:, 1, :], T1[:, half, :], start=False, stop=True).then_inc(part, 1)
                        else:
                            pe.wait_ge(part_read, cc)
                            pe.matmul(pO[:, :], W[:, 2, :], T1[:, half, :], start=True, stop=True).then_inc(part, 1)

                    def rows_back(cc):
                        pe.wait_ge(ys, cc + 1)
                        for i in range(IB):
                            last = pe.transpose(pN[:, i, :], EX[:, 0, i * P:(i + 1) * P], ident[:, :])
                        last.then_inc(nat, 1)

                    with pe.Fori(0, NC // 2) as pp:
                        pe.wait_ge(t1, pp * 2)
                        for half in range(2):
                            product_rows(pp * 2 + half, half)
                        for half in range(2):
                            weights(pp * 2 + half, half)
                            if final:
                                rows_back(pp * 2 + half)

                @block.scalar
                def _(act):
                    with act.Fori(0, NC // 2) as pp:
                        act.wait_ge(part, pp * 2)
                        for half in range(2):
                            act.wait_ge(used, pp * (2 * SUBS) + (half + 1) * SUBS)
                            nc.scalar.mul(T1[:, half, :], pA[:, half, :], 1.0 / ONE).then_inc(t1, 1)
                        for half in range(2):
                            cc = pp * 2 + half
                            if product == 0:
                                act.wait_ge(nat, cc + 1)
                                net.met(act)
                                nc.scalar.copy(N2[:, 0, ds(cc * IB, IB), :], pN[:, :, :]).then_inc(nat_hi, 1)
                            else:
                                act.wait_ge(zs, cc + 1)
                                nc.scalar.activation(EX[:, 0, :], EX[:, 0, :], ACT.Exp).then_inc(ex, 1)

                @block.vector
                def _(dve):
                    with dve.Fori(0, NC) as cc:
                        cols = ds(cc * CI, CI)
                        if product == 0:
                            dve.wait_ge(nat_hi, cc + 1)
                            dve.tensor_tensor(N2[:, 1, ds(cc * IB, IB), :], pN[:, :, :], N2[:, 0, ds(cc * IB, IB), :],
                                              ALU.subtract).then_inc(nat_lo, 1)
                            dve.wait_ge(part, cc + 1)
                            dve.tensor_copy(HT[:, cols], pO[:, :]).then_inc(part_read, 1)
                        else:
                            dve.wait_ge(ys, cc)
                            dve.wait_ge(part, cc + 1)
                            dve.scalar_tensor_tensor(EX[:, 1, :], pO[:, :], B, HT[:, cols], ALU.add, ALU.add).then_inc(part_read, 1)
                            dve.wait_ge(part_read, cc + 1)
                            if final:
                                dve.wait_ge(ynat, cc)
                            dve.tensor_scalar(EX[:, 0, :], EX[:, 1, :], 0.0, None, ALU.min).then_inc(zs, 1)
                            dve.wait_ge(ex, cc + 1)
                            dve.tensor_scalar(EX[:, 1, :], EX[:, 1, :], 0.0, None, ALU.max).then_inc(steps, 1)
                            dve.wait_ge(steps, cc + 1)
                            dst = EX[:, 0, :] if final else HT[:, cols]
                            dve.scalar_tensor_tensor(dst, EX[:, 0, :], -1.0, EX[:, 1, :], ALU.add, ALU.add).then_inc(ys, 1)
                            if final:
                                dve.wait_ge(xin, cc * 16 + 16)
                                dve.wait_ge(nat, cc + 1)
                                dve.tensor_tensor(XR[:, :, :], XR[:, :, :], pN[:, :, :], ALU.add).then_inc(ynat, 1)


def rescale(net, g, W, HT, NT):
    nc, NB, NC, D = net.nc, net.NB, net.NC, net.D
    with ExitStack() as c:
        T = net.sb(c, "scaled", [P, 2, CI], F32)
        S = net.sb(c, "scales", [P, 2], F32)
        pN = net.ps(c, "p_scaled", [P, 2, IB, P])
        steps, sc, nat, hi, lo = (net.sem(f"f_{n}") for n in ("steps", "scaled", "nat", "hi", "lo"))
        def low_part(dve, n):
            blocks = slice(n * IB, (n + 1) * IB)
            dve.wait_ge(hi, n + 1)
            dve.tensor_tensor(NT[:, 1, blocks, :], pN[:, n % 2, :, :], NT[:, 0, blocks, :], ALU.subtract).then_inc(lo, 1)

        with nc.Block() as block:
            @block.vector
            def _(dve):
                ch = Chain(dve, steps)
                ch.done(dve.tensor_reduce(S[:, 0:1], HT[:, :], AXX, ALU.max, apply_absolute_value=True))
                ch.done(dve.tensor_scalar(S[:, 0:1], S[:, 0:1], 1e-30, 0.125, ALU.max, ALU.mult))
                ch.done(dve.reciprocal(S[:, 1:2], S[:, 0:1]))
                ch.done(dve.tensor_scalar(W[:, :, :], W[:, :, :], S[:, 0:1], None, ALU.mult))
                for n in range(NC):
                    cols = slice(n * CI, (n + 1) * CI)
                    if n >= 2:
                        dve.wait_ge(nat, n - 1)
                    ch.done(dve.tensor_scalar(T[:, n % 2, :], HT[:, cols], S[:, 1:2], None, ALU.mult))
                    dve.tensor_copy(HT[:, cols], T[:, n % 2, :]).then_inc(sc, 1)
                    if n >= 1:
                        low_part(dve, n - 1)
                low_part(dve, NC - 1)

            @block.tensor
            def _(pe):
                for n in range(NC):
                    pe.wait_ge(sc, n + 1)
                    if n >= 2:
                        pe.wait_ge(lo, n - 1)
                    for i in range(IB):
                        last = pe.transpose(pN[:, n % 2, i, :], T[:, n % 2, i * P:(i + 1) * P], g["ident"][:, :])
                    last.then_inc(nat, 1)

            @block.scalar
            def _(act):
                for n in range(NC):
                    act.wait_ge(nat, n + 1)
                    nc.scalar.copy(NT[:, 0, n * IB:(n + 1) * IB, :], pN[:, n % 2, :, :]).then_inc(hi, 1)


def cheb_weights(net, WL, BL):
    nc = net.nc
    ld, steps = net.sem("w_ld"), net.sem("w_steps")
    with nc.Block() as block:
        @block.sync
        def _(sp):
            for n in range(2):
                sp.dma_start(WL[n][:, :, :], net.dram[f"L3_gnn_W{n}"].rearrange("k d f -> d k f")).then_inc(ld, 16)
                sp.dma_start(BL[n][:, :], net.dram[f"L3_gnn_b{n}"].unsqueeze(1)).then_inc(ld, 16)

        @block.vector
        def _(dve):
            ch = Chain(dve, steps)
            dve.wait_ge(ld, 64)
            for n in range(2):
                ch.done(dve.tensor_tensor(WL[n][:, 0, :], WL[n][:, 0, :], WL[n][:, 2, :], ALU.subtract))
                ch.done(dve.tensor_scalar(WL[n][:, 2, :], WL[n][:, 2, :], 2.0, None, ALU.mult))


def gnn_stack(nc, dram, out):
    with ExitStack() as ctx:
        net = Net(nc, ctx, dram)
        N, D, NB, NC = net.N, net.D, net.NB, net.NC
        g = {"slope": (0.2, 0.01)}
        for name, shape, dt in (("ident", [P, P], F32), ("ones", [P, P], F32), ("ones16", [P, P], F16),
                                ("zero", [P, 1], F32), ("sig", [P, 1], F32), ("beta", [P, 1], F32),
                                ("neg_shift", [P, 1], F32), ("exp_shift", [P, 1], F32), ("lift", [P, 2], F32),
                                ("hsum", [P, 2 * D + 1], F32), ("deg", [P, NB], F32), ("dis", [P, NB], F32),
                                ("ln_cols", [P, 4, NB], F32),
                                ("store", [P, (NC - 1) * SUBS * net.PW], U32), ("stage", [P, SUBS, net.JS, CI], FP8)):
            g[name] = net.sb(ctx, name, shape, dt)
        g["score"] = [net.sb(ctx, f"score{k}", [P, 4, NB], F32) for k in range(2)]
        g["top"] = [net.sb(ctx, f"top{k}", [P, NB], F32) for k in range(2)]
        g["last_chunk"] = nc.dram_tensor("adj_last_chunk", [P, SUBS, net.PW], U32, kind="Internal").ap()
        xres = nc.dram_tensor("x_residual", [N, D], F32, kind="Internal").ap()
        num = nc.dram_tensor("weighted_sums", [N, D + 1], F32, kind="Internal").ap()
        num_cos = nc.dram_tensor("cosine_sums", [N, 3 * D + 1], F32, kind="Internal").ap()

        with ExitStack() as c:
            g["H"] = net.sb(c, "h_gat", [P, NB, D + 1], F32)
            setup(net, g)
            net.phase_end()
            transpose_adj(net, g)
            net.phase_end()
            attend_masked(net, g, 0, g["H"], num)
            net.phase_end()
        with ExitStack() as c:
            HL = net.sb(c, "h_lo_hi", [P, NB, 2 * D + 1], F16)
            XT = net.sb(c, "unit_rows_T", [P, 2, N], F16)
            DH = net.sb(c, "dis_h", [P, 2, NB, D], F16)
            with ExitStack() as c2:
                NUM = net.sb(c2, "num0", [P, NB, D + 1], F32)
                X = DH.rearrange("p a b d -> p (a b d)").bitcast(F32).rearrange("p (b d) -> p b d", b=NB)
                update(net, g, 0, NUM, X, dram["x"], num, xres, XT=XT, HL=HL, DH=DH)
                net.phase_end()
            attend_cosine(net, g, XT, HL, DH, num_cos)
            net.phase_end()
        with ExitStack() as c:
            H = net.sb(c, "num1", [P, NB, D + 1], F32)
            with ExitStack() as c2:
                X = net.sb(c2, "x1", [P, NB, D], F32)
                DS = net.sb(c2, "diffused", [P, NB, D], F32)
                update(net, g, 1, H, X, xres, num_cos, xres, DH=DS)
                net.phase_end()
            attend_masked(net, g, 1, H, num)
            net.phase_end()
        with ExitStack() as c:
            NT = net.sb(c, "h_parts", [P, 2, NB, D], F16)
            HT = net.sb(c, "h_T", [P, N], F32)
            WL = [net.sb(c, f"cheb_w{k}", [P, 3, D], F32) for k in range(2)]
            BL = [net.sb(c, f"cheb_b{k}", [P, 1], F32) for k in range(2)]
            cheb_weights(net, WL, BL)
            net.phase_end()
            with ExitStack() as c2:
                NUM = net.sb(c2, "num2", [P, NB, D + 1], F32)
                X = net.sb(c2, "x2", [P, NB, D], F32)
                update(net, g, 2, NUM, X, xres, num, xres, HT=HT, NT=NT)
                net.phase_end()
            N2 = net.sb(c, "Lh_parts", [P, 2, NB, D], F16)
            chebyshev(net, g, 0, WL[0], BL[0][:, 0:1], HT, NT, N2, xres, out)
            net.phase_end()
            rescale(net, g, WL[1], HT, NT)
            net.phase_end()
            chebyshev(net, g, 1, WL[1], BL[1][:, 0:1], HT, NT, N2, xres, out)
            net.phase_end()


_INS = ['x', 'adj', 'L0_gnn_W', 'L0_gnn_a1', 'L0_gnn_a2', 'L0_gnn_a_bias', 'L1_gnn_alpha', 'L1_gnn_beta',
        'L2_gnn_inlayer2', 'L2_gnn_W1', 'L2_gnn_w2', 'L2_gnn_b2', 'L2_gnn_w3', 'L2_gnn_b3',
        'L3_gnn_W0', 'L3_gnn_b0', 'L3_gnn_W1', 'L3_gnn_b1']


def kernel(**inputs):
    import numpy as _np
    import concourse.bacc as _bacc
    from concourse import mybir as _mybir
    from concourse.bass_utils import run_bass_kernel_spmd as _run

    nc = _bacc.Bacc("TRN2", target_bir_lowering=False, num_devices=1)
    arrays, dram = {}, {}
    for name in _INS:
        a = _np.ascontiguousarray(inputs[name])
        if a.ndim == 0:
            a = a.reshape(1)
        arrays[f"in_{name}_dram"] = a
        dram[name] = nc.dram_tensor(f"in_{name}_dram", a.shape, _mybir.dt.from_np(a.dtype), kind="ExternalInput").ap()
    out = nc.dram_tensor("out_0_dram", inputs["x"].shape, _mybir.dt.float32, kind="ExternalOutput").ap()
    gnn_stack(nc, dram, out)
    r = _run(nc, [arrays], core_ids=[0])
    return r.results[0]["out_0_dram"]
```

```python
from contextlib import ExitStack

import concourse.bass as bass
from concourse import mybir

ALU = mybir.AluOpType
ACT = mybir.ActivationFunctionType
AXX = mybir.AxisListType.X
F32 = mybir.dt.float32
F16 = mybir.dt.float16
BF16 = mybir.dt.bfloat16
FP8 = mybir.dt.float8e5
U8 = mybir.dt.uint8
U16 = mybir.dt.uint16
U32 = mybir.dt.uint32
RMAX = bass.bass_isa.ReduceOp.max
ds = bass.ds

P = 128
CI = 512
IB = CI // P
SUBS = 4
ONE = 32768.0
ONE_BYTE = 120
EPS = 1e-5
COS_EPS = 1e-8


class Chain:

    def __init__(self, eng, sem):
        self.eng, self.sem, self.n = eng, sem, 0

    def done(self, ins):
        self.n += 1
        ins.then_inc(self.sem, 1)
        self.eng.wait_ge(self.sem, self.n)


class Net:

    def __init__(self, nc, ctx, dram):
        self.nc, self.ctx, self.dram = nc, ctx, dram
        self.phase_sems = []
        self.passed, self.phase = {}, 0
        self.N, self.D = dram["x"].shape
        self.NB = self.N // P
        self.NC = self.N // CI
        self.JS = self.NB // SUBS
        self.PW = self.JS * CI // 4
        assert self.D == P and self.JS * SUBS == self.NB

    def sb(self, ctx, name, shape, dt):
        return ctx.enter_context(self.nc.sbuf_tensor(name, shape, dt))

    def ps(self, ctx, name, shape, dt=F32):
        return ctx.enter_context(self.nc.psum_tensor(name, shape, dt))

    def sem(self, name):
        s = self.nc.alloc_semaphore(name=name)
        self.phase_sems.append(s)
        return s

    def met(self, eng):
        key = str(eng.engine)
        if key not in self.passed:
            self.passed[key] = self.sem(f"passed{self.phase}_{len(self.passed)}")
        eng.sem_inc(self.passed[key], 1)

    def phase_end(self):
        self.nc.clear_and_free_semaphores(self.phase_sems)
        self.phase_sems, self.passed, self.phase = [], {}, self.phase + 1
        self.nc.all_engine_barrier()


def wait(eng, sem, value):
    if not (isinstance(value, int) and value <= 0):
        eng.wait_ge(sem, value)


def rotated(eng, last, first, step, head):
    for u in range(first[0]):
        step(0, u, False)
    with eng.Fori(0, last) as cc:
        for u in range(first[0], first[1]):
            step(cc, u, False)
        for u in range(first[0]):
            step(cc + 1, u, False)
            head(cc, u)
    for u in range(first[0], first[1]):
        step(last, u, True)
    for u in range(first[0]):
        head(last, u)


def rows_view(ap):
    return ap.rearrange("(b p) w -> p b w", p=P)


def newton_rsqrt(dve, ch, r, v, tmp):
    ch.done(dve.tensor_tensor(tmp, r, r, ALU.mult))
    ch.done(dve.tensor_tensor(tmp, tmp, v, ALU.mult))
    ch.done(dve.tensor_scalar(tmp, tmp, -0.5, 1.5, ALU.mult, ALU.add))
    ch.done(dve.tensor_tensor(r, r, tmp, ALU.mult))


def layernorm_relu(net, dve, ch, xt, xc, h, st, need_root, root_done):
    NB, D = net.NB, net.D
    full = [P, NB, D]
    mean, var, r, tmp = st[:, 0, :], st[:, 1, :], st[:, 2, :], st[:, 3, :]
    ch.done(dve.tensor_reduce(mean, xt, AXX, ALU.add))
    ch.done(dve.tensor_scalar(mean, mean, 1.0 / D, None, ALU.mult))
    dve.tensor_tensor(xc, xt, mean.unsqueeze(2).to_broadcast(full), ALU.subtract).then_inc(need_root, 1)
    dve.wait_ge(root_done, 1)
    ch.done(dve.tensor_reduce(var, h, AXX, ALU.add))
    ch.done(dve.tensor_scalar(var, var, 1.0 / D, EPS, ALU.mult, ALU.add))
    ch.done(dve.reciprocal(tmp, var))
    dve.nop().then_inc(need_root, 1)
    dve.wait_ge(root_done, 2)
    newton_rsqrt(dve, ch, r, var, tmp)
    ch.done(dve.scalar_tensor_tensor(h, xc, 0.0, r.unsqueeze(2).to_broadcast(full), ALU.max, ALU.mult))


def layernorm_scalar_part(act, nc, xc, h, st, need_root, root_done):
    act.wait_ge(need_root, 1)
    nc.scalar.activation(h, xc, ACT.Square).then_inc(root_done, 1)
    act.wait_ge(need_root, 2)
    nc.scalar.activation(st[:, 2, :], st[:, 3, :], ACT.Sqrt).then_inc(root_done, 1)


def setup(net, g):
    nc, dram, NB, D = net.nc, net.dram, net.NB, net.D
    E2 = dram["L2_gnn_inlayer2"].shape[1] // P
    with ExitStack() as c:
        X = net.sb(c, "x_in", [P, NB, D], F32)
        XC = net.sb(c, "x_centred", [P, NB, D], F32)
        IN2 = g["store"][:, 0:NB * E2 * D].bitcast(F32).rearrange("p (b e) -> p b e", b=NB)
        W = net.sb(c, "w_gat", [P, D], F32)
        W1 = net.sb(c, "w1_gat2", [P, E2 * D], F32)
        A12 = net.sb(c, "a12", [P, 2], F32)
        W23 = net.sb(c, "w23", [P, 2], F32)
        SC = net.sb(c, "scalars_in", [P, 5], F32)
        WT = net.sb(c, "w_gat_T", [P, D], F32)
        VC = net.sb(c, "score_vectors", [P, 1 + E2, 2], F32)
        TT = net.sb(c, "transposed", [P, 2, 4, P], F32)
        MX = net.sb(c, "absmax", [P, 2], F32)
        MR = net.sb(c, "absmax_all", [P, 2], F32)
        st = net.sb(c, "ln_cols_in", [P, 4, NB], F32)
        ident, H = g["ident"], g["H"]
        pW = net.ps(c, "p_wt", [P, D])
        pV = net.ps(c, "p_vec", [P, 1 + E2, 2])
        pT = net.ps(c, "p_tr", [P, 2, 4, P])
        pS = net.ps(c, "p_scores", [P, 2, NB, 2])
        ld_x, ld_in2, ld_w = net.sem("a_ld_x"), net.sem("a_ld_in2"), net.sem("a_ld_w")
        id0, id1 = net.sem("a_id0"), net.sem("a_ident")
        ch_s, pc_s = net.sem("a_dve_steps"), net.sem("a_act_steps")
        need_root, root_done = net.sem("a_need_root"), net.sem("a_root_done")
        wt_ps, wt_sb, vec_ps, vec_sb = (net.sem(n) for n in ("a_wt_ps", "a_wt_sb", "a_vec_ps", "a_vec_sb"))
        h_rdy, tr_ps, tr_sb, tr_used, sc_ps = (net.sem(n) for n in ("a_h", "a_tr_ps", "a_tr_sb", "a_tr_used", "a_sc_ps"))
        mx_rdy, mx_all = net.sem("a_mx"), net.sem("a_mx_all")
        GROUPS = [(0, b) for b in range(0, NB, 4)] + [(1 + e, b) for b in range(0, NB, 4) for e in range(E2)]

        with nc.Block() as block:
            @block.sync
            def _(sp):
                sp.dma_start(X[:, :, :], rows_view(dram["x"])).then_inc(ld_x, 16)
                sp.dma_start(IN2, rows_view(dram["L2_gnn_inlayer2"])).then_inc(ld_in2, 16)
                for dst, src in ((W[:, :], dram["L0_gnn_W"]), (W1[:, :], dram["L2_gnn_W1"]),
                                 (A12[:, 0:1], dram["L0_gnn_a1"].unsqueeze(1)), (A12[:, 1:2], dram["L0_gnn_a2"].unsqueeze(1)),
                                 (W23[:, 0:1], dram["L2_gnn_w2"].unsqueeze(1)), (W23[:, 1:2], dram["L2_gnn_w3"].unsqueeze(1))):
                    sp.dma_start(dst, src).then_inc(ld_w, 16)
                for k, n in enumerate(("L0_gnn_a_bias", "L2_gnn_b2", "L2_gnn_b3", "L1_gnn_alpha", "L1_gnn_beta")):
                    sp.dma_start(SC[:, k:k + 1], dram[n].partition_broadcast(P)).then_inc(ld_w, 16)

            @block.gpsimd
            def _(pool):
                nc.gpsimd.memset(ident[:, :], 0.0).then_inc(id0, 1)
                pool.wait_ge(id0, 1)
                nc.gpsimd.affine_select(out=ident[:, :], in_=ident[:, :], compare_op=ALU.not_equal, fill=1.0,
                                        base=0, pattern=[[-1, P]], channel_multiplier=1).then_inc(id1, 1)
                pool.wait_ge(mx_rdy, 1)
                nc.gpsimd.partition_all_reduce(MR[:, :], MX[:, :], P, RMAX).then_inc(mx_all, 1)

            @block.tensor
            def _(pe):
                pe.wait_ge(id1, 1)
                pe.wait_ge(ld_w, 16 * 11)
                pe.transpose(pW[:, :], W[:, :], ident[:, :]).then_inc(wt_ps, 1)
                pe.wait_ge(wt_sb, 1)
                pe.matmul(pV[:, 0, :], WT[:, :], A12[:, :], start=True, stop=True)
                for e in range(E2):
                    last = pe.matmul(pV[:, 1 + e, :], W1[:, e * P:(e + 1) * P], W23[:, :], start=True, stop=True)
                last.then_inc(vec_ps, 1)

                def project(n):
                    kind, b0 = GROUPS[n]
                    pe.wait_ge(tr_sb, n + 1)
                    for k in range(4):
                        last = pe.matmul(pS[:, 0 if kind == 0 else 1, b0 + k, :], TT[:, n % 2, k, :], VC[:, kind, :],
                                         start=kind == 0 or (kind == 1 and k == 0), stop=kind in (0, E2), skip_group_check=True)
                    last.then_inc(tr_used, 1)

                pe.wait_ge(h_rdy, 1)
                for n, (kind, b0) in enumerate(GROUPS):
                    if kind == 1 and b0 == 0:
                        pe.wait_ge(ld_in2, 16)
                    if n >= 2:
                        pe.wait_ge(tr_sb, n - 1)
                    for k in range(4):
                        src = H[:, b0 + k, 0:D] if kind == 0 else IN2[:, b0 + k, (kind - 1) * P:kind * P]
                        last = pe.transpose(pT[:, n % 2, k, :], src, ident[:, :])
                    last.then_inc(tr_ps, 1)
                    if n == 0:
                        pe.wait_ge(vec_sb, 1)
                    else:
                        project(n - 1)
                project(len(GROUPS) - 1)
                pe.wait_ge(tr_used, len(GROUPS))
                pe.nop().then_inc(sc_ps, 1)

            @block.scalar
            def _(act):
                n_ln = 0
                pc = Chain(act, pc_s)
                act.wait_ge(wt_ps, 1)
                nc.scalar.copy(WT[:, :], pW[:, :]).then_inc(wt_sb, 1)
                act.wait_ge(vec_ps, 1)
                nc.scalar.copy(VC[:, :, :], pV[:, :, :]).then_inc(vec_sb, 1)
                for n, (kind, b0) in enumerate(GROUPS):
                    if kind == 0 and b0 == 0:
                        layernorm_scalar_part(act, nc, XC[:, :, :], H[:, :, 0:D], st, need_root, root_done)
                    act.wait_ge(tr_ps, n + 1)
                    if n >= 2:
                        act.wait_ge(tr_used, n - 1)
                    nc.scalar.copy(TT[:, n % 2, :, :], pT[:, n % 2, :, :]).then_inc(tr_sb, 1)
                act.wait_ge(h_rdy, 2)
                pc.done(nc.scalar.activation(g["sig"][:, :], SC[:, 3:4], ACT.Exp, scale=-1.0))
                pc.done(nc.scalar.activation(g["exp_shift"][:, :], g["zero"][:, :], ACT.Exp,
                                             bias=g["neg_shift"][:, 0:1], scale=g["beta"][:, 0:1]))

            @block.vector
            def _(dve):
                ch = Chain(dve, ch_s)
                dve.memset(g["ones16"][:, :], 1.0)
                dve.memset(g["zero"][:, :], 0.0)
                ch.done(dve.memset(H[:, :, D:D + 1], 1.0))
                dve.wait_ge(ld_x, 16)
                layernorm_relu(net, dve, ch, X[:, :, :], XC[:, :, :], H[:, :, 0:D], st, need_root, root_done)
                dve.nop().then_inc(h_rdy, 1)
                dve.wait_ge(ld_w, 16 * 11)
                ch.done(dve.tensor_scalar(g["neg_shift"][:, :], SC[:, 4:5], 0.0, -1.0, ALU.max, ALU.mult))
                ch.done(dve.tensor_scalar(g["beta"][:, :], SC[:, 4:5], 1.0, None, ALU.mult))
                dve.nop().then_inc(h_rdy, 1)
                dve.wait_ge(pc_s, 2)
                ch.done(dve.tensor_scalar(g["sig"][:, :], g["sig"][:, :], 1.0, None, ALU.add))
                ch.done(dve.reciprocal(g["sig"][:, :], g["sig"][:, :]))
                dve.wait_ge(sc_ps, 1)
                for k, (own, oth) in enumerate(((SC[:, 0:1], None), (SC[:, 1:2], SC[:, 2:3]))):
                    sc = g["score"][k]
                    ch.done(dve.tensor_scalar(sc[:, 0, :], pS[:, k, :, 0], own, None, ALU.add))
                    if oth is None:
                        ch.done(dve.tensor_scalar(sc[:, 1, :], pS[:, k, :, 1], 1.0, None, ALU.mult))
                    else:
                        ch.done(dve.tensor_scalar(sc[:, 1, :], pS[:, k, :, 1], oth, None, ALU.add))
                    ch.done(dve.tensor_scalar(sc[:, 2, :], sc[:, 1, :], g["slope"][k], None, ALU.mult))
                    ch.done(dve.tensor_reduce(MX[:, k:k + 1], sc[:, 1, :], AXX, ALU.max, apply_absolute_value=True))
                dve.nop().then_inc(mx_rdy, 1)
                dve.wait_ge(mx_all, 1)
                ch.done(dve.tensor_scalar(g["lift"][:, :], MR[:, :], 1.0, None, ALU.add))
                for k in range(2):
                    ch.done(dve.tensor_scalar(g["score"][k][:, 3, :], g["score"][k][:, 1, :], g["lift"][:, k:k + 1],
                                              None, ALU.add))


def transpose_adj(net, g):
    nc, NB, NC, JS, PW = net.nc, net.NB, net.NC, net.JS, net.PW
    RING, TILES = 8, SUBS * IB
    MOPS = NB
    TC = JS * P
    stage, store16, ident = g["stage"], g["store"].bitcast(U16), g["ident"]
    with ExitStack() as c:
        A = net.sb(c, "adj_rows", [P, RING, TC], F32)
        ident16 = net.sb(c, "ident16", [P, P], BF16)
        halves = A.rearrange("p r j -> p (r j)").bitcast(BF16).rearrange("p (r j w) -> p r j w", r=RING, w=2)
        MA = net.sb(c, "max_acc", [P, 2, CI], F32)
        MB = net.sb(c, "max_done", [P, 2, CI], F32)
        pT = net.ps(c, "p_adjT", [P, 2, JS, P], BF16)
        pM = net.ps(c, "p_max", [P, IB, 2, P])
        pD = net.ps(c, "p_deg", [P, IB])
        ld = [net.sem(f"b_ld{k}") for k in range(RING)]
        transposed, staged = net.sem("b_transposed"), net.sem("b_staged")
        stored, kept = net.sem("b_stored"), net.sem("b_kept")
        degs, deg_read = net.sem("b_degrees"), net.sem("b_degree_read")
        maxed, max_ps = net.sem("b_maxed"), net.sem("b_max_ps")
        max_out, id_rdy = net.sem("b_max_out"), net.sem("b_ident16")
        rows = net.dram["adj"].rearrange("(c i p) j -> p c i j", p=P, i=IB)

        def degree(pe, cc, q):
            pe.wait_ge(staged, cc * TILES + (q + 1) * IB + 2)
            if q == 0:
                pe.wait_ge(deg_read, cc + 1)
            net.met(pe)
            for k in range(JS):
                for i in range(IB):
                    last = pe.matmul(pD[:, i:i + 1], stage[:, q, k, i * P:(i + 1) * P], g["ones16"][:, 0:1],
                                     start=(q == 0 and k == 0 and i == 0), stop=(q == SUBS - 1 and k == JS - 1),
                                     skip_group_check=True)
            last.then_inc(degs, 1)

        with nc.Block() as block:
            @block.sync
            def _(sp):
                def load(cc, t):
                    sp.dma_start(A[:, t % RING, :], rows[:, cc, t % IB, (t // IB) * TC:(t // IB + 1) * TC]
                                 if isinstance(cc, int) else
                                 rows[:, ds(cc, 1), t % IB, (t // IB) * TC:(t // IB + 1) * TC].rearrange("p c j -> p (c j)")
                                 ).then_inc(ld[t % RING], 16)
                for t in range(RING):
                    load(0, t)
                with sp.Fori(0, NC - 1) as cc:
                    for t in range(RING, TILES + RING):
                        sp.wait_ge(transposed, cc * TILES + (t - RING + 1))
                        load(cc if t < TILES else cc + 1, t % TILES)
                for t in range(RING, TILES):
                    sp.wait_ge(transposed, (NC - 1) * TILES + t - RING + 1)
                    load(NC - 1, t)

            @block.tensor
            def _(pe):
                pe.wait_ge(id_rdy, 1)
                pe.sem_inc(degs, SUBS)

                def tile(cc, t, last_chunk):
                    pe.wait_ge(ld[t % RING], cc * (16 * TILES // RING) + 16 * (t // RING + 1))
                    pe.wait_ge(staged, cc * TILES + t + 1)
                    for k in range(JS):
                        last = pe.transpose(pT[:, t % 2, k, :], halves[:, t % RING, k * P:(k + 1) * P, 1], ident16[:, :])
                    last.then_inc(transposed, 1)
                    if t in (9, 11, 13):
                        degree(pe, cc, (t - 9) // 2)

                def behind(cc, t):
                    if t == 1:
                        degree(pe, cc, SUBS - 1)
                    if t == 5:
                        pe.wait_ge(max_out, cc + 2)
                        for k in range(2):
                            for i in range(IB):
                                last = pe.transpose(pM[:, i, k, :], MB[:, k, i * P:(i + 1) * P], ident[:, :])
                        last.then_inc(max_ps, 1)

                rotated(pe, NC - 1, (6, TILES), tile, behind)

            @block.scalar
            def _(act):
                act.sem_inc(staged, 2)
                act.sem_inc(kept, SUBS)
                with act.Fori(0, NC) as cc:
                    for t in range(TILES):
                        q, i = t // IB, t % IB
                        if i == 0:
                            act.wait_ge(kept, cc * SUBS + q + 1)
                            act.wait_ge(degs, cc * SUBS + q + 1)
                            act.wait_ge(maxed, cc * MOPS + (q + 1) * MOPS // SUBS)
                        act.wait_ge(transposed, cc * TILES + t + 1)
                        net.met(act)
                        nc.scalar.activation(stage[:, q, :, i * P:(i + 1) * P], pT[:, t % 2, :, :], ACT.Copy,
                                             scale=ONE, saturate=False).then_inc(staged, 1)

            @block.gpsimd
            def _(pool):
                with pool.Fori(0, NC - 1) as cc:
                    for q in range(SUBS):
                        pool.wait_ge(staged, cc * TILES + (q + 1) * IB + 2)
                        net.met(pool)
                        nc.gpsimd.tensor_copy(store16[:, ds(cc * (SUBS * 2 * PW) + q * 2 * PW, 2 * PW)],
                                              stage[:, q, :, :].rearrange("p k i -> p (k i)").bitcast(U16)
                                              ).then_inc(kept, 1)
                for q in range(SUBS):
                    pool.wait_ge(staged, (NC - 1) * TILES + (q + 1) * IB + 2)
                    pool.dma_start(g["last_chunk"][:, q, :],
                                   stage[:, q, :, :].rearrange("p k i -> p (k i)").bitcast(U32)).then_inc(stored, 16)
                pool.wait_ge(stored, SUBS * 16)

            @block.vector
            def _(dve):
                dve.tensor_copy(ident16[:, :], ident[:, :]).then_inc(id_rdy, 1)
                dve.sem_inc(maxed, MOPS)
                dve.sem_inc(max_ps, 1)
                dve.sem_inc(max_out, 1)
                dve.sem_inc(deg_read, 1)

                def piece(cc, q, last):
                    dve.wait_ge(staged, cc * TILES + (q + 1) * IB + 2)
                    if q == 0:
                        dve.wait_ge(max_out, cc + 1)
                    for k in range(JS):
                        running_max(net, dve, cc, q * JS + k, g["score"][0], MA, stage[:, q, k, :], maxed, MOPS)
                    if q == SUBS - 1:
                        dve.wait_ge(maxed, cc * MOPS + 2 * MOPS)
                        dve.wait_ge(max_ps, cc + 1)
                        dve.tensor_copy(MB[:, :, :], MA[:, :, :]).then_inc(max_out, 1)

                def tops(cc, u):
                    dve.wait_ge(max_ps, cc + 2)
                    dve.tensor_reduce(g["top"][0][:, ds(cc * IB, IB)], pM[:, :, :, :].rearrange("p i k j -> p i (k j)"),
                                      AXX, ALU.max)
                    dve.wait_ge(degs, cc * SUBS + 2 * SUBS)
                    dve.tensor_scalar(g["deg"][:, ds(cc * IB, IB)], pD[:, :], 1.0 / ONE, None,
                                      ALU.mult).then_inc(deg_read, 1)

                rotated(dve, NC - 1, (1, SUBS), piece, tops)


def running_max(net, dve, cc, jt, score, MA, piece, maxed, credit):
    s = score[:, 3, jt:jt + 1]
    dve.wait_ge(maxed, cc * net.NB + credit + max(jt - 1, 0))
    net.met(dve)
    if jt < 2:
        dve.tensor_scalar(MA[:, jt % 2, :], piece, s, None, ALU.mult).then_inc(maxed, 1)
    else:
        dve.scalar_tensor_tensor(MA[:, jt % 2, :], piece, s, MA[:, jt % 2, :], ALU.mult, ALU.max).then_inc(maxed, 1)


def load_pieces(sp, g, net, arrived, used, per_piece):
    SUBS_W = SUBS * net.PW

    def load(src, q):
        sp.dma_start(g["stage"][:, q, :, :].rearrange("p k i -> p (k i)").bitcast(U32), src).then_inc(arrived[q], 16)

    for q in range(SUBS):
        load(g["store"][:, q * net.PW:(q + 1) * net.PW], q)
    with sp.Fori(0, net.NC - 2) as cc:
        for q in range(SUBS):
            sp.wait_ge(used, cc * (SUBS * per_piece) + (q + 1) * per_piece)
            load(g["store"][:, ds(cc * SUBS_W + (SUBS_W + q * net.PW), net.PW)], q)
    for q in range(SUBS):
        sp.wait_ge(used, (net.NC - 2) * (SUBS * per_piece) + (q + 1) * per_piece)
        load(g["last_chunk"][:, q, :], q)


def attend_masked(net, g, m, H, num):
    nc, NB, NC, JS, D = net.nc, net.NB, net.NC, net.JS, net.D
    stage, ident = g["stage"], g["ident"]
    sc, slope = g["score"][m], g["slope"][m]
    PAIRS = NB // 2
    RT = 4
    AHEAD = 2
    U_DIAG, U_ROWS, U_ROWS_SB = 5, 6, 9
    with ExitStack() as c:
        ones = net.sb(c, f"ones{m}", [P, P], F32)
        R = net.sb(c, f"rows{m}", [P, 2, net.N], F32)
        T = net.sb(c, f"logits{m}", [P, RT, 2, CI], F32)
        PR = net.sb(c, f"probs{m}", [P, 2, 2, CI], F32)
        O = net.sb(c, f"num_out{m}", [P, IB, D + 1], F32)
        RC = net.sb(c, f"row_cols{m}", [P, 3, NB], F32)
        acc = net.ps(c, f"p_acc{m}", [P, 2, 512])
        pR = net.ps(c, f"p_rows{m}", [P, 2, CI])
        pH = net.ps(c, f"p_hsum{m}", [P, D + 1])
        names = ("steps", "diag", "rows_ps", "rows_sb", "hsum", "branch", "logit", "exped", "masked", "summed",
                 "acc_read", "out_dma", "ones_set", "out_free")
        (steps, diag, rows_ps, rows_sb, hs, branch, logit, exped, masked, summed,
         acc_read, out_dma, ones_set, out_free) = (net.sem(f"c{m}_{n}") for n in names)
        arrived = [net.sem(f"c{m}_piece{k}") for k in range(SUBS)]
        num_rows = num.rearrange("(c i p) w -> p c i w", p=P, i=IB)

        def block_of(i):
            return acc[:, i // 2, (i % 2) * (D + 1):(i % 2 + 1) * (D + 1)]

        with nc.Block() as block:
            @block.sync
            def _(sp):
                load_pieces(sp, g, net, arrived, masked, JS // 2)

            @block.gpsimd
            def _(pool):
                with pool.Fori(0, NC) as cc:
                    pool.wait_ge(acc_read, cc + 2)
                    pool.dma_start(num_rows[:, ds(cc, 1), :, :].rearrange("p c i w -> p (c i) w"),
                                   O[:, :, :]).then_inc(out_dma, 16)
                    pool.wait_ge(out_dma, cc * 16 + 16)
                    pool.sem_inc(out_free, 1)
                pool.wait_ge(out_dma, NC * 16)

            @block.tensor
            def _(pe):
                pe.wait_ge(ones_set, 1)
                for b in range(NB):
                    last = pe.matmul(pH[:, :], ones[:, :], H[:, b, :], start=b == 0, stop=b == NB - 1)
                last.then_inc(hs, 1)

                def rows(cc):
                    wait(pe, diag, cc + 1)
                    for k in range(2):
                        last = pe.matmul(pR[:, k, :], ones[:, :], R[:, k, ds(cc * CI, CI)], start=True, stop=True)
                    last.then_inc(rows_ps, 1)

                def pair(cc, u, last_chunk):
                    if u == 0:
                        pe.wait_ge(acc_read, cc + 1)
                    pe.wait_ge(exped, cc * PAIRS + u + 1)
                    for k in range(2):
                        jt = 2 * u + k
                        for i in range(IB):
                            last = pe.matmul(block_of(i), PR[:, u % 2, k, i * P:(i + 1) * P], H[:, jt, :],
                                             start=(jt == 0 and i % 2 == 0), stop=(jt == NB - 1),
                                             skip_group_check=True)
                    last.then_inc(summed, 1)
                    if u == U_ROWS and not last_chunk:
                        rows(cc + 1)

                rows(0)
                rotated(pe, NC - 1, (AHEAD, PAIRS), pair, lambda cc, u: None)

            @block.scalar
            def _(act):
                act.sem_inc(acc_read, 1)
                act.sem_inc(out_free, 1)

                def rows(cc):
                    act.wait_ge(rows_ps, cc + 1)
                    net.met(act)
                    nc.scalar.copy(R[:, :, ds(cc * CI, CI)], pR[:, :, :]).then_inc(rows_sb, 1)

                def slope_branch(cc, u):
                    if u == 0:
                        act.wait_ge(rows_sb, cc + 1)
                    wait(act, exped, cc * PAIRS + u - RT + 1)
                    net.met(act)
                    for k in range(2):
                        last = nc.scalar.activation(T[:, u % RT, k, :], R[:, 1, ds(cc * CI, CI)], ACT.Identity,
                                                    bias=sc[:, 2, 2 * u + k:2 * u + k + 1])
                    last.then_inc(branch, 1)

                def pair(cc, u, last_chunk):
                    if u + 2 < PAIRS:
                        slope_branch(cc, u + 2)
                    elif not last_chunk:
                        slope_branch(cc + 1, u + 2 - PAIRS)
                    act.wait_ge(masked, cc * PAIRS + u + 1)
                    wait(act, summed, cc * PAIRS + u - 1)
                    nc.scalar.activation(PR[:, u % 2, :, :], T[:, u % RT, :, :], ACT.Exp).then_inc(exped, 1)
                    if u == U_ROWS_SB and not last_chunk:
                        rows(cc + 1)

                def take(cc, u):
                    act.wait_ge(summed, cc * PAIRS + PAIRS)
                    act.wait_ge(out_free, cc + 1)
                    nc.scalar.copy(O[:, :, :].rearrange("p (a b) w -> p a (b w)", a=2),
                                   acc[:, :, 0:2 * (D + 1)]).then_inc(acc_read, 1)

                rows(0)
                slope_branch(0, 0)
                slope_branch(0, 1)
                rotated(act, NC - 1, (1, PAIRS), pair, take)

            @block.vector
            def _(dve):
                ch = Chain(dve, steps)
                dve.memset(ones[:, :], 1.0).then_inc(ones_set, 1)
                top = RC[:, 2, :]
                ch.done(dve.tensor_scalar(top, g["top"][m][:, :], 1.0 / ONE, g["lift"][:, m:m + 1], ALU.mult, ALU.subtract))
                ch.done(dve.tensor_tensor(top, top, sc[:, 0, :], ALU.add))
                ch.done(dve.scalar_tensor_tensor(top, top, slope, top, ALU.mult, ALU.max))
                ch.done(dve.tensor_tensor(RC[:, 0, :], sc[:, 0, :], top, ALU.subtract))
                ch.done(dve.scalar_tensor_tensor(RC[:, 1, :], sc[:, 0, :], slope, top, ALU.mult, ALU.subtract))

                def rows(cc):
                    for k in range(2):
                        last = dve.tensor_tensor(R[:, k, ds(cc * CI, CI)].rearrange("p (i f) -> p i f", i=IB),
                                                 ident[:, :].unsqueeze(1).to_broadcast([P, IB, P]),
                                                 RC[:, k, ds(cc * IB, IB)].unsqueeze(2).to_broadcast([P, IB, P]),
                                                 ALU.mult)
                    last.then_inc(diag, 1)

                def logits(cc, u):
                    if u == 0:
                        dve.wait_ge(rows_sb, cc + 1)
                    dve.wait_ge(branch, cc * PAIRS + u + 1)
                    for k in range(2):
                        last = dve.scalar_tensor_tensor(T[:, u % RT, k, :], R[:, 0, ds(cc * CI, CI)],
                                                        sc[:, 1, 2 * u + k:2 * u + k + 1], T[:, u % RT, k, :],
                                                        ALU.add, ALU.max)
                    last.then_inc(logit, 1)

                def pair(cc, u, last_chunk):
                    if u + 1 < PAIRS:
                        logits(cc, u + 1)
                    elif not last_chunk:
                        logits(cc + 1, 0)
                    q, k0 = 2 * u // JS, 2 * u % JS
                    if k0 == 0:
                        dve.wait_ge(arrived[q], cc * 16 + 16)
                    dve.wait_ge(logit, cc * PAIRS + u + 1)
                    dve.scalar_tensor_tensor(T[:, u % RT, :, :], stage[:, q, k0:k0 + 2, :].bitcast(U8), float(ONE_BYTE),
                                             T[:, u % RT, :, :], ALU.subtract, ALU.min).then_inc(masked, 1)
                    if u == U_DIAG and not last_chunk:
                        rows(cc + 1)

                rows(0)
                dve.wait_ge(hs, 1)
                dve.tensor_copy(g["hsum"][:, 0:D + 1], pH[:, :])
                logits(0, 0)
                rotated(dve, NC - 1, (AHEAD, PAIRS), pair, lambda cc, u: None)


def attend_cosine(net, g, XT, HL, DH, num, maxima_out):
    nc, NB, NC, JS, D = net.nc, net.NB, net.NC, net.JS, net.D
    stage = g["stage"]
    PAIRS = NB // 2
    WH = 2 * D + 1
    WO = WH + D
    AHEAD, TAKE = 2, 1
    with ExitStack() as c:
        E = net.sb(c, "cos_exp", [P, 2, 2, CI], F32)
        PH = net.sb(c, "cos_hi", [P, 2, 2, CI], F16)
        PL = net.sb(c, "cos_lo", [P, 2, 2, CI], F16)
        O = net.sb(c, "cos_out", [P, IB, WO], F32)
        MA = net.sb(c, "cos_max_acc", [P, 2, CI], F32)
        MB = net.sb(c, "cos_max_done", [P, CI], F32)
        acc = net.ps(c, "p_cos_acc", [P, IB, 512])
        pS = net.ps(c, "p_cos", [P, 2, 2, CI])
        names = ("hsum", "hsum_read", "cos", "exped", "prob", "hi", "lo", "summed", "acc_read", "out_dma",
                 "maxed", "max_out", "max_dma", "max_free", "out_free")
        (hs, hs_read, cos, exped, prob, hi, lo, summed, acc_read, out_dma, maxed, max_out, max_dma,
         max_free, out_free) = (net.sem(f"d_{n}") for n in names)
        arrived = [net.sem(f"d_piece{k}") for k in range(SUBS)]
        num_rows = num.rearrange("(c i p) w -> p c i w", p=P, i=IB)

        with nc.Block() as block:
            @block.sync
            def _(sp):
                load_pieces(sp, g, net, arrived, summed, JS // 2)

            @block.gpsimd
            def _(pool):
                pool.sem_inc(max_free, 1)
                with pool.Fori(0, NC) as cc:
                    pool.wait_ge(max_out, cc + 2)
                    net.met(pool)
                    pool.dma_start(maxima_out[:, ds(cc * CI, CI)], MB[:, :]).then_inc(max_dma, 16)
                    pool.wait_ge(max_dma, cc * 16 + 16)
                    pool.sem_inc(max_free, 1)
                    pool.wait_ge(acc_read, cc * 2 + 4)
                    pool.dma_start(num_rows[:, ds(cc, 1), :, :].rearrange("p c i w -> p (c i) w"),
                                   O[:, :, :]).then_inc(out_dma, 16)
                    pool.wait_ge(out_dma, cc * 16 + 16)
                    pool.sem_inc(out_free, 1)
                pool.wait_ge(out_dma, NC * 16)
                pool.wait_ge(max_dma, NC * 16)

            @block.tensor
            def _(pe):
                for b in range(NB):
                    last = pe.matmul(acc[:, 0, 0:WH], g["ones16"][:, :], HL[:, b, :], start=b == 0, stop=b == NB - 1)
                last.then_inc(hs, 1)
                pe.wait_ge(hs_read, 1)

                def cosines(cc, u):
                    pe.wait_ge(exped, cc * PAIRS + u + 1)
                    for k in range(2):
                        jt = 2 * u + k
                        for n, (a, b) in enumerate(((0, 0), (0, 1), (1, 0))):
                            last = pe.matmul(pS[:, u % 2, k, :], XT[:, a, jt * P:(jt + 1) * P],
                                             XT[:, b, ds(cc * CI, CI)], start=n == 0, stop=n == 2)
                    last.then_inc(cos, 1)

                def pair(cc, u, last_chunk):
                    if u + 2 < PAIRS:
                        cosines(cc, u + 2)
                    elif not last_chunk:
                        cosines(cc + 1, u + 2 - PAIRS)
                    if u == 0:
                        pe.wait_ge(acc_read, cc * 2 + 2)
                    q, k0 = 2 * u // JS, 2 * u % JS
                    if k0 == 0:
                        pe.wait_ge(arrived[q], cc * 16 + 16)
                    pe.wait_ge(lo, cc * PAIRS + u + 1)
                    for k in range(2):
                        jt = 2 * u + k
                        for i in range(IB):
                            blk = slice(i * P, (i + 1) * P)
                            adj = stage[:, q, k0 + k, blk]
                            first, end = jt == 0, jt == NB - 1
                            pe.matmul(acc[:, i, 0:WH], PH[:, u % 2, k, blk], HL[:, jt, :],
                                      start=first, stop=end, skip_group_check=True)
                            pe.matmul(acc[:, i, D:WH], PL[:, u % 2, k, blk], HL[:, jt, D:WH],
                                      start=False, stop=end, skip_group_check=True)
                            for part in range(2):
                                last = pe.matmul(acc[:, i, WH:WO], adj, DH[:, part, jt, :],
                                                 start=False, stop=end, skip_group_check=True)
                    last.then_inc(summed, 1)

                cosines(0, 0)
                cosines(0, 1)
                rotated(pe, NC - 1, (AHEAD, PAIRS), pair, lambda cc, u: None)

            @block.scalar
            def _(act):
                act.sem_inc(acc_read, 2)
                act.sem_inc(out_free, 1)
                act.sem_inc(exped, 2)

                def exps(cc, u):
                    act.wait_ge(cos, cc * PAIRS + u + 1)
                    wait(act, lo, cc * PAIRS + u - 1)
                    nc.scalar.activation(E[:, u % 2, :, :], pS[:, u % 2, :, :], ACT.Exp, bias=g["neg_shift"][:, 0:1],
                                         scale=g["beta"][:, 0:1]).then_inc(exped, 1)

                def pair(cc, u, last_chunk):
                    if u == 1:
                        exps(cc, 1)
                    act.wait_ge(prob, cc * PAIRS + u + 1)
                    wait(act, summed, cc * PAIRS + u - 1)
                    nc.scalar.copy(PH[:, u % 2, :, :], E[:, u % 2, :, :]).then_inc(hi, 1)
                    if 1 <= u < PAIRS - 1:
                        exps(cc, u + 1)
                    elif u > 0 and not last_chunk:
                        exps(cc + 1, 0)

                def take(cc, u):
                    act.wait_ge(summed, cc * PAIRS + PAIRS)
                    act.wait_ge(out_free, cc + 1)
                    nc.scalar.mul(O[:, 0:2, :], acc[:, 0:2, 0:WO], 1.0 / ONE).then_inc(acc_read, 1)

                exps(0, 0)
                rotated(act, NC - 1, (TAKE, PAIRS), pair, take)

            @block.vector
            def _(dve):
                dve.sem_inc(maxed, NB)
                dve.sem_inc(max_out, 1)
                dve.wait_ge(hs, 1)
                dve.tensor_copy(g["hsum"][:, 0:WH], acc[:, 0, 0:WH]).then_inc(hs_read, 1)

                def probs(cc, u):
                    q, k0 = 2 * u // JS, 2 * u % JS
                    if k0 == 0:
                        dve.wait_ge(arrived[q], cc * 16 + 16)
                    dve.wait_ge(exped, cc * PAIRS + u + 3)
                    net.met(dve)
                    dve.scalar_tensor_tensor(E[:, u % 2, :, :], E[:, u % 2, :, :], g["exp_shift"][:, 0:1],
                                             stage[:, q, k0:k0 + 2, :], ALU.subtract, ALU.mult).then_inc(prob, 1)

                def maxima(cc, u):
                    q, k0 = 2 * u // JS, 2 * u % JS
                    if u == 0:
                        dve.wait_ge(max_out, cc + 1)
                    for k in range(2):
                        running_max(net, dve, cc, 2 * u + k, g["score"][1], MA, stage[:, q, k0 + k, :], maxed, NB)
                    if u == PAIRS - 1:
                        dve.wait_ge(maxed, cc * NB + 2 * NB)
                        dve.wait_ge(max_free, cc + 1)
                        dve.tensor_tensor(MB[:, :], MA[:, 0, :], MA[:, 1, :], ALU.max).then_inc(max_out, 1)

                def pair(cc, u, last_chunk):
                    if u == 1:
                        probs(cc, 1)
                    maxima(cc, u)
                    dve.wait_ge(hi, cc * PAIRS + u + 1)
                    dve.tensor_tensor(PL[:, u % 2, :, :], E[:, u % 2, :, :], PH[:, u % 2, :, :],
                                      ALU.subtract).then_inc(lo, 1)
                    if 1 <= u < PAIRS - 1:
                        probs(cc, u + 1)
                    elif u > 0 and not last_chunk:
                        probs(cc + 1, 0)

                def take(cc, u):
                    dve.wait_ge(summed, cc * PAIRS + PAIRS)
                    dve.wait_ge(out_free, cc + 1)
                    dve.tensor_scalar(O[:, 2:4, :], acc[:, 2:4, 0:WO], 1.0 / ONE, None, ALU.mult).then_inc(acc_read, 1)

                probs(0, 0)
                rotated(dve, NC - 1, (TAKE, PAIRS), pair, take)


def update(net, g, kind, NUM, X, x_src, num, x_dst, XT=None, HL=None, DH=None, HT=None, NT=None,
           maxima=None):
    nc, NB, D = net.nc, net.NB, net.D
    full = [P, NB, D]
    XC = g["stage"].rearrange("p q k i -> p (q k i)").bitcast(F32).rearrange("p (b d) -> p b d", b=NB)
    h, ident = NUM[:, :, 0:D], g["ident"]
    with ExitStack() as c:
        st = net.sb(c, f"ln_cols{kind}", [P, 4, NB], F32)
        W = net.sb(c, f"w_up{kind}", [P, D], F32) if kind == 0 else None
        TT = net.sb(c, f"tt_up{kind}", [P, 2, 4, P], F32) if kind == 0 else None
        MX = net.sb(c, "maxima_in", [P, net.N], F32) if kind == 1 else None
        pT = net.ps(c, f"p_up_t{kind}", [P, 2, 4, P])
        pW = net.ps(c, f"p_up_w{kind}", [P, 2, 4, P])
        names = ("ld", "ld_x", "ld_lo", "ld_mx", "steps", "act_steps", "att", "tr_ps", "tr_sb", "tr_sb2", "w_ps", "w_read", "need_root",
                 "root_done", "xdone", "xout", "ask", "told", "turned")
        (ld, ld_x, ld_lo, ld_mx, steps, act_steps, att, tr_ps, tr_sb, tr_sb2, w_ps, w_read, need_root, root_done, xdone, xout,
         ask, told, turned) = (net.sem(f"u{kind}_{n}") for n in names)
        G = NB // 4

        with nc.Block() as block:
            @block.sync
            def _(sp):
                rows = rows_view(num)
                if kind == 1:
                    sp.dma_start(MX[:, :], maxima).then_inc(ld_mx, 16)
                    sp.dma_start(NUM[:, :, :], rows[:, :, D:2 * D + 1]).then_inc(ld, 16)
                    sp.dma_start(XC, rows[:, :, 0:D]).then_inc(ld_lo, 16)
                    sp.dma_start(DH[:, :, :], rows[:, :, 2 * D + 1:3 * D + 1]).then_inc(ld_lo, 16)
                else:
                    sp.dma_start(NUM[:, :, :], rows).then_inc(ld, 16)
                sp.dma_start(X[:, :, :], rows_view(x_src)).then_inc(ld_x, 16)
                if kind == 0:
                    sp.dma_start(W[:, :], net.dram["L0_gnn_W"]).then_inc(ld_x, 16)
                sp.wait_ge(xdone, 1)
                sp.dma_start(rows_view(x_dst), X[:, :, :]).then_inc(xout, 16)
                sp.wait_ge(xout, 16)

            @block.vector
            def _(dve):
                ch = Chain(dve, steps)
                e, rz = st[:, 0, :], st[:, 1, :]
                dve.wait_ge(ld, 16)
                if kind == 1:
                    for n in range(G):
                        dve.wait_ge(tr_ps, n + 1)
                        dve.tensor_reduce(g["top"][1][:, 4 * n:4 * n + 4], pT[:, n % 2, :, :], AXX,
                                          ALU.max).then_inc(turned, 1)
                    dve.wait_ge(ld_lo, 32)
                    hs = g["hsum"]
                    ch.done(dve.tensor_tensor(hs[:, D:2 * D], hs[:, D:2 * D], hs[:, 0:D], ALU.add))
                    ch.done(dve.tensor_scalar(hs[:, D:2 * D + 1], hs[:, D:2 * D + 1], g["exp_shift"][:, 0:1], None, ALU.mult))
                    ch.done(dve.tensor_tensor(h, h, XC, ALU.add))
                    ch.done(dve.tensor_tensor(NUM[:, :, :], NUM[:, :, :],
                                              hs[:, D:2 * D + 1].unsqueeze(1).to_broadcast([P, NB, D + 1]), ALU.add))
                else:
                    ch.done(dve.tensor_scalar(e, g["deg"][:, :], 0.5, None, ALU.is_lt))
                    for b in range(NB):
                        last = dve.scalar_tensor_tensor(NUM[:, b, :], g["hsum"][:, 0:D + 1], e[:, b:b + 1], NUM[:, b, :],
                                                        ALU.mult, ALU.add)
                    ch.done(last)
                ch.done(dve.reciprocal(rz, NUM[:, :, D]))
                wide = rz.unsqueeze(2).to_broadcast(full)
                dve.wait_ge(ld_x, 32 if kind == 0 else 16)
                if kind == 0:
                    ch.done(dve.tensor_tensor(XC, h, wide, ALU.mult))
                    dve.nop().then_inc(att, 1)
                    for n in range(G):
                        dve.wait_ge(w_ps, n + 1)
                        last = dve.tensor_tensor(X[:, 4 * n:4 * n + 4, :], X[:, 4 * n:4 * n + 4, :], pW[:, n % 2, :, :],
                                                 ALU.add)
                        last.then_inc(w_read, 1)
                    dve.wait_ge(w_read, G)
                elif kind == 1:
                    ch.done(dve.tensor_tensor(DH[:, :, :], DH[:, :, :], g["dis"][:, :].unsqueeze(2).to_broadcast(full), ALU.mult))
                    ch.done(dve.tensor_tensor(X[:, :, :], X[:, :, :], DH[:, :, :], ALU.add))
                    ch.done(dve.tensor_tensor(XC, h, wide, ALU.mult))
                    ch.done(dve.scalar_tensor_tensor(X[:, :, :], XC, g["sig"][:, 0:1], X[:, :, :], ALU.mult, ALU.add))
                else:
                    ch.done(dve.tensor_tensor(XC, h, wide, ALU.mult))
                    ch.done(dve.tensor_tensor(X[:, :, :], X[:, :, :], XC, ALU.add))
                if kind != 0:
                    dve.nop().then_inc(xdone, 1)
                layernorm_relu(net, dve, ch, X[:, :, :], XC, h, st, need_root, root_done)
                if kind == 0:
                    nsq, tmp, r = st[:, 0, :], st[:, 1, :], st[:, 2, :]
                    dve.nop().then_inc(ask, 1)
                    dve.wait_ge(told, 1)
                    ch.done(dve.tensor_reduce(nsq, XC, AXX, ALU.add))
                    ch.done(dve.tensor_scalar(nsq, nsq, COS_EPS * COS_EPS, None, ALU.max))
                    ch.done(dve.reciprocal(tmp, nsq))
                    ch.done(dve.tensor_scalar(st[:, 3, :], g["deg"][:, :], 1.0, None, ALU.max))
                    ch.done(dve.reciprocal(g["dis"][:, :], st[:, 3, :]))
                    dve.nop().then_inc(ask, 1)
                    dve.wait_ge(told, 3)
                    newton_rsqrt(dve, ch, r, nsq, tmp)
                    newton_rsqrt(dve, ch, g["dis"][:, :], st[:, 3, :], tmp)
                    ch.done(dve.tensor_tensor(XC, h, r.unsqueeze(2).to_broadcast(full), ALU.mult))
                    dve.nop().then_inc(att, 1)
                    ch.done(dve.tensor_scalar(tmp[:, 0:1], g["sig"][:, :], -1.0, -1.0, ALU.mult, ALU.add))
                    ch.done(dve.scalar_tensor_tensor(X[:, :, :], h, tmp[:, 0:1], X[:, :, :], ALU.mult, ALU.add))
                    dve.nop().then_inc(xdone, 1)
                    dve.wait_ge(told, 4)
                    dve.tensor_tensor(HL[:, :, 0:D], h, HL[:, :, D:2 * D], ALU.subtract)
                    dve.memset(HL[:, :, 2 * D:2 * D + 1], 1.0)
                    for n in range(G):
                        dve.wait_ge(tr_sb, G + n + 1)
                        dve.tensor_tensor(XT[:, 1, 4 * n * P:4 * (n + 1) * P], pT[:, n % 2, :, :].rearrange("p k i -> p (k i)"),
                                          XT[:, 0, 4 * n * P:4 * (n + 1) * P], ALU.subtract).then_inc(turned, 1)
                    dve.wait_ge(turned, G)
                    ch.done(dve.tensor_tensor(XC, h, g["dis"][:, :].unsqueeze(2).to_broadcast(full), ALU.mult))
                    dve.nop().then_inc(ask, 1)
                    dve.wait_ge(told, 5)
                    dve.tensor_tensor(DH[:, 1, :, :], XC, DH[:, 0, :, :], ALU.subtract)
                elif kind == 1:
                    dve.memset(NUM[:, :, D:D + 1], 1.0)
                else:
                    dve.nop().then_inc(att, 1)
                    dve.nop().then_inc(ask, 1)
                    dve.wait_ge(told, 1)
                    dve.tensor_tensor(NT[:, 1, :, :], h, NT[:, 0, :, :], ALU.subtract)

            @block.tensor
            def _(pe):
                def turn(n, first, src, freed, need):
                    if n >= 2:
                        pe.wait_ge(freed, need + n - 1)
                    for k in range(4):
                        last = pe.transpose(pT[:, n % 2, k, :], src(4 * n + k), ident[:, :])
                    last.then_inc(tr_ps, 1)
                if kind == 0:
                    pe.wait_ge(att, 1)
                    for n in range(G + 1):
                        if n < G:
                            turn(n, 0, lambda b: XC[:, b, :], tr_sb, 0)
                        if n >= 1:
                            pe.wait_ge(tr_sb, n)
                            if n >= 3:
                                pe.wait_ge(w_read, n - 2)
                            for k in range(4):
                                last = pe.matmul(pW[:, (n - 1) % 2, k, :], TT[:, (n - 1) % 2, k, :], W[:, :],
                                                 start=True, stop=True, skip_group_check=True)
                            last.then_inc(w_ps, 1)
                    pe.wait_ge(att, 2)
                    for n in range(G):
                        turn(n, 1, lambda b: XC[:, b, :], turned, 0)
                elif kind == 1:
                    pe.wait_ge(ld_mx, 16)
                    for n in range(G):
                        turn(n, 0, lambda b: MX[:, b * P:(b + 1) * P], turned, 0)
                elif kind == 2:
                    pe.wait_ge(att, 1)
                    for n in range(G):
                        turn(n, 0, lambda b: h[:, b, :], tr_sb, 0)

            @block.scalar
            def _(act):
                if kind == 0:
                    for n in range(G):
                        act.wait_ge(tr_ps, n + 1)
                        if n >= 2:
                            act.wait_ge(w_ps, n - 1)
                        nc.scalar.copy(TT[:, n % 2, :, :], pT[:, n % 2, :, :]).then_inc(tr_sb, 1)
                layernorm_scalar_part(act, nc, XC, h, st, need_root, root_done)
                if kind == 0:
                    act.wait_ge(ask, 1)
                    nc.scalar.activation(XC, h, ACT.Square).then_inc(told, 1)
                    act.wait_ge(ask, 2)
                    nc.scalar.activation(st[:, 2, :], st[:, 1, :], ACT.Sqrt).then_inc(told, 1)
                    nc.scalar.activation(g["dis"][:, :], g["dis"][:, :], ACT.Sqrt).then_inc(told, 1)
                    nc.scalar.copy(HL[:, :, D:2 * D], h).then_inc(told, 1)
                    for n in range(G):
                        act.wait_ge(tr_ps, G + n + 1)
                        nc.scalar.copy(XT[:, 0, 4 * n * P:4 * (n + 1) * P],
                                       pT[:, n % 2, :, :].rearrange("p k i -> p (k i)")).then_inc(tr_sb, 1)
                    act.wait_ge(ask, 3)
                    act.wait_ge(xout, 16)
                    nc.scalar.copy(DH[:, 0, :, :], XC).then_inc(told, 1)
                elif kind == 2:
                    act.wait_ge(ask, 1)
                    nc.scalar.copy(NT[:, 0, :, :], h).then_inc(told, 1)
                    for n in range(G):
                        act.wait_ge(tr_ps, n + 1)
                        nc.scalar.copy(HT[:, 4 * n * P:4 * (n + 1) * P],
                                       pT[:, n % 2, :, :].rearrange("p k i -> p (k i)")).then_inc(tr_sb, 1)


def chebyshev(net, g, layer, W, B, HT, NT, N2, x_src, out):
    nc, NB, NC, JS, D = net.nc, net.NB, net.NC, net.JS, net.D
    stage, ident = g["stage"], g["ident"]
    with ExitStack() as c:
        T1 = net.sb(c, f"cheb_t{layer}", [P, 2, CI], F32)
        EX = net.sb(c, f"cheb_e{layer}", [P, 2, CI], F32)
        XR = net.sb(c, f"cheb_x{layer}", [P, IB, D], F32)
        pA = net.ps(c, f"p_prod{layer}", [P, 2, CI])
        pN = net.ps(c, f"p_nat{layer}", [P, IB, P])
        pO = net.ps(c, f"p_out{layer}", [P, CI])

        for product in range(2):
            names = ("used", "prod", "t1", "nat", "nat_hi", "nat_lo", "part", "part_read", "z", "ex", "xin", "y", "ynat", "xout", "steps")
            (used, prod, t1, nat, nat_hi, nat_lo, part, part_read, zs, ex, xin, ys, ynat, xout, steps) = (
                net.sem(f"e{layer}{product}_{n}") for n in names)
            arrived = [net.sem(f"e{layer}{product}_piece{k}") for k in range(SUBS)]
            SRC = NT if product == 0 else N2
            final = product == 1 and layer == 1
            xr_in = x_src.rearrange("(c i p) w -> p c i w", p=P, i=IB)
            xr_out = out.rearrange("(c i p) w -> p c i w", p=P, i=IB)

            with nc.Block() as block:
                @block.sync
                def _(sp):
                    load_pieces(sp, g, net, arrived, used, 1)

                @block.gpsimd
                def _(pool):
                    if final:
                        with pool.Fori(0, NC) as cc:
                            pool.dma_start(XR[:, :, :], xr_in[:, ds(cc, 1), :, :].rearrange("p c i w -> p (c i) w")
                                           ).then_inc(xin, 16)
                            pool.wait_ge(ynat, cc + 2)
                            net.met(pool)
                            pool.dma_start(xr_out[:, ds(cc, 1), :, :].rearrange("p c i w -> p (c i) w"),
                                           XR[:, :, :]).then_inc(xout, 16)
                            pool.wait_ge(xout, cc * 16 + 16)
                        pool.wait_ge(xout, NC * 16)

                @block.tensor
                def _(pe):
                    def piece(pp, u, last_pair):
                        half, q = u // SUBS, u % SUBS
                        cc = pp * 2 + half
                        if q == 0:
                            pe.wait_ge(t1, cc + 1)
                        pe.wait_ge(arrived[q], cc * 16 + 16)
                        net.met(pe)
                        for k in range(JS):
                            jt = q * JS + k
                            for part_ in range(2):
                                last = pe.matmul(pA[:, half, :], SRC[:, part_, jt, :], stage[:, q, k, :],
                                                 start=jt == 0 and part_ == 0, stop=jt == NB - 1 and part_ == 1)
                        last.then_inc(used, 1)
                        if u == SUBS:
                            weights(pp * 2, 0)
                        if u == SUBS + 2 and final:
                            rows_back(pp * 2)

                    def behind(pp, u):
                        if u == 0:
                            weights(pp * 2 + 1, 1)
                        if u == 2 and final:
                            rows_back(pp * 2 + 1)

                    def weights(cc, half):
                        pe.wait_ge(t1, cc + 3)
                        if product == 0:
                            pe.wait_ge(nat_lo, cc + 1)
                            for i in range(IB):
                                last = pe.transpose(pN[:, i, :], T1[:, half, i * P:(i + 1) * P], ident[:, :])
                            last.then_inc(nat, 1)
                            pe.wait_ge(part_read, cc + 1)
                            pe.matmul(pO[:, :], W[:, 0, :], HT[:, ds(cc * CI, CI)], start=True, stop=False)
                            pe.matmul(pO[:, :], W[:, 1, :], T1[:, half, :], start=False, stop=True).then_inc(part, 1)
                        else:
                            pe.wait_ge(part_read, cc + 1)
                            pe.matmul(pO[:, :], W[:, 2, :], T1[:, half, :], start=True, stop=True).then_inc(part, 1)

                    def rows_back(cc):
                        pe.wait_ge(ys, cc + 2)
                        for i in range(IB):
                            last = pe.transpose(pN[:, i, :], EX[:, 0, i * P:(i + 1) * P], ident[:, :])
                        last.then_inc(nat, 1)

                    rotated(pe, NC // 2 - 1, (3, 2 * SUBS), piece, behind)

                @block.scalar
                def _(act):
                    act.sem_inc(t1, 2)
                    act.sem_inc(part, 2)
                    with act.Fori(0, NC // 2) as pp:
                        for half in range(2):
                            cc = pp * 2 + half
                            act.wait_ge(part, cc + 1)
                            act.wait_ge(used, cc * SUBS + SUBS)
                            nc.scalar.mul(T1[:, half, :], pA[:, half, :], 1.0 / ONE).then_inc(t1, 1)
                            if product == 0:
                                act.wait_ge(nat, cc + 1)
                                net.met(act)
                                nc.scalar.copy(N2[:, 0, ds(cc * IB, IB), :], pN[:, :, :]).then_inc(nat_hi, 1)
                            else:
                                act.wait_ge(zs, cc + 1)
                                nc.scalar.activation(EX[:, 0, :], EX[:, 0, :], ACT.Exp).then_inc(ex, 1)

                @block.vector
                def _(dve):
                    for credit in (nat_lo, part_read, ys, ynat):
                        dve.sem_inc(credit, 1)
                    with dve.Fori(0, NC) as cc:
                        cols = ds(cc * CI, CI)
                        if product == 0:
                            dve.wait_ge(nat_hi, cc + 1)
                            dve.tensor_tensor(N2[:, 1, ds(cc * IB, IB), :], pN[:, :, :], N2[:, 0, ds(cc * IB, IB), :],
                                              ALU.subtract).then_inc(nat_lo, 1)
                            dve.wait_ge(part, cc + 3)
                            dve.tensor_copy(HT[:, cols], pO[:, :]).then_inc(part_read, 1)
                        else:
                            dve.wait_ge(ys, cc + 1)
                            dve.wait_ge(part, cc + 3)
                            dve.scalar_tensor_tensor(EX[:, 1, :], pO[:, :], B, HT[:, cols], ALU.add, ALU.add).then_inc(part_read, 1)
                            dve.wait_ge(part_read, cc + 2)
                            if final:
                                dve.wait_ge(ynat, cc + 1)
                            dve.tensor_scalar(EX[:, 0, :], EX[:, 1, :], 0.0, None, ALU.min).then_inc(zs, 1)
                            dve.wait_ge(ex, cc + 1)
                            dve.tensor_scalar(EX[:, 1, :], EX[:, 1, :], 0.0, None, ALU.max).then_inc(steps, 1)
                            dve.wait_ge(steps, cc + 1)
                            dst = EX[:, 0, :] if final else HT[:, cols]
                            dve.scalar_tensor_tensor(dst, EX[:, 0, :], -1.0, EX[:, 1, :], ALU.add, ALU.add).then_inc(ys, 1)
                            if final:
                                dve.wait_ge(xin, cc * 16 + 16)
                                dve.wait_ge(nat, cc + 1)
                                dve.tensor_tensor(XR[:, :, :], XR[:, :, :], pN[:, :, :], ALU.add).then_inc(ynat, 1)


def rescale(net, g, W, HT, NT):
    nc, NB, NC, D = net.nc, net.NB, net.NC, net.D
    with ExitStack() as c:
        T = net.sb(c, "scaled", [P, 2, CI], F32)
        S = net.sb(c, "scales", [P, 2], F32)
        pN = net.ps(c, "p_scaled", [P, 2, IB, P])
        steps, sc, nat, hi, lo = (net.sem(f"f_{n}") for n in ("steps", "scaled", "nat", "hi", "lo"))
        def low_part(dve, n):
            blocks = slice(n * IB, (n + 1) * IB)
            dve.wait_ge(hi, n + 1)
            dve.tensor_tensor(NT[:, 1, blocks, :], pN[:, n % 2, :, :], NT[:, 0, blocks, :], ALU.subtract).then_inc(lo, 1)

        with nc.Block() as block:
            @block.vector
            def _(dve):
                ch = Chain(dve, steps)
                ch.done(dve.tensor_reduce(S[:, 0:1], HT[:, :], AXX, ALU.max, apply_absolute_value=True))
                ch.done(dve.tensor_scalar(S[:, 0:1], S[:, 0:1], 1e-30, 0.125, ALU.max, ALU.mult))
                ch.done(dve.reciprocal(S[:, 1:2], S[:, 0:1]))
                ch.done(dve.tensor_scalar(W[:, :, :], W[:, :, :], S[:, 0:1], None, ALU.mult))
                for n in range(NC):
                    cols = slice(n * CI, (n + 1) * CI)
                    if n >= 2:
                        dve.wait_ge(nat, n - 1)
                    ch.done(dve.tensor_scalar(T[:, n % 2, :], HT[:, cols], S[:, 1:2], None, ALU.mult))
                    dve.tensor_copy(HT[:, cols], T[:, n % 2, :]).then_inc(sc, 1)
                    if n >= 1:
                        low_part(dve, n - 1)
                low_part(dve, NC - 1)

            @block.tensor
            def _(pe):
                for n in range(NC):
                    pe.wait_ge(sc, n + 1)
                    if n >= 2:
                        pe.wait_ge(lo, n - 1)
                    for i in range(IB):
                        last = pe.transpose(pN[:, n % 2, i, :], T[:, n % 2, i * P:(i + 1) * P], g["ident"][:, :])
                    last.then_inc(nat, 1)

            @block.scalar
            def _(act):
                for n in range(NC):
                    act.wait_ge(nat, n + 1)
                    nc.scalar.copy(NT[:, 0, n * IB:(n + 1) * IB, :], pN[:, n % 2, :, :]).then_inc(hi, 1)


def cheb_weights(net, WL, BL):
    nc = net.nc
    ld, steps = net.sem("w_ld"), net.sem("w_steps")
    with nc.Block() as block:
        @block.sync
        def _(sp):
            for n in range(2):
                sp.dma_start(WL[n][:, :, :], net.dram[f"L3_gnn_W{n}"].rearrange("k d f -> d k f")).then_inc(ld, 16)
                sp.dma_start(BL[n][:, :], net.dram[f"L3_gnn_b{n}"].unsqueeze(1)).then_inc(ld, 16)

        @block.vector
        def _(dve):
            ch = Chain(dve, steps)
            dve.wait_ge(ld, 64)
            for n in range(2):
                ch.done(dve.tensor_tensor(WL[n][:, 0, :], WL[n][:, 0, :], WL[n][:, 2, :], ALU.subtract))
                ch.done(dve.tensor_scalar(WL[n][:, 2, :], WL[n][:, 2, :], 2.0, None, ALU.mult))


def gnn_stack(nc, dram, out):
    with ExitStack() as ctx:
        net = Net(nc, ctx, dram)
        N, D, NB, NC = net.N, net.D, net.NB, net.NC
        g = {"slope": (0.2, 0.01)}
        for name, shape, dt in (("ident", [P, P], F32), ("ones16", [P, P], F16),
                                ("zero", [P, 1], F32), ("sig", [P, 1], F32), ("beta", [P, 1], F32),
                                ("neg_shift", [P, 1], F32), ("exp_shift", [P, 1], F32), ("lift", [P, 2], F32),
                                ("hsum", [P, 2 * D + 1], F32), ("deg", [P, NB], F32), ("dis", [P, NB], F32),
                                ("store", [P, (NC - 1) * SUBS * net.PW], U32), ("stage", [P, SUBS, net.JS, CI], FP8)):
            g[name] = net.sb(ctx, name, shape, dt)
        g["score"] = [net.sb(ctx, f"score{k}", [P, 4, NB], F32) for k in range(2)]
        g["top"] = [net.sb(ctx, f"top{k}", [P, NB], F32) for k in range(2)]
        g["last_chunk"] = nc.dram_tensor("adj_last_chunk", [P, SUBS, net.PW], U32, kind="Internal").ap()
        xres = nc.dram_tensor("x_residual", [N, D], F32, kind="Internal").ap()
        num = nc.dram_tensor("weighted_sums", [N, D + 1], F32, kind="Internal").ap()
        maxima = nc.dram_tensor("neighbour_maxima", [P, N], F32, kind="Internal").ap()
        num_cos = nc.dram_tensor("cosine_sums", [N, 3 * D + 1], F32, kind="Internal").ap()

        with ExitStack() as c:
            g["H"] = net.sb(c, "h_gat", [P, NB, D + 1], F32)
            setup(net, g)
            net.phase_end()
            transpose_adj(net, g)
            net.phase_end()
            attend_masked(net, g, 0, g["H"], num)
            net.phase_end()
        with ExitStack() as c:
            HL = net.sb(c, "h_lo_hi", [P, NB, 2 * D + 1], F16)
            XT = net.sb(c, "unit_rows_T", [P, 2, N], F16)
            DH = net.sb(c, "dis_h", [P, 2, NB, D], F16)
            with ExitStack() as c2:
                NUM = net.sb(c2, "num0", [P, NB, D + 1], F32)
                X = DH.rearrange("p a b d -> p (a b d)").bitcast(F32).rearrange("p (b d) -> p b d", b=NB)
                update(net, g, 0, NUM, X, dram["x"], num, xres, XT=XT, HL=HL, DH=DH)
                net.phase_end()
            attend_cosine(net, g, XT, HL, DH, num_cos, maxima)
            net.phase_end()
        with ExitStack() as c:
            H = net.sb(c, "num1", [P, NB, D + 1], F32)
            with ExitStack() as c2:
                X = net.sb(c2, "x1", [P, NB, D], F32)
                DS = net.sb(c2, "diffused", [P, NB, D], F32)
                update(net, g, 1, H, X, xres, num_cos, xres, DH=DS, maxima=maxima)
                net.phase_end()
            attend_masked(net, g, 1, H, num)
            net.phase_end()
        with ExitStack() as c:
            NT = net.sb(c, "h_parts", [P, 2, NB, D], F16)
            HT = net.sb(c, "h_T", [P, N], F32)
            WL = [net.sb(c, f"cheb_w{k}", [P, 3, D], F32) for k in range(2)]
            BL = [net.sb(c, f"cheb_b{k}", [P, 1], F32) for k in range(2)]
            cheb_weights(net, WL, BL)
            net.phase_end()
            with ExitStack() as c2:
                NUM = net.sb(c2, "num2", [P, NB, D + 1], F32)
                X = net.sb(c2, "x2", [P, NB, D], F32)
                update(net, g, 2, NUM, X, xres, num, xres, HT=HT, NT=NT)
                net.phase_end()
            N2 = net.sb(c, "Lh_parts", [P, 2, NB, D], F16)
            chebyshev(net, g, 0, WL[0], BL[0][:, 0:1], HT, NT, N2, xres, out)
            net.phase_end()
            rescale(net, g, WL[1], HT, NT)
            net.phase_end()
            chebyshev(net, g, 1, WL[1], BL[1][:, 0:1], HT, NT, N2, xres, out)
            net.phase_end()


_INS = ['x', 'adj', 'L0_gnn_W', 'L0_gnn_a1', 'L0_gnn_a2', 'L0_gnn_a_bias', 'L1_gnn_alpha', 'L1_gnn_beta',
        'L2_gnn_inlayer2', 'L2_gnn_W1', 'L2_gnn_w2', 'L2_gnn_b2', 'L2_gnn_w3', 'L2_gnn_b3',
        'L3_gnn_W0', 'L3_gnn_b0', 'L3_gnn_W1', 'L3_gnn_b1']


def kernel(**inputs):
    import numpy as _np
    import concourse.bacc as _bacc
    from concourse import mybir as _mybir
    from concourse.bass_utils import run_bass_kernel_spmd as _run

    nc = _bacc.Bacc("TRN2", target_bir_lowering=False, num_devices=1)
    arrays, dram = {}, {}
    for name in _INS:
        a = _np.ascontiguousarray(inputs[name])
        if a.ndim == 0:
            a = a.reshape(1)
        arrays[f"in_{name}_dram"] = a
        dram[name] = nc.dram_tensor(f"in_{name}_dram", a.shape, _mybir.dt.from_np(a.dtype), kind="ExternalInput").ap()
    out = nc.dram_tensor("out_0_dram", inputs["x"].shape, _mybir.dt.float32, kind="ExternalOutput").ap()
    gnn_stack(nc, dram, out)
    r = _run(nc, [arrays], core_ids=[0])
    return r.results[0]["out_0_dram"]
```

```python
from contextlib import ExitStack

import concourse.bass as bass
from concourse import mybir

ALU = mybir.AluOpType
ACT = mybir.ActivationFunctionType
AXX = mybir.AxisListType.X
F32 = mybir.dt.float32
F16 = mybir.dt.float16
BF16 = mybir.dt.bfloat16
FP8 = mybir.dt.float8e5
U8 = mybir.dt.uint8
U16 = mybir.dt.uint16
U32 = mybir.dt.uint32
RMAX = bass.bass_isa.ReduceOp.max
ds = bass.ds

P = 128
CI = 512
IB = CI // P
SUBS = 4
ONE = 32768.0
ONE_BYTE = 120
EPS = 1e-5
COS_EPS = 1e-8


class Chain:

    def __init__(self, eng, sem):
        self.eng, self.sem, self.n = eng, sem, 0

    def done(self, ins):
        self.n += 1
        ins.then_inc(self.sem, 1)
        self.eng.wait_ge(self.sem, self.n)


class Net:

    def __init__(self, nc, ctx, dram):
        self.nc, self.ctx, self.dram = nc, ctx, dram
        self.phase_sems = []
        self.passed, self.phase = {}, 0
        self.N, self.D = dram["x"].shape
        self.NB = self.N // P
        self.NC = self.N // CI
        self.JS = self.NB // SUBS
        self.PW = self.JS * CI // 4
        assert self.D == P and self.JS * SUBS == self.NB

    def sb(self, ctx, name, shape, dt):
        return ctx.enter_context(self.nc.sbuf_tensor(name, shape, dt))

    def ps(self, ctx, name, shape, dt=F32):
        return ctx.enter_context(self.nc.psum_tensor(name, shape, dt))

    def sem(self, name):
        s = self.nc.alloc_semaphore(name=name)
        self.phase_sems.append(s)
        return s

    def met(self, eng):
        key = str(eng.engine)
        if key not in self.passed:
            self.passed[key] = self.sem(f"passed{self.phase}_{len(self.passed)}")
        eng.sem_inc(self.passed[key], 1)

    def phase_end(self):
        self.nc.clear_and_free_semaphores(self.phase_sems)
        self.phase_sems, self.passed, self.phase = [], {}, self.phase + 1
        self.nc.all_engine_barrier()


def wait(eng, sem, value):
    if not (isinstance(value, int) and value <= 0):
        eng.wait_ge(sem, value)


def rotated(eng, last, first, step, head):
    for u in range(first[0]):
        step(0, u, False)
    with eng.Fori(0, last) as cc:
        for u in range(first[0], first[1]):
            step(cc, u, False)
        for u in range(first[0]):
            step(cc + 1, u, False)
            head(cc, u)
    for u in range(first[0], first[1]):
        step(last, u, True)
    for u in range(first[0]):
        head(last, u)


def rows_view(ap):
    return ap.rearrange("(b p) w -> p b w", p=P)


def newton_rsqrt(dve, ch, r, v, tmp):
    ch.done(dve.tensor_tensor(tmp, r, r, ALU.mult))
    ch.done(dve.tensor_tensor(tmp, tmp, v, ALU.mult))
    ch.done(dve.tensor_scalar(tmp, tmp, -0.5, 1.5, ALU.mult, ALU.add))
    ch.done(dve.tensor_tensor(r, r, tmp, ALU.mult))


def layernorm_relu(net, dve, ch, xt, xc, h, st, need_root, root_done, centred, have_stats=False):
    nc, NB, D = net.nc, net.NB, net.D
    mean, var, r, tmp = st[:, 0, :], st[:, 1, :], st[:, 2, :], st[:, 3, :]
    if not have_stats:
        for b in range(NB):
            last = nc.vector.bn_stats(xc[:, b, 0:6], xt[:, b, :])
        ch.done(last)
    dve.tensor_tensor(mean, xc[:, :, 1], xc[:, :, 4], ALU.add)
    dve.tensor_tensor(tmp, xc[:, :, 1], xc[:, :, 4], ALU.subtract)
    ch.done(dve.tensor_tensor(var, xc[:, :, 2], xc[:, :, 5], ALU.add))
    dve.tensor_scalar(mean, mean, 0.5, None, ALU.mult)
    dve.tensor_scalar(var, var, 1.0 / D, EPS, ALU.mult, ALU.add)
    ch.done(dve.tensor_tensor(tmp, tmp, tmp, ALU.mult))
    ch.done(dve.scalar_tensor_tensor(var, tmp, 0.25, var, ALU.mult, ALU.add))
    dve.reciprocal(tmp, var).then_inc(need_root, 1)
    for b in range(NB):
        last = dve.tensor_scalar(h[:, b, :], xt[:, b, :], mean[:, b:b + 1], 0.0, ALU.subtract, ALU.max)
        if b % 4 == 3:
            last.then_inc(centred, 1)
        if b == 7:
            dve.wait_ge(root_done, 1)
            newton_rsqrt(dve, ch, r, var, tmp)
            dve.nop().then_inc(need_root, 1)


def layernorm_scalar_part(act, nc, h, st, need_root, root_done, centred, scaled, behind=None):
    act.wait_ge(need_root, 1)
    nc.scalar.activation(st[:, 2, :], st[:, 3, :], ACT.Sqrt).then_inc(root_done, 1)
    act.wait_ge(need_root, 2)
    for b in range(h.shape[1]):
        if b % 4 == 0:
            act.wait_ge(centred, b // 4 + 1)
        last = nc.scalar.activation(h[:, b, :], h[:, b, :], ACT.Copy, scale=st[:, 2, b:b + 1])
        if b % 4 == 3:
            last.then_inc(scaled, 1)
            if behind:
                behind(b // 4)


def setup(net, g):
    nc, dram, NB, D = net.nc, net.dram, net.NB, net.D
    E2 = dram["L2_gnn_inlayer2"].shape[1] // P
    with ExitStack() as c:
        X = net.sb(c, "x_in", [P, NB, D], F32)
        XC = net.sb(c, "x_centred", [P, NB, D], F32)
        W = net.sb(c, "w_gat", [P, D], F32)
        W1 = net.sb(c, "w1_gat2", [P, E2 * D], F32)
        A12 = net.sb(c, "a12", [P, 2], F32)
        W23 = net.sb(c, "w23", [P, 2], F32)
        SC, VC = g["scalars"], g["score_vectors"]
        WT = net.sb(c, "w_gat_T", [P, D], F32)
        TT = net.sb(c, "transposed", [P, 2, 4, P], F32)
        MX = net.sb(c, "absmax", [P, 1], F32)
        MR = net.sb(c, "absmax_all", [P, 1], F32)
        st = net.sb(c, "ln_cols_in", [P, 4, NB], F32)
        ident, H = g["ident"], g["H"]
        pW = net.ps(c, "p_wt", [P, D])
        pV = net.ps(c, "p_vec", [P, 1 + E2, 2])
        pT = net.ps(c, "p_tr", [P, 2, 4, P])
        pS = net.ps(c, "p_scores", [P, NB, 2])
        ld_x, ld_w = net.sem("a_ld_x"), net.sem("a_ld_w")
        id0, id1 = net.sem("a_id0"), net.sem("a_ident")
        ch_s, pc_s = net.sem("a_dve_steps"), net.sem("a_act_steps")
        need_root, root_done = net.sem("a_need_root"), net.sem("a_root_done")
        centred, scaled = net.sem("a_centred"), net.sem("a_scaled")
        wt_ps, wt_sb, vec_ps, vec_sb = (net.sem(n) for n in ("a_wt_ps", "a_wt_sb", "a_vec_ps", "a_vec_sb"))
        h_rdy, tr_ps, tr_sb, tr_used, sc_ps = (net.sem(n) for n in ("a_h", "a_tr_ps", "a_tr_sb", "a_tr_used", "a_sc_ps"))
        mx_rdy, mx_all = net.sem("a_mx"), net.sem("a_mx_all")
        G = NB // 4

        with nc.Block() as block:
            @block.sync
            def _(sp):
                sp.dma_start(X[:, :, :], rows_view(dram["x"])).then_inc(ld_x, 16)
                for dst, src in ((W[:, :], dram["L0_gnn_W"]), (W1[:, :], dram["L2_gnn_W1"]),
                                 (A12[:, 0:1], dram["L0_gnn_a1"].unsqueeze(1)), (A12[:, 1:2], dram["L0_gnn_a2"].unsqueeze(1)),
                                 (W23[:, 0:1], dram["L2_gnn_w2"].unsqueeze(1)), (W23[:, 1:2], dram["L2_gnn_w3"].unsqueeze(1))):
                    sp.dma_start(dst, src).then_inc(ld_w, 16)
                for k, n in enumerate(("L0_gnn_a_bias", "L2_gnn_b2", "L2_gnn_b3", "L1_gnn_alpha", "L1_gnn_beta")):
                    sp.dma_start(SC[:, k:k + 1], dram[n].partition_broadcast(P)).then_inc(ld_w, 16)

            @block.gpsimd
            def _(pool):
                nc.gpsimd.memset(ident[:, :], 0.0).then_inc(id0, 1)
                pool.wait_ge(id0, 1)
                nc.gpsimd.affine_select(out=ident[:, :], in_=ident[:, :], compare_op=ALU.not_equal, fill=1.0,
                                        base=0, pattern=[[-1, P]], channel_multiplier=1).then_inc(id1, 1)
                pool.wait_ge(mx_rdy, 1)
                nc.gpsimd.partition_all_reduce(MR[:, :], MX[:, :], P, RMAX).then_inc(mx_all, 1)

            @block.tensor
            def _(pe):
                pe.wait_ge(id1, 1)
                pe.wait_ge(ld_w, 16 * 11)
                pe.transpose(pW[:, :], W[:, :], ident[:, :]).then_inc(wt_ps, 1)
                pe.wait_ge(wt_sb, 1)
                pe.matmul(pV[:, 0, :], WT[:, :], A12[:, :], start=True, stop=True)
                for e in range(E2):
                    last = pe.matmul(pV[:, 1 + e, :], W1[:, e * P:(e + 1) * P], W23[:, :], start=True, stop=True)
                last.then_inc(vec_ps, 1)

                def project(n):
                    pe.wait_ge(tr_sb, n + 1)
                    for k in range(4):
                        last = pe.matmul(pS[:, 4 * n + k, :], TT[:, n % 2, k, :], VC[:, 0, :],
                                         start=True, stop=True, skip_group_check=True)
                    last.then_inc(tr_used, 1)

                for n in range(G):
                    pe.wait_ge(scaled, n + 1)
                    if n >= 2:
                        pe.wait_ge(tr_sb, n - 1)
                    for k in range(4):
                        last = pe.transpose(pT[:, n % 2, k, :], H[:, 4 * n + k, 0:D], ident[:, :])
                    last.then_inc(tr_ps, 1)
                    if n == 0:
                        pe.wait_ge(vec_sb, 1)
                    else:
                        project(n - 1)
                project(G - 1)
                pe.wait_ge(tr_used, G)
                pe.nop().then_inc(sc_ps, 1)

            @block.scalar
            def _(act):
                n_ln = 0
                pc = Chain(act, pc_s)
                act.wait_ge(wt_ps, 1)
                nc.scalar.copy(WT[:, :], pW[:, :]).then_inc(wt_sb, 1)
                act.wait_ge(vec_ps, 1)
                nc.scalar.copy(VC[:, :, :], pV[:, :, :]).then_inc(vec_sb, 1)
                layernorm_scalar_part(act, nc, H[:, :, 0:D], st, need_root, root_done, centred, scaled)
                for n in range(G):
                    act.wait_ge(tr_ps, n + 1)
                    if n >= 2:
                        act.wait_ge(tr_used, n - 1)
                    nc.scalar.copy(TT[:, n % 2, :, :], pT[:, n % 2, :, :]).then_inc(tr_sb, 1)
                act.wait_ge(h_rdy, 1)
                pc.done(nc.scalar.activation(g["sig"][:, :], SC[:, 3:4], ACT.Exp, scale=-1.0))
                pc.done(nc.scalar.activation(g["exp_shift"][:, :], g["zero"][:, :], ACT.Exp,
                                             bias=g["neg_shift"][:, 0:1], scale=g["beta"][:, 0:1]))

            @block.vector
            def _(dve):
                ch = Chain(dve, ch_s)
                dve.memset(g["ones16"][:, :], 1.0)
                dve.memset(g["zero"][:, :], 0.0)
                ch.done(dve.memset(H[:, :, D:D + 1], 1.0))
                dve.wait_ge(ld_x, 16)
                layernorm_relu(net, dve, ch, X[:, :, :], XC[:, :, :], H[:, :, 0:D], st, need_root, root_done, centred)
                dve.wait_ge(ld_w, 16 * 11)
                ch.done(dve.tensor_scalar(g["neg_shift"][:, :], SC[:, 4:5], 0.0, -1.0, ALU.max, ALU.mult))
                ch.done(dve.tensor_scalar(g["beta"][:, :], SC[:, 4:5], 1.0, None, ALU.mult))
                dve.nop().then_inc(h_rdy, 1)
                dve.wait_ge(pc_s, 2)
                ch.done(dve.tensor_scalar(g["sig"][:, :], g["sig"][:, :], 1.0, None, ALU.add))
                ch.done(dve.reciprocal(g["sig"][:, :], g["sig"][:, :]))
                dve.wait_ge(sc_ps, 1)
                sc = g["score"][0]
                ch.done(dve.tensor_scalar(sc[:, 0, :], pS[:, :, 0], SC[:, 0:1], None, ALU.add))
                ch.done(dve.tensor_scalar(sc[:, 1, :], pS[:, :, 1], 1.0, None, ALU.mult))
                finish_scores(net, g, 0, dve, ch, MX, MR, mx_rdy, mx_all)


def finish_scores(net, g, k, dve, ch, MX, MR, mx_rdy, mx_all):
    sc = g["score"][k]
    ch.done(dve.tensor_scalar(sc[:, 2, :], sc[:, 1, :], g["slope"][k], None, ALU.mult))
    ch.done(dve.tensor_reduce(MX[:, :], sc[:, 1, :], AXX, ALU.max, apply_absolute_value=True))
    dve.nop().then_inc(mx_rdy, 1)
    dve.wait_ge(mx_all, 1)
    ch.done(dve.tensor_scalar(g["lift"][:, k:k + 1], MR[:, :], 1.0, None, ALU.add))
    ch.done(dve.tensor_scalar(sc[:, 3, :], sc[:, 1, :], g["lift"][:, k:k + 1], None, ALU.add))


def transpose_adj(net, g):
    nc, NB, NC, JS, PW = net.nc, net.NB, net.NC, net.JS, net.PW
    RING, TILES = 8, SUBS * IB
    MOPS = NB
    TC = JS * P
    stage, store16, ident = g["stage"], g["store"].bitcast(U16), g["ident"]
    with ExitStack() as c:
        A = net.sb(c, "adj_rows", [P, RING, TC], F32)
        ident16 = net.sb(c, "ident16", [P, P], BF16)
        halves = A.rearrange("p r j -> p (r j)").bitcast(BF16).rearrange("p (r j w) -> p r j w", r=RING, w=2)
        MA = net.sb(c, "max_acc", [P, 2, CI], F32)
        MB = net.sb(c, "max_done", [P, 2, CI], F32)
        pT = net.ps(c, "p_adjT", [P, 2, JS, P], BF16)
        pM = net.ps(c, "p_max", [P, IB, 2, P])
        pD = net.ps(c, "p_deg", [P, IB])
        E2 = net.dram["L2_gnn_inlayer2"].shape[1] // P
        IN2 = net.sb(c, "inlayer2_rows", [P, IB, E2 * P], F32)
        TI = net.sb(c, "inlayer2_T", [P, IB, E2, P], F32)
        MX = net.sb(c, "absmax2", [P, 1], F32)
        MR = net.sb(c, "absmax2_all", [P, 1], F32)
        pX = net.ps(c, "p_inlayer2_T", [P, IB, E2, P])
        pS = net.ps(c, "p_scores2", [P, IB, 2])
        in2_ld, in2_ps, in2_sb, in2_scores, in2_read = (net.sem(f"b_in2_{n}") for n in ("ld", "ps", "sb", "scores", "read"))
        fin, mx_rdy, mx_all = net.sem("b_finish"), net.sem("b_mx"), net.sem("b_mx_all")
        in2_rows = net.dram["L2_gnn_inlayer2"].rearrange("(c i p) w -> p c i w", p=P, i=IB)
        ld = [net.sem(f"b_ld{k}") for k in range(RING)]
        transposed, staged = net.sem("b_transposed"), net.sem("b_staged")
        stored, kept = net.sem("b_stored"), net.sem("b_kept")
        degs, deg_read = net.sem("b_degrees"), net.sem("b_degree_read")
        maxed, max_ps = net.sem("b_maxed"), net.sem("b_max_ps")
        max_out, id_rdy = net.sem("b_max_out"), net.sem("b_ident16")
        rows = net.dram["adj"].rearrange("(c i p) j -> p c i j", p=P, i=IB)

        def degree(pe, cc, q):
            pe.wait_ge(staged, cc * TILES + (q + 1) * IB + 2)
            if q == 0:
                pe.wait_ge(deg_read, cc + 1)
            net.met(pe)
            for k in range(JS):
                for i in range(IB):
                    last = pe.matmul(pD[:, i:i + 1], stage[:, q, k, i * P:(i + 1) * P], g["ones16"][:, 0:1],
                                     start=(q == 0 and k == 0 and i == 0), stop=(q == SUBS - 1 and k == JS - 1),
                                     skip_group_check=True)
            last.then_inc(degs, 1)

        with nc.Block() as block:
            @block.sync
            def _(sp):
                def load(cc, t):
                    sp.dma_start(A[:, t % RING, :], rows[:, cc, t % IB, (t // IB) * TC:(t // IB + 1) * TC]
                                 if isinstance(cc, int) else
                                 rows[:, ds(cc, 1), t % IB, (t // IB) * TC:(t // IB + 1) * TC].rearrange("p c j -> p (c j)")
                                 ).then_inc(ld[t % RING], 16)
                for t in range(RING):
                    load(0, t)
                sp.dma_start(IN2[:, :, :], in2_rows[:, 0, :, :]).then_inc(in2_ld, 16)
                with sp.Fori(0, NC - 1) as cc:
                    for t in range(RING, TILES + RING):
                        if t == RING + 5:
                            sp.wait_ge(in2_ps, cc + 1)
                            sp.dma_start(IN2[:, :, :], in2_rows[:, ds(cc + 1, 1), :, :].rearrange("p c i w -> p (c i) w")
                                         ).then_inc(in2_ld, 16)
                        sp.wait_ge(transposed, cc * TILES + (t - RING + 1))
                        load(cc if t < TILES else cc + 1, t % TILES)
                for t in range(RING, TILES):
                    sp.wait_ge(transposed, (NC - 1) * TILES + t - RING + 1)
                    load(NC - 1, t)

            @block.tensor
            def _(pe):
                pe.wait_ge(id_rdy, 1)
                pe.sem_inc(degs, SUBS)

                def tile(cc, t, last_chunk):
                    pe.wait_ge(ld[t % RING], cc * (16 * TILES // RING) + 16 * (t // RING + 1))
                    pe.wait_ge(staged, cc * TILES + t + 1)
                    for k in range(JS):
                        last = pe.transpose(pT[:, t % 2, k, :], halves[:, t % RING, k * P:(k + 1) * P, 1], ident16[:, :])
                    last.then_inc(transposed, 1)
                    if t in (9, 11, 13):
                        degree(pe, cc, (t - 9) // 2)
                    if t == 3:
                        pe.wait_ge(in2_ld, cc * 16 + 16)
                        pe.wait_ge(in2_sb, cc + 1)
                        for i in range(IB):
                            for e in range(E2):
                                last = pe.transpose(pX[:, i, e, :], IN2[:, i, e * P:(e + 1) * P], ident[:, :])
                        last.then_inc(in2_ps, 1)
                    if t == 7:
                        pe.wait_ge(in2_sb, cc + 2)
                        pe.wait_ge(in2_read, cc + 1)
                        for i in range(IB):
                            for e in range(E2):
                                last = pe.matmul(pS[:, i, :], TI[:, i, e, :], g["score_vectors"][:, 1 + e, :],
                                                 start=i == 0 and e == 0, stop=e == E2 - 1, skip_group_check=True)
                        last.then_inc(in2_scores, 1)

                def behind(cc, t):
                    if t == 1:
                        degree(pe, cc, SUBS - 1)
                    if t == 5:
                        pe.wait_ge(max_out, cc + 2)
                        for k in range(2):
                            for i in range(IB):
                                last = pe.transpose(pM[:, i, k, :], MB[:, k, i * P:(i + 1) * P], ident[:, :])
                        last.then_inc(max_ps, 1)

                rotated(pe, NC - 1, (6, TILES), tile, behind)

            @block.scalar
            def _(act):
                act.sem_inc(staged, 2)
                act.sem_inc(kept, SUBS)
                act.sem_inc(in2_sb, 1)
                act.sem_inc(in2_scores, 1)
                with act.Fori(0, NC) as cc:
                    for t in range(TILES):
                        q, i = t // IB, t % IB
                        if i == 0:
                            act.wait_ge(kept, cc * SUBS + q + 1)
                            act.wait_ge(degs, cc * SUBS + q + 1)
                            act.wait_ge(maxed, cc * MOPS + (q + 1) * MOPS // SUBS)
                        act.wait_ge(transposed, cc * TILES + t + 1)
                        net.met(act)
                        nc.scalar.activation(stage[:, q, :, i * P:(i + 1) * P], pT[:, t % 2, :, :], ACT.Copy,
                                             scale=ONE, saturate=False).then_inc(staged, 1)
                        if t == 5:
                            act.wait_ge(in2_ps, cc + 1)
                            act.wait_ge(in2_scores, cc + 1)
                            nc.scalar.copy(TI[:, :, :, :], pX[:, :, :, :]).then_inc(in2_sb, 1)

            @block.gpsimd
            def _(pool):
                with pool.Fori(0, NC - 1) as cc:
                    for q in range(SUBS):
                        pool.wait_ge(staged, cc * TILES + (q + 1) * IB + 2)
                        net.met(pool)
                        nc.gpsimd.tensor_copy(store16[:, ds(cc * (SUBS * 2 * PW) + q * 2 * PW, 2 * PW)],
                                              stage[:, q, :, :].rearrange("p k i -> p (k i)").bitcast(U16)
                                              ).then_inc(kept, 1)
                for q in range(SUBS):
                    pool.wait_ge(staged, (NC - 1) * TILES + (q + 1) * IB + 2)
                    pool.dma_start(g["last_chunk"][:, q, :],
                                   stage[:, q, :, :].rearrange("p k i -> p (k i)").bitcast(U32)).then_inc(stored, 16)
                pool.wait_ge(stored, SUBS * 16)
                pool.wait_ge(mx_rdy, 1)
                nc.gpsimd.partition_all_reduce(MR[:, :], MX[:, :], P, RMAX).then_inc(mx_all, 1)

            @block.vector
            def _(dve):
                dve.tensor_copy(ident16[:, :], ident[:, :]).then_inc(id_rdy, 1)
                dve.sem_inc(maxed, MOPS)
                dve.sem_inc(max_ps, 1)
                dve.sem_inc(max_out, 1)
                dve.sem_inc(deg_read, 1)
                dve.sem_inc(in2_read, 1)

                def piece(cc, q, last):
                    dve.wait_ge(staged, cc * TILES + (q + 1) * IB + 2)
                    if q == 0:
                        dve.wait_ge(max_out, cc + 1)
                    for k in range(JS):
                        running_max(net, dve, cc, q * JS + k, g["score"][0], MA, stage[:, q, k, :], maxed, MOPS)
                    if q == 2:
                        dve.wait_ge(in2_scores, cc + 2)
                        dve.tensor_scalar(g["score"][1][:, 0, ds(cc * IB, IB)], pS[:, :, 0], g["scalars"][:, 1:2], None, ALU.add)
                        dve.tensor_scalar(g["score"][1][:, 1, ds(cc * IB, IB)], pS[:, :, 1], g["scalars"][:, 2:3], None,
                                          ALU.add).then_inc(in2_read, 1)
                    if q == SUBS - 1:
                        dve.wait_ge(maxed, cc * MOPS + 2 * MOPS)
                        dve.wait_ge(max_ps, cc + 1)
                        dve.tensor_copy(MB[:, :, :], MA[:, :, :]).then_inc(max_out, 1)

                def tops(cc, u):
                    dve.wait_ge(max_ps, cc + 2)
                    dve.tensor_reduce(g["top"][0][:, ds(cc * IB, IB)], pM[:, :, :, :].rearrange("p i k j -> p i (k j)"),
                                      AXX, ALU.max)
                    dve.wait_ge(degs, cc * SUBS + 2 * SUBS)
                    dve.tensor_scalar(g["deg"][:, ds(cc * IB, IB)], pD[:, :], 1.0 / ONE, None,
                                      ALU.mult).then_inc(deg_read, 1)

                rotated(dve, NC - 1, (1, SUBS), piece, tops)
                dve.wait_ge(in2_read, NC + 1)
                finish_scores(net, g, 1, dve, Chain(dve, fin), MX, MR, mx_rdy, mx_all)


def running_max(net, dve, cc, jt, score, MA, piece, maxed, credit):
    s = score[:, 3, jt:jt + 1]
    dve.wait_ge(maxed, cc * net.NB + credit + max(jt - 1, 0))
    net.met(dve)
    if jt < 2:
        dve.tensor_scalar(MA[:, jt % 2, :], piece, s, None, ALU.mult).then_inc(maxed, 1)
    else:
        dve.scalar_tensor_tensor(MA[:, jt % 2, :], piece, s, MA[:, jt % 2, :], ALU.mult, ALU.max).then_inc(maxed, 1)


def load_pieces(sp, g, net, arrived, used, per_piece, before=None):
    SUBS_W = SUBS * net.PW

    def load(src, q):
        sp.dma_start(g["stage"][:, q, :, :].rearrange("p k i -> p (k i)").bitcast(U32), src).then_inc(arrived[q], 16)

    for q in range(SUBS):
        if before:
            sp.wait_ge(before[0], before[1] + q + 1)
        load(g["store"][:, q * net.PW:(q + 1) * net.PW], q)
    with sp.Fori(0, net.NC - 2) as cc:
        for q in range(SUBS):
            sp.wait_ge(used, cc * (SUBS * per_piece) + (q + 1) * per_piece)
            load(g["store"][:, ds(cc * SUBS_W + (SUBS_W + q * net.PW), net.PW)], q)
    for q in range(SUBS):
        sp.wait_ge(used, (net.NC - 2) * (SUBS * per_piece) + (q + 1) * per_piece)
        load(g["last_chunk"][:, q, :], q)


def attend_masked(net, g, m, H, num):
    nc, NB, NC, JS, D = net.nc, net.NB, net.NC, net.JS, net.D
    stage, ident = g["stage"], g["ident"]
    sc, slope = g["score"][m], g["slope"][m]
    PAIRS = NB // 2
    RT = 4
    AHEAD = 2
    U_DIAG, U_ROWS, U_ROWS_SB = 5, 6, 9
    with ExitStack() as c:
        ones = net.sb(c, f"ones{m}", [P, P], F32)
        R = net.sb(c, f"rows{m}", [P, 2, net.N], F32)
        T = net.sb(c, f"logits{m}", [P, RT, 2, CI], F32)
        PR = net.sb(c, f"probs{m}", [P, 2, 2, CI], F32)
        O = net.sb(c, f"num_out{m}", [P, IB, D + 1], F32)
        RC = net.sb(c, f"row_cols{m}", [P, 3, NB], F32)
        acc = net.ps(c, f"p_acc{m}", [P, 2, 512])
        pR = net.ps(c, f"p_rows{m}", [P, 2, CI])
        pH = net.ps(c, f"p_hsum{m}", [P, D + 1])
        names = ("steps", "diag", "rows_ps", "rows_sb", "hsum", "branch", "logit", "exped", "masked", "summed",
                 "acc_read", "out_dma", "ones_set", "out_free")
        (steps, diag, rows_ps, rows_sb, hs, branch, logit, exped, masked, summed,
         acc_read, out_dma, ones_set, out_free) = (net.sem(f"c{m}_{n}") for n in names)
        arrived = [net.sem(f"c{m}_piece{k}") for k in range(SUBS)]
        num_rows = num.rearrange("(c i p) w -> p c i w", p=P, i=IB)

        def block_of(i):
            return acc[:, i // 2, (i % 2) * (D + 1):(i % 2 + 1) * (D + 1)]

        with nc.Block() as block:
            @block.sync
            def _(sp):
                load_pieces(sp, g, net, arrived, masked, JS // 2)

            @block.gpsimd
            def _(pool):
                with pool.Fori(0, NC) as cc:
                    pool.wait_ge(acc_read, cc + 2)
                    pool.dma_start(num_rows[:, ds(cc, 1), :, :].rearrange("p c i w -> p (c i) w"),
                                   O[:, :, :]).then_inc(out_dma, 16)
                    pool.wait_ge(out_dma, cc * 16 + 16)
                    pool.sem_inc(out_free, 1)
                pool.wait_ge(out_dma, NC * 16)

            @block.tensor
            def _(pe):
                pe.wait_ge(ones_set, 1)

                def rows(cc):
                    wait(pe, diag, cc + 1)
                    for k in range(2):
                        last = pe.matmul(pR[:, k, :], ones[:, :], R[:, k, ds(cc * CI, CI)], start=True, stop=True)
                    last.then_inc(rows_ps, 1)

                def pair(cc, u, last_chunk):
                    if u == 0:
                        pe.wait_ge(acc_read, cc + 1)
                    pe.wait_ge(exped, cc * PAIRS + u + 1)
                    for k in range(2):
                        jt = 2 * u + k
                        for i in range(IB):
                            last = pe.matmul(block_of(i), PR[:, u % 2, k, i * P:(i + 1) * P], H[:, jt, :],
                                             start=(jt == 0 and i % 2 == 0), stop=(jt == NB - 1),
                                             skip_group_check=True)
                    last.then_inc(summed, 1)
                    if u == U_ROWS and not last_chunk:
                        rows(cc + 1)
                    if last_chunk:
                        for b in range(0 if u == AHEAD else 2 * u, 2 * u + 2):
                            last = pe.matmul(pH[:, :], ones[:, :], H[:, b, :], start=b == 0, stop=b == NB - 1)
                        if u == PAIRS - 1:
                            last.then_inc(hs, 1)

                rows(0)
                rotated(pe, NC - 1, (AHEAD, PAIRS), pair, lambda cc, u: None)

            @block.scalar
            def _(act):
                act.sem_inc(acc_read, 1)
                act.sem_inc(out_free, 1)

                def rows(cc):
                    act.wait_ge(rows_ps, cc + 1)
                    net.met(act)
                    nc.scalar.copy(R[:, :, ds(cc * CI, CI)], pR[:, :, :]).then_inc(rows_sb, 1)

                def slope_branch(cc, u):
                    if u == 0:
                        act.wait_ge(rows_sb, cc + 1)
                    wait(act, exped, cc * PAIRS + u - RT + 1)
                    net.met(act)
                    for k in range(2):
                        last = nc.scalar.activation(T[:, u % RT, k, :], R[:, 1, ds(cc * CI, CI)], ACT.Identity,
                                                    bias=sc[:, 2, 2 * u + k:2 * u + k + 1])
                    last.then_inc(branch, 1)

                def pair(cc, u, last_chunk):
                    if u + 2 < PAIRS:
                        slope_branch(cc, u + 2)
                    elif not last_chunk:
                        slope_branch(cc + 1, u + 2 - PAIRS)
                    act.wait_ge(masked, cc * PAIRS + u + 1)
                    wait(act, summed, cc * PAIRS + u - 1)
                    nc.scalar.activation(PR[:, u % 2, :, :], T[:, u % RT, :, :], ACT.Exp).then_inc(exped, 1)
                    if u == U_ROWS_SB and not last_chunk:
                        rows(cc + 1)

                def take(cc, u):
                    act.wait_ge(summed, cc * PAIRS + PAIRS)
                    act.wait_ge(out_free, cc + 1)
                    nc.scalar.copy(O[:, :, :].rearrange("p (a b) w -> p a (b w)", a=2),
                                   acc[:, :, 0:2 * (D + 1)]).then_inc(acc_read, 1)

                rows(0)
                slope_branch(0, 0)
                slope_branch(0, 1)
                rotated(act, NC - 1, (1, PAIRS), pair, take)

            @block.vector
            def _(dve):
                ch = Chain(dve, steps)
                dve.memset(ones[:, :], 1.0).then_inc(ones_set, 1)
                top = RC[:, 2, :]
                ch.done(dve.tensor_scalar(top, g["top"][m][:, :], 1.0 / ONE, g["lift"][:, m:m + 1], ALU.mult, ALU.subtract))
                ch.done(dve.tensor_tensor(top, top, sc[:, 0, :], ALU.add))
                ch.done(dve.scalar_tensor_tensor(top, top, slope, top, ALU.mult, ALU.max))
                ch.done(dve.tensor_tensor(RC[:, 0, :], sc[:, 0, :], top, ALU.subtract))
                ch.done(dve.scalar_tensor_tensor(RC[:, 1, :], sc[:, 0, :], slope, top, ALU.mult, ALU.subtract))

                def rows(cc):
                    for k in range(2):
                        last = dve.tensor_tensor(R[:, k, ds(cc * CI, CI)].rearrange("p (i f) -> p i f", i=IB),
                                                 ident[:, :].unsqueeze(1).to_broadcast([P, IB, P]),
                                                 RC[:, k, ds(cc * IB, IB)].unsqueeze(2).to_broadcast([P, IB, P]),
                                                 ALU.mult)
                    last.then_inc(diag, 1)

                def logits(cc, u):
                    if u == 0:
                        dve.wait_ge(rows_sb, cc + 1)
                    dve.wait_ge(branch, cc * PAIRS + u + 1)
                    for k in range(2):
                        last = dve.scalar_tensor_tensor(T[:, u % RT, k, :], R[:, 0, ds(cc * CI, CI)],
                                                        sc[:, 1, 2 * u + k:2 * u + k + 1], T[:, u % RT, k, :],
                                                        ALU.add, ALU.max)
                    last.then_inc(logit, 1)

                def pair(cc, u, last_chunk):
                    if u + 1 < PAIRS:
                        logits(cc, u + 1)
                    elif not last_chunk:
                        logits(cc + 1, 0)
                    q, k0 = 2 * u // JS, 2 * u % JS
                    if k0 == 0:
                        dve.wait_ge(arrived[q], cc * 16 + 16)
                    dve.wait_ge(logit, cc * PAIRS + u + 1)
                    dve.scalar_tensor_tensor(T[:, u % RT, :, :], stage[:, q, k0:k0 + 2, :].bitcast(U8), float(ONE_BYTE),
                                             T[:, u % RT, :, :], ALU.subtract, ALU.min).then_inc(masked, 1)
                    if u == U_DIAG and not last_chunk:
                        rows(cc + 1)

                rows(0)
                logits(0, 0)
                rotated(dve, NC - 1, (AHEAD, PAIRS), pair, lambda cc, u: None)
                dve.wait_ge(hs, 1)
                dve.tensor_copy(g["hsum"][:, :], pH[:, :])


def attend_cosine(net, g, XT, HL, DH, num, maxima_out):
    nc, NB, NC, JS, D = net.nc, net.NB, net.NC, net.JS, net.D
    stage = g["stage"]
    PAIRS = NB // 2
    WH = 2 * D + 1
    WO = WH + D
    AHEAD, TAKE = 2, 1
    with ExitStack() as c:
        E = net.sb(c, "cos_exp", [P, 2, 2, CI], F32)
        PH = net.sb(c, "cos_hi", [P, 2, 2, CI], F16)
        PL = net.sb(c, "cos_lo", [P, 2, 2, CI], F16)
        O = net.sb(c, "cos_out", [P, IB, WO], F32)
        MA = net.sb(c, "cos_max_acc", [P, 2, CI], F32)
        MB = net.sb(c, "cos_max_done", [P, CI], F32)
        acc = net.ps(c, "p_cos_acc", [P, IB, 512])
        pS = net.ps(c, "p_cos", [P, 2, 2, CI])
        names = ("cos", "exped", "prob", "hi", "lo", "summed", "acc_read", "out_dma",
                 "maxed", "max_out", "max_dma", "max_free", "out_free")
        (cos, exped, prob, hi, lo, summed, acc_read, out_dma, maxed, max_out, max_dma,
         max_free, out_free) = (net.sem(f"d_{n}") for n in names)
        arrived = [net.sem(f"d_piece{k}") for k in range(SUBS)]
        num_rows = num.rearrange("(c i p) w -> p c i w", p=P, i=IB)

        with nc.Block() as block:
            @block.sync
            def _(sp):
                load_pieces(sp, g, net, arrived, summed, JS // 2)

            @block.gpsimd
            def _(pool):
                pool.sem_inc(max_free, 1)
                with pool.Fori(0, NC) as cc:
                    pool.wait_ge(max_out, cc + 2)
                    net.met(pool)
                    pool.dma_start(maxima_out[:, ds(cc * CI, CI)], MB[:, :]).then_inc(max_dma, 16)
                    pool.wait_ge(max_dma, cc * 16 + 16)
                    pool.sem_inc(max_free, 1)
                    pool.wait_ge(acc_read, cc * 2 + 4)
                    pool.dma_start(num_rows[:, ds(cc, 1), :, :].rearrange("p c i w -> p (c i) w"),
                                   O[:, :, :]).then_inc(out_dma, 16)
                    pool.wait_ge(out_dma, cc * 16 + 16)
                    pool.sem_inc(out_free, 1)
                pool.wait_ge(out_dma, NC * 16)
                pool.wait_ge(max_dma, NC * 16)

            @block.tensor
            def _(pe):
                def cosines(cc, u):
                    pe.wait_ge(exped, cc * PAIRS + u + 1)
                    for k in range(2):
                        jt = 2 * u + k
                        for n, (a, b) in enumerate(((0, 0), (0, 1), (1, 0))):
                            last = pe.matmul(pS[:, u % 2, k, :], XT[:, a, jt * P:(jt + 1) * P],
                                             XT[:, b, ds(cc * CI, CI)], start=n == 0, stop=n == 2)
                    last.then_inc(cos, 1)

                def pair(cc, u, last_chunk):
                    if u + 2 < PAIRS:
                        cosines(cc, u + 2)
                    elif not last_chunk:
                        cosines(cc + 1, u + 2 - PAIRS)
                    if u == 0:
                        pe.wait_ge(acc_read, cc * 2 + 2)
                    q, k0 = 2 * u // JS, 2 * u % JS
                    if k0 == 0:
                        pe.wait_ge(arrived[q], cc * 16 + 16)
                    pe.wait_ge(lo, cc * PAIRS + u + 1)
                    for k in range(2):
                        jt = 2 * u + k
                        for i in range(IB):
                            blk = slice(i * P, (i + 1) * P)
                            adj = stage[:, q, k0 + k, blk]
                            first, end = jt == 0, jt == NB - 1
                            pe.matmul(acc[:, i, 0:WH], PH[:, u % 2, k, blk], HL[:, jt, :],
                                      start=first, stop=end, skip_group_check=True)
                            pe.matmul(acc[:, i, D:WH], PL[:, u % 2, k, blk], HL[:, jt, D:WH],
                                      start=False, stop=end, skip_group_check=True)
                            for part in range(2):
                                last = pe.matmul(acc[:, i, WH:WO], adj, DH[:, part, jt, :],
                                                 start=False, stop=end, skip_group_check=True)
                    last.then_inc(summed, 1)

                cosines(0, 0)
                cosines(0, 1)
                rotated(pe, NC - 1, (AHEAD, PAIRS), pair, lambda cc, u: None)

            @block.scalar
            def _(act):
                act.sem_inc(acc_read, 2)
                act.sem_inc(out_free, 1)
                act.sem_inc(exped, 2)

                def exps(cc, u):
                    act.wait_ge(cos, cc * PAIRS + u + 1)
                    wait(act, lo, cc * PAIRS + u - 1)
                    nc.scalar.activation(E[:, u % 2, :, :], pS[:, u % 2, :, :], ACT.Exp, bias=g["neg_shift"][:, 0:1],
                                         scale=g["beta"][:, 0:1]).then_inc(exped, 1)

                def pair(cc, u, last_chunk):
                    if u == 1:
                        exps(cc, 1)
                    act.wait_ge(prob, cc * PAIRS + u + 1)
                    wait(act, summed, cc * PAIRS + u - 1)
                    nc.scalar.copy(PH[:, u % 2, :, :], E[:, u % 2, :, :]).then_inc(hi, 1)
                    if 1 <= u < PAIRS - 1:
                        exps(cc, u + 1)
                    elif u > 0 and not last_chunk:
                        exps(cc + 1, 0)

                def take(cc, u):
                    act.wait_ge(summed, cc * PAIRS + PAIRS)
                    act.wait_ge(out_free, cc + 1)
                    nc.scalar.mul(O[:, 0:2, :], acc[:, 0:2, 0:WO], 1.0 / ONE).then_inc(acc_read, 1)

                exps(0, 0)
                rotated(act, NC - 1, (TAKE, PAIRS), pair, take)

            @block.vector
            def _(dve):
                dve.sem_inc(maxed, NB)
                dve.sem_inc(max_out, 1)

                def probs(cc, u):
                    q, k0 = 2 * u // JS, 2 * u % JS
                    if k0 == 0:
                        dve.wait_ge(arrived[q], cc * 16 + 16)
                    dve.wait_ge(exped, cc * PAIRS + u + 3)
                    net.met(dve)
                    dve.scalar_tensor_tensor(E[:, u % 2, :, :], E[:, u % 2, :, :], g["exp_shift"][:, 0:1],
                                             stage[:, q, k0:k0 + 2, :], ALU.subtract, ALU.mult).then_inc(prob, 1)

                def maxima(cc, u):
                    q, k0 = 2 * u // JS, 2 * u % JS
                    if u == 0:
                        dve.wait_ge(max_out, cc + 1)
                    for k in range(2):
                        running_max(net, dve, cc, 2 * u + k, g["score"][1], MA, stage[:, q, k0 + k, :], maxed, NB)
                    if u == PAIRS - 1:
                        dve.wait_ge(maxed, cc * NB + 2 * NB)
                        dve.wait_ge(max_free, cc + 1)
                        dve.tensor_tensor(MB[:, :], MA[:, 0, :], MA[:, 1, :], ALU.max).then_inc(max_out, 1)

                def pair(cc, u, last_chunk):
                    if u == 1:
                        probs(cc, 1)
                    maxima(cc, u)
                    dve.wait_ge(hi, cc * PAIRS + u + 1)
                    dve.tensor_tensor(PL[:, u % 2, :, :], E[:, u % 2, :, :], PH[:, u % 2, :, :],
                                      ALU.subtract).then_inc(lo, 1)
                    if 1 <= u < PAIRS - 1:
                        probs(cc, u + 1)
                    elif u > 0 and not last_chunk:
                        probs(cc + 1, 0)

                def take(cc, u):
                    dve.wait_ge(summed, cc * PAIRS + PAIRS)
                    dve.wait_ge(out_free, cc + 1)
                    dve.tensor_scalar(O[:, 2:4, :], acc[:, 2:4, 0:WO], 1.0 / ONE, None, ALU.mult).then_inc(acc_read, 1)

                probs(0, 0)
                rotated(dve, NC - 1, (TAKE, PAIRS), pair, take)


def update(net, g, kind, NUM, X, x_src, num, x_dst, XT=None, HL=None, DH=None, HT=None, NT=None,
           maxima=None):
    nc, NB, D = net.nc, net.NB, net.D
    full = [P, NB, D]
    XC = g["stage"].rearrange("p q k i -> p (q k i)").bitcast(F32).rearrange("p (b d) -> p b d", b=NB)
    h, ident = NUM[:, :, 0:D], g["ident"]
    with ExitStack() as c:
        st = net.sb(c, f"ln_cols{kind}", [P, 8, NB], F32)
        W = net.sb(c, f"w_up{kind}", [P, D], F32) if kind == 0 else None
        TT = net.sb(c, f"tt_up{kind}", [P, 2, 4, P], F32) if kind == 0 else None
        MX = net.sb(c, "maxima_in", [P, net.N], F32) if kind == 1 else None
        pT = net.ps(c, f"p_up_t{kind}", [P, 2, 4, P])
        pW = net.ps(c, f"p_up_w{kind}", [P, 2, 4, P])
        if kind == 0:
            ones = net.sb(c, "ones_up", [P, P], F32)
            pH = net.ps(c, "p_hsum_up", [P, D])
        names = ("ld", "ld_x", "ld_lo", "ld_mx", "ld_dif", "steps", "act_steps", "att", "tr_ps", "tr_sb", "tr_sb2", "w_ps", "w_read", "need_root",
                 "root_done", "xdone", "xout", "ask", "told", "turned", "centred", "scaled", "ones_set",
                 "hsum", "spread", "inverse", "high", "unit", "dis_h", "ld_w", "ld_b")
        (ld, ld_x, ld_lo, ld_mx, ld_dif, steps, act_steps, att, tr_ps, tr_sb, tr_sb2, w_ps, w_read, need_root, root_done, xdone, xout,
         ask, told, turned, centred, scaled, ones_set, hs, spread, inverse, high,
         unit, dis_h, ld_w, ld_b) = (net.sem(f"u{kind}_{n}") for n in names)
        G = NB // 4

        with nc.Block() as block:
            @block.sync
            def _(sp):
                rows = rows_view(num)
                if kind == 0:
                    sp.dma_start(W[:, :], net.dram["L0_gnn_W"]).then_inc(ld_w, 16)
                if kind == 1:
                    sp.dma_start(NUM[:, :, :], rows[:, :, D:2 * D + 1]).then_inc(ld, 16)
                    sp.dma_start(XC, rows[:, :, 0:D]).then_inc(ld_lo, 16)
                    sp.dma_start(DH[:, :, :], rows[:, :, 2 * D + 1:3 * D + 1]).then_inc(ld_dif, 16)
                else:
                    sp.dma_start(NUM[:, 0:NB // 2, :], rows[:, 0:NB // 2, :]).then_inc(ld, 16)
                    sp.dma_start(NUM[:, NB // 2:NB, :], rows[:, NB // 2:NB, :]).then_inc(ld_b, 16)
                sp.dma_start(X[:, :, :], rows_view(x_src)).then_inc(ld_x, 16)
                if kind == 1:
                    sp.dma_start(MX[:, :], maxima).then_inc(ld_mx, 16)
                sp.wait_ge(xdone, 1)
                sp.dma_start(rows_view(x_dst), X[:, :, :]).then_inc(xout, 16)
                sp.wait_ge(xout, 16)

            @block.vector
            def _(dve):
                ch = Chain(dve, steps)
                e, rz, nsq, dg = (st[:, k, :] for k in (4, 5, 6, 7))
                r, tmp = st[:, 2, :], st[:, 3, :]
                four = [slice(4 * n, 4 * n + 4) for n in range(G)]

                if kind == 0:
                    dve.memset(ones[:, :], 1.0).then_inc(ones_set, 1)
                    ch.done(dve.tensor_scalar(dg, g["deg"][:, :], 1.0, None, ALU.max))
                    dve.reciprocal(g["dis"][:, :], dg).then_inc(ask, 1)
                    dve.wait_ge(told, 1)
                    newton_rsqrt(dve, ch, g["dis"][:, :], dg, tmp)
                if kind == 1:
                    dve.wait_ge(ld, 16)
                    dve.wait_ge(ld_lo, 16)
                    ch.done(dve.tensor_scalar(g["hsum"][:, :], g["hsum"][:, :], g["exp_shift"][:, 0:1], None, ALU.mult))
                    ch.done(dve.tensor_tensor(h, h, XC, ALU.add))
                    ch.done(dve.tensor_tensor(NUM[:, :, :], NUM[:, :, :],
                                              g["hsum"][:, :].unsqueeze(1).to_broadcast([P, NB, D + 1]), ALU.add))
                    ch.done(dve.reciprocal(rz, NUM[:, :, D]))
                    ch.done(dve.tensor_tensor(XC, h, rz.unsqueeze(2).to_broadcast(full), ALU.mult))
                    dve.wait_ge(ld_x, 16)
                    ch.done(dve.scalar_tensor_tensor(X[:, :, :], XC, g["sig"][:, 0:1], X[:, :, :], ALU.mult, ALU.add))
                    dve.wait_ge(spread, 1)
                    ch.done(dve.tensor_tensor(X[:, :, :], X[:, :, :], DH[:, :, :], ALU.add))
                else:
                    ch.done(dve.tensor_scalar(e, g["deg"][:, :], 0.5, None, ALU.is_lt))
                    dve.wait_ge(ld, 16)

                    def softmax_rows(n):
                        for b in range(4 * n, 4 * n + 4):
                            last = dve.scalar_tensor_tensor(NUM[:, b, :], g["hsum"][:, :], e[:, b:b + 1], NUM[:, b, :],
                                                            ALU.mult, ALU.add)
                        ch.done(last)
                        dve.reciprocal(rz[:, four[n]], NUM[:, four[n], D]).then_inc(inverse, 1)

                    def residual(n):
                        if kind == 0:
                            dve.wait_ge(w_ps, n + 1)
                            rows = pW[:, n % 2, :, :]
                        else:
                            dve.wait_ge(att, n + 1)
                            rows = XC[:, four[n], :]
                        dve.tensor_tensor(X[:, four[n], :], X[:, four[n], :], rows, ALU.add).then_inc(w_read, 1)
                        dve.wait_ge(w_read, n + 1)
                        for b in range(4 * n, 4 * n + 4):
                            last = nc.vector.bn_stats(XC[:, b, 0:6], X[:, b, :])
                        ch.done(last)

                    for n in range(G + 2):
                        if n == G // 2:
                            dve.wait_ge(ld_b, 16)
                        if n < G:
                            softmax_rows(n)
                        if n == 2:
                            dve.wait_ge(ld_x, 16)
                        if n >= 2:
                            residual(n - 2)
                if kind != 0:
                    dve.nop().then_inc(xdone, 1)
                layernorm_relu(net, dve, ch, X[:, :, :], XC, h, st, need_root, root_done, centred, have_stats=kind != 1)
                if kind == 0:
                    less = dg[:, 0:1]
                    ch.done(dve.tensor_scalar(less, g["sig"][:, :], -1.0, -1.0, ALU.mult, ALU.add))
                    for n in range(G):
                        dve.wait_ge(scaled, n + 1)
                        for b in range(4 * n, 4 * n + 4):
                            dve.scalar_tensor_tensor(XC[:, b, :], h[:, b, :], 1.0, h[:, b, :], ALU.mult, ALU.mult,
                                                     accum_out=nsq[:, b:b + 1])
                        last = dve.scalar_tensor_tensor(X[:, four[n], :], h[:, four[n], :], less, X[:, four[n], :],
                                                        ALU.mult, ALU.add)
                    last.then_inc(xdone, 1)
                    dve.wait_ge(xdone, 1)
                    ch.done(dve.tensor_scalar(nsq, nsq, COS_EPS * COS_EPS, None, ALU.max))
                    dve.reciprocal(tmp, nsq).then_inc(ask, 1)
                    for n in range(G):
                        dve.wait_ge(high, n + 1)
                        dve.tensor_tensor(HL[:, four[n], 0:D], h[:, four[n], :], HL[:, four[n], D:2 * D], ALU.subtract)
                    dve.memset(HL[:, :, 2 * D:2 * D + 1], 1.0)
                    dve.wait_ge(told, 2)
                    newton_rsqrt(dve, ch, r, nsq, tmp)
                    for n in range(G):
                        dve.tensor_tensor(XC[:, four[n], :], h[:, four[n], :],
                                          r[:, four[n]].unsqueeze(2).to_broadcast([P, 4, D]), ALU.mult).then_inc(unit, 1)
                    for n in range(G + 1):
                        if n < G:
                            dve.wait_ge(tr_sb, G + n + 1)
                            dve.tensor_tensor(XT[:, 1, 4 * n * P:4 * (n + 1) * P],
                                              pT[:, n % 2, :, :].rearrange("p k i -> p (k i)"),
                                              XT[:, 0, 4 * n * P:4 * (n + 1) * P], ALU.subtract).then_inc(turned, 1)
                        if n >= 1:
                            dve.wait_ge(spread, n)
                            dve.tensor_tensor(DH[:, 1, four[n - 1], :], XC[:, four[n - 1], :], DH[:, 0, four[n - 1], :],
                                              ALU.subtract)
                    dve.wait_ge(hs, 1)
                    dve.tensor_copy(g["hsum"][:, 0:D], pH[:, :])
                    dve.memset(g["hsum"][:, D:D + 1], float(net.N))
                elif kind == 1:
                    dve.memset(NUM[:, :, D:D + 1], 1.0)
                    for n in range(G):
                        dve.wait_ge(tr_ps, n + 1)
                        dve.tensor_reduce(g["top"][1][:, 4 * n:4 * n + 4], pT[:, n % 2, :, :], AXX,
                                          ALU.max).then_inc(turned, 1)
                else:
                    for n in range(G):
                        dve.wait_ge(told, n + 1)
                        dve.tensor_tensor(NT[:, 1, 4 * n:4 * n + 4, :], h[:, 4 * n:4 * n + 4, :],
                                          NT[:, 0, 4 * n:4 * n + 4, :], ALU.subtract)

            @block.tensor
            def _(pe):
                def turn(n, first, src, freed, need):
                    if n >= 2:
                        pe.wait_ge(freed, need + n - 1)
                    for k in range(4):
                        last = pe.transpose(pT[:, n % 2, k, :], src(4 * n + k), ident[:, :])
                    last.then_inc(tr_ps, 1)
                if kind == 0:
                    pe.wait_ge(ld_w, 16)
                    for n in range(G + 1):
                        if n < G:
                            pe.wait_ge(att, n + 1)
                            turn(n, 0, lambda b: XC[:, b, :], tr_sb, 0)
                        if n >= 1:
                            pe.wait_ge(tr_sb, n)
                            if n >= 3:
                                pe.wait_ge(w_read, n - 2)
                            for k in range(4):
                                last = pe.matmul(pW[:, (n - 1) % 2, k, :], TT[:, (n - 1) % 2, k, :], W[:, :],
                                                 start=True, stop=True, skip_group_check=True)
                            last.then_inc(w_ps, 1)
                    pe.wait_ge(ones_set, 1)
                    for n in range(G):
                        pe.wait_ge(scaled, n + 1)
                        for b in range(4 * n, 4 * n + 4):
                            last = pe.matmul(pH[:, :], ones[:, :], h[:, b, :], start=b == 0, stop=b == NB - 1)
                    last.then_inc(hs, 1)
                    for n in range(G):
                        pe.wait_ge(unit, n + 1)
                        turn(n, 1, lambda b: XC[:, b, :], turned, 0)
                elif kind == 1:
                    pe.wait_ge(ld_mx, 16)
                    for n in range(G):
                        turn(n, 0, lambda b: MX[:, b * P:(b + 1) * P], turned, 0)
                elif kind == 2:
                    for n in range(G):
                        pe.wait_ge(scaled, n + 1)
                        turn(n, 0, lambda b: h[:, b, :], tr_sb, 0)

            @block.scalar
            def _(act):
                if kind == 0:
                    act.wait_ge(ask, 1)
                    nc.scalar.activation(g["dis"][:, :], g["dis"][:, :], ACT.Sqrt).then_inc(told, 1)
                if kind != 1:
                    for n in range(G + 1):
                        if n < G:
                            act.wait_ge(inverse, n + 1)
                            for b in range(4 * n, 4 * n + 4):
                                last = nc.scalar.activation(XC[:, b, :], h[:, b, :], ACT.Copy, scale=st[:, 5, b:b + 1])
                            last.then_inc(att, 1)
                        if n >= 1 and kind == 0:
                            act.wait_ge(tr_ps, n)
                            if n >= 3:
                                act.wait_ge(w_ps, n - 2)
                            nc.scalar.copy(TT[:, (n - 1) % 2, :, :], pT[:, (n - 1) % 2, :, :]).then_inc(tr_sb, 1)
                if kind == 1:
                    act.wait_ge(ld_dif, 16)
                    for b in range(NB):
                        last = nc.scalar.activation(DH[:, b, :], DH[:, b, :], ACT.Copy, scale=g["dis"][:, b:b + 1])
                    last.then_inc(spread, 1)
                def high_half(n):
                    act.wait_ge(scaled, n + 1)
                    nc.scalar.copy(HL[:, 4 * n:4 * n + 4, D:2 * D], h[:, 4 * n:4 * n + 4, :]).then_inc(high, 1)

                layernorm_scalar_part(act, nc, h, st, need_root, root_done, centred, scaled,
                                      behind=high_half if kind == 0 else None)
                if kind == 0:
                    act.wait_ge(ask, 2)
                    nc.scalar.activation(st[:, 2, :], st[:, 3, :], ACT.Sqrt).then_inc(told, 1)
                    for n in range(G):
                        act.wait_ge(tr_ps, G + n + 1)
                        nc.scalar.copy(XT[:, 0, 4 * n * P:4 * (n + 1) * P],
                                       pT[:, n % 2, :, :].rearrange("p k i -> p (k i)")).then_inc(tr_sb, 1)
                        for b in range(4 * n, 4 * n + 4):
                            last = nc.scalar.activation(XC[:, b, :], h[:, b, :], ACT.Copy, scale=g["dis"][:, b:b + 1])
                        last.then_inc(dis_h, 1)
                        act.wait_ge(dis_h, n + 1)
                        if n == 0:
                            act.wait_ge(xout, 16)
                        nc.scalar.copy(DH[:, 0, 4 * n:4 * n + 4, :], XC[:, 4 * n:4 * n + 4, :]).then_inc(spread, 1)
                elif kind == 2:
                    for n in range(G):
                        act.wait_ge(scaled, n + 1)
                        nc.scalar.copy(NT[:, 0, 4 * n:4 * n + 4, :], h[:, 4 * n:4 * n + 4, :]).then_inc(told, 1)
                        act.wait_ge(tr_ps, n + 1)
                        nc.scalar.copy(HT[:, 4 * n * P:4 * (n + 1) * P],
                                       pT[:, n % 2, :, :].rearrange("p k i -> p (k i)")).then_inc(tr_sb, 1)


def chebyshev(net, g, layer, W, B, HT, NT, N2, x_src, out):
    nc, NB, NC, JS, D = net.nc, net.NB, net.NC, net.JS, net.D
    stage, ident = g["stage"], g["ident"]
    with ExitStack() as c:
        T1 = net.sb(c, f"cheb_t{layer}", [P, 2, CI], F32)
        EX = net.sb(c, f"cheb_e{layer}", [P, 2, CI], F32)
        XR = net.sb(c, f"cheb_x{layer}", [P, IB, D], F32)
        pA = net.ps(c, f"p_prod{layer}", [P, 2, CI])
        pN = net.ps(c, f"p_nat{layer}", [P, IB, P])
        pO = net.ps(c, f"p_out{layer}", [P, CI])

        NAMES = ("used", "t1", "nat", "nat_hi", "nat_lo", "part", "part_read", "z", "ex", "xin", "y", "ynat", "xout",
                 "steps")
        sems = [{n: net.sem(f"e{layer}{product}_{n}") for n in NAMES} for product in range(2)]

        def programs(product):
            (used, t1, nat, nat_hi, nat_lo, part, part_read, zs, ex, xin, ys, ynat, xout, steps) = (sems[product][n] for n in NAMES)
            first = sems[0]
            arrived = [net.sem(f"e{layer}{product}_piece{k}") for k in range(SUBS)]
            SRC = NT if product == 0 else N2
            final = product == 1 and layer == 1
            xr_in = x_src.rearrange("(c i p) w -> p c i w", p=P, i=IB)
            xr_out = out.rearrange("(c i p) w -> p c i w", p=P, i=IB)

            def sp_part(sp):
                load_pieces(sp, g, net, arrived, used, 1,
                            before=(first["used"], (NC - 1) * SUBS) if product == 1 else None)

            def pool_part(pool):
                if final:
                    with pool.Fori(0, NC) as cc:
                        pool.dma_start(XR[:, :, :], xr_in[:, ds(cc, 1), :, :].rearrange("p c i w -> p (c i) w")
                                       ).then_inc(xin, 16)
                        pool.wait_ge(ynat, cc + 2)
                        net.met(pool)
                        pool.dma_start(xr_out[:, ds(cc, 1), :, :].rearrange("p c i w -> p (c i) w"),
                                       XR[:, :, :]).then_inc(xout, 16)
                        pool.wait_ge(xout, cc * 16 + 16)
                    pool.wait_ge(xout, NC * 16)

            def pe_part(pe):
                if product == 1:
                    pe.wait_ge(first["nat_lo"], NC + 1)
                    pe.wait_ge(first["t1"], NC + 2)
                    pe.wait_ge(first["part_read"], NC + 1)

                def piece(pp, u, last_pair):
                    half, q = u // SUBS, u % SUBS
                    cc = pp * 2 + half
                    if q == 0:
                        pe.wait_ge(t1, cc + 1)
                    pe.wait_ge(arrived[q], cc * 16 + 16)
                    net.met(pe)
                    for k in range(JS):
                        jt = q * JS + k
                        for part_ in range(2):
                            last = pe.matmul(pA[:, half, :], SRC[:, part_, jt, :], stage[:, q, k, :],
                                             start=jt == 0 and part_ == 0, stop=jt == NB - 1 and part_ == 1)
                    last.then_inc(used, 1)
                    if u == SUBS:
                        weights(pp * 2, 0)
                    if u == SUBS + 2 and final:
                        rows_back(pp * 2)

                def behind(pp, u):
                    if u == 0:
                        weights(pp * 2 + 1, 1)
                    if u == 2 and final:
                        rows_back(pp * 2 + 1)

                def weights(cc, half):
                    pe.wait_ge(t1, cc + 3)
                    if product == 0:
                        pe.wait_ge(nat_lo, cc + 1)
                        for i in range(IB):
                            last = pe.transpose(pN[:, i, :], T1[:, half, i * P:(i + 1) * P], ident[:, :])
                        last.then_inc(nat, 1)
                        pe.wait_ge(part_read, cc + 1)
                        pe.matmul(pO[:, :], W[:, 0, :], HT[:, ds(cc * CI, CI)], start=True, stop=False)
                        pe.matmul(pO[:, :], W[:, 1, :], T1[:, half, :], start=False, stop=True).then_inc(part, 1)
                    else:
                        pe.wait_ge(part_read, cc + 1)
                        pe.matmul(pO[:, :], W[:, 2, :], T1[:, half, :], start=True, stop=True).then_inc(part, 1)

                def rows_back(cc):
                    pe.wait_ge(ys, cc + 2)
                    for i in range(IB):
                        last = pe.transpose(pN[:, i, :], EX[:, 0, i * P:(i + 1) * P], ident[:, :])
                    last.then_inc(nat, 1)

                rotated(pe, NC // 2 - 1, (3, 2 * SUBS), piece, behind)

            def act_part(act):
                if product == 1:
                    act.wait_ge(first["part"], NC + 2)
                act.sem_inc(t1, 2)
                act.sem_inc(part, 2)
                with act.Fori(0, NC // 2) as pp:
                    for half in range(2):
                        cc = pp * 2 + half
                        act.wait_ge(part, cc + 1)
                        act.wait_ge(used, cc * SUBS + SUBS)
                        nc.scalar.mul(T1[:, half, :], pA[:, half, :], 1.0 / ONE).then_inc(t1, 1)
                        if product == 0:
                            act.wait_ge(nat, cc + 1)
                            net.met(act)
                            nc.scalar.copy(N2[:, 0, ds(cc * IB, IB), :], pN[:, :, :]).then_inc(nat_hi, 1)
                        else:
                            act.wait_ge(zs, cc + 1)
                            nc.scalar.activation(EX[:, 0, :], EX[:, 0, :], ACT.Exp).then_inc(ex, 1)

            def dve_part(dve):
                if product == 1:
                    dve.wait_ge(first["part_read"], NC + 1)
                for credit in (nat_lo, part_read, ys, ynat):
                    dve.sem_inc(credit, 1)
                with dve.Fori(0, NC) as cc:
                    cols = ds(cc * CI, CI)
                    if product == 0:
                        dve.wait_ge(nat_hi, cc + 1)
                        dve.tensor_tensor(N2[:, 1, ds(cc * IB, IB), :], pN[:, :, :], N2[:, 0, ds(cc * IB, IB), :],
                                          ALU.subtract).then_inc(nat_lo, 1)
                        dve.wait_ge(part, cc + 3)
                        dve.tensor_copy(HT[:, cols], pO[:, :]).then_inc(part_read, 1)
                    else:
                        dve.wait_ge(ys, cc + 1)
                        dve.wait_ge(part, cc + 3)
                        dve.scalar_tensor_tensor(EX[:, 1, :], pO[:, :], B, HT[:, cols], ALU.add, ALU.add).then_inc(part_read, 1)
                        dve.wait_ge(part_read, cc + 2)
                        if final:
                            dve.wait_ge(ynat, cc + 1)
                        dve.tensor_scalar(EX[:, 0, :], EX[:, 1, :], 0.0, None, ALU.min).then_inc(zs, 1)
                        dve.wait_ge(ex, cc + 1)
                        dve.tensor_scalar(EX[:, 1, :], EX[:, 1, :], 0.0, None, ALU.max).then_inc(steps, 1)
                        dve.wait_ge(steps, cc + 1)
                        dst = EX[:, 0, :] if final else HT[:, cols]
                        dve.scalar_tensor_tensor(dst, EX[:, 0, :], -1.0, EX[:, 1, :], ALU.add, ALU.add).then_inc(ys, 1)
                        if not final:
                            dve.wait_ge(ys, cc + 2)
                            dve.tensor_reduce(g["chunk_max"][:, ds(cc, 1)], HT[:, cols], AXX, ALU.max,
                                              apply_absolute_value=True)
                        if final:
                            dve.wait_ge(xin, cc * 16 + 16)
                            dve.wait_ge(nat, cc + 1)
                            dve.tensor_tensor(XR[:, :, :], XR[:, :, :], pN[:, :, :], ALU.add).then_inc(ynat, 1)
            return sp_part, pool_part, pe_part, act_part, dve_part

        first_product, second_product = programs(0), programs(1)
        with nc.Block() as block:
            @block.sync
            def _(sp):
                first_product[0](sp)
                second_product[0](sp)

            @block.gpsimd
            def _(pool):
                second_product[1](pool)

            @block.tensor
            def _(pe):
                first_product[2](pe)
                second_product[2](pe)

            @block.scalar
            def _(act):
                first_product[3](act)
                second_product[3](act)

            @block.vector
            def _(dve):
                first_product[4](dve)
                second_product[4](dve)


def rescale(net, g, W, HT, NT):
    nc, NB, NC, D = net.nc, net.NB, net.NC, net.D
    with ExitStack() as c:
        T = net.sb(c, "scaled", [P, 2, CI], F32)
        S = net.sb(c, "scales", [P, 2], F32)
        pN = net.ps(c, "p_scaled", [P, 2, IB, P])
        steps, sc, nat, hi, lo = (net.sem(f"f_{n}") for n in ("steps", "scaled", "nat", "hi", "lo"))
        def low_part(dve, n):
            blocks = slice(n * IB, (n + 1) * IB)
            dve.wait_ge(hi, n + 1)
            dve.tensor_tensor(NT[:, 1, blocks, :], pN[:, n % 2, :, :], NT[:, 0, blocks, :], ALU.subtract).then_inc(lo, 1)

        with nc.Block() as block:
            @block.vector
            def _(dve):
                ch = Chain(dve, steps)
                ch.done(dve.tensor_reduce(S[:, 0:1], g["chunk_max"][:, :], AXX, ALU.max))
                ch.done(dve.tensor_scalar(S[:, 0:1], S[:, 0:1], 1e-30, 0.125, ALU.max, ALU.mult))
                ch.done(dve.reciprocal(S[:, 1:2], S[:, 0:1]))
                ch.done(dve.tensor_scalar(W[:, 1:3, :], W[:, 1:3, :], S[:, 0:1], None, ALU.mult))
                for n in range(NC):
                    cols = slice(n * CI, (n + 1) * CI)
                    if n >= 2:
                        dve.wait_ge(nat, n - 1)
                    dve.tensor_scalar(T[:, n % 2, :], HT[:, cols], S[:, 1:2], None, ALU.mult).then_inc(sc, 1)
                    if n >= 1:
                        low_part(dve, n - 1)
                low_part(dve, NC - 1)

            @block.tensor
            def _(pe):
                for n in range(NC):
                    pe.wait_ge(sc, n + 1)
                    if n >= 2:
                        pe.wait_ge(lo, n - 1)
                    for i in range(IB):
                        last = pe.transpose(pN[:, n % 2, i, :], T[:, n % 2, i * P:(i + 1) * P], g["ident"][:, :])
                    last.then_inc(nat, 1)

            @block.scalar
            def _(act):
                for n in range(NC):
                    act.wait_ge(nat, n + 1)
                    nc.scalar.copy(NT[:, 0, n * IB:(n + 1) * IB, :], pN[:, n % 2, :, :]).then_inc(hi, 1)


def cheb_weights(net, WL, BL):
    nc = net.nc
    ld, steps = net.sem("w_ld"), net.sem("w_steps")
    with nc.Block() as block:
        @block.sync
        def _(sp):
            for n in range(2):
                sp.dma_start(WL[n][:, :, :], net.dram[f"L3_gnn_W{n}"].rearrange("k d f -> d k f")).then_inc(ld, 16)
                sp.dma_start(BL[n][:, :], net.dram[f"L3_gnn_b{n}"].unsqueeze(1)).then_inc(ld, 16)

        @block.vector
        def _(dve):
            ch = Chain(dve, steps)
            dve.wait_ge(ld, 64)
            for n in range(2):
                ch.done(dve.tensor_tensor(WL[n][:, 0, :], WL[n][:, 0, :], WL[n][:, 2, :], ALU.subtract))
                ch.done(dve.tensor_scalar(WL[n][:, 2, :], WL[n][:, 2, :], 2.0, None, ALU.mult))


def gnn_stack(nc, dram, out):
    with ExitStack() as ctx:
        net = Net(nc, ctx, dram)
        N, D, NB, NC = net.N, net.D, net.NB, net.NC
        g = {"slope": (0.2, 0.01)}
        for name, shape, dt in (("ident", [P, P], F32), ("ones16", [P, P], F16),
                                ("zero", [P, 1], F32), ("sig", [P, 1], F32), ("beta", [P, 1], F32),
                                ("neg_shift", [P, 1], F32), ("exp_shift", [P, 1], F32), ("lift", [P, 2], F32), ("scalars", [P, 5], F32), ("chunk_max", [P, NC], F32),
                                ("score_vectors", [P, 1 + dram["L2_gnn_inlayer2"].shape[1] // P, 2], F32),
                                ("hsum", [P, D + 1], F32), ("deg", [P, NB], F32), ("dis", [P, NB], F32),
                                ("store", [P, (NC - 1) * SUBS * net.PW], U32), ("stage", [P, SUBS, net.JS, CI], FP8)):
            g[name] = net.sb(ctx, name, shape, dt)
        g["score"] = [net.sb(ctx, f"score{k}", [P, 4, NB], F32) for k in range(2)]
        g["top"] = [net.sb(ctx, f"top{k}", [P, NB], F32) for k in range(2)]
        g["last_chunk"] = nc.dram_tensor("adj_last_chunk", [P, SUBS, net.PW], U32, kind="Internal").ap()
        xres = nc.dram_tensor("x_residual", [N, D], F32, kind="Internal").ap()
        num = nc.dram_tensor("weighted_sums", [N, D + 1], F32, kind="Internal").ap()
        maxima = nc.dram_tensor("neighbour_maxima", [P, N], F32, kind="Internal").ap()
        num_cos = nc.dram_tensor("cosine_sums", [N, 3 * D + 1], F32, kind="Internal").ap()

        with ExitStack() as c:
            g["H"] = net.sb(c, "h_gat", [P, NB, D + 1], F32)
            setup(net, g)
            net.phase_end()
            transpose_adj(net, g)
            net.phase_end()
            attend_masked(net, g, 0, g["H"], num)
            net.phase_end()
        with ExitStack() as c:
            HL = net.sb(c, "h_lo_hi", [P, NB, 2 * D + 1], F16)
            XT = net.sb(c, "unit_rows_T", [P, 2, N], F16)
            DH = net.sb(c, "dis_h", [P, 2, NB, D], F16)
            with ExitStack() as c2:
                NUM = net.sb(c2, "num0", [P, NB, D + 1], F32)
                X = DH.rearrange("p a b d -> p (a b d)").bitcast(F32).rearrange("p (b d) -> p b d", b=NB)
                update(net, g, 0, NUM, X, dram["x"], num, xres, XT=XT, HL=HL, DH=DH)
                net.phase_end()
            attend_cosine(net, g, XT, HL, DH, num_cos, maxima)
            net.phase_end()
        with ExitStack() as c:
            H = net.sb(c, "num1", [P, NB, D + 1], F32)
            with ExitStack() as c2:
                X = net.sb(c2, "x1", [P, NB, D], F32)
                DS = net.sb(c2, "diffused", [P, NB, D], F32)
                update(net, g, 1, H, X, xres, num_cos, xres, DH=DS, maxima=maxima)
                net.phase_end()
            attend_masked(net, g, 1, H, num)
            net.phase_end()
        with ExitStack() as c:
            NT = net.sb(c, "h_parts", [P, 2, NB, D], F16)
            HT = net.sb(c, "h_T", [P, N], F32)
            WL = [net.sb(c, f"cheb_w{k}", [P, 3, D], F32) for k in range(2)]
            BL = [net.sb(c, f"cheb_b{k}", [P, 1], F32) for k in range(2)]
            cheb_weights(net, WL, BL)
            net.phase_end()
            with ExitStack() as c2:
                NUM = net.sb(c2, "num2", [P, NB, D + 1], F32)
                X = net.sb(c2, "x2", [P, NB, D], F32)
                update(net, g, 2, NUM, X, xres, num, xres, HT=HT, NT=NT)
                net.phase_end()
            N2 = net.sb(c, "Lh_parts", [P, 2, NB, D], F16)
            chebyshev(net, g, 0, WL[0], BL[0][:, 0:1], HT, NT, N2, xres, out)
            net.phase_end()
            rescale(net, g, WL[1], HT, NT)
            net.phase_end()
            chebyshev(net, g, 1, WL[1], BL[1][:, 0:1], HT, NT, N2, xres, out)
            net.phase_end()


_INS = ['x', 'adj', 'L0_gnn_W', 'L0_gnn_a1', 'L0_gnn_a2', 'L0_gnn_a_bias', 'L1_gnn_alpha', 'L1_gnn_beta',
        'L2_gnn_inlayer2', 'L2_gnn_W1', 'L2_gnn_w2', 'L2_gnn_b2', 'L2_gnn_w3', 'L2_gnn_b3',
        'L3_gnn_W0', 'L3_gnn_b0', 'L3_gnn_W1', 'L3_gnn_b1']


def kernel(**inputs):
    import numpy as _np
    import concourse.bacc as _bacc
    from concourse import mybir as _mybir
    from concourse.bass_utils import run_bass_kernel_spmd as _run

    nc = _bacc.Bacc("TRN2", target_bir_lowering=False, num_devices=1)
    arrays, dram = {}, {}
    for name in _INS:
        a = _np.ascontiguousarray(inputs[name])
        if a.ndim == 0:
            a = a.reshape(1)
        arrays[f"in_{name}_dram"] = a
        dram[name] = nc.dram_tensor(f"in_{name}_dram", a.shape, _mybir.dt.from_np(a.dtype), kind="ExternalInput").ap()
    out = nc.dram_tensor("out_0_dram", inputs["x"].shape, _mybir.dt.float32, kind="ExternalOutput").ap()
    gnn_stack(nc, dram, out)
    r = _run(nc, [arrays], core_ids=[0])
    return r.results[0]["out_0_dram"]
```
